# Optimizing a Trainium2 kernel written in Bass

```python
import numpy as np
import jax
import jax.numpy as jnp

def _softmax(x, axis=-1):
    return jax.nn.softmax(x, axis=axis)

def _gelu(x):
    return jax.nn.gelu(x, approximate=True)

def _silu(x):
    return jax.nn.silu(x)

def _sigmoid(x):
    return jax.nn.sigmoid(x)

def _layernorm(x, axis=-1, eps=1e-05):
    m = jnp.mean(x, axis=axis, keepdims=True)
    v = jnp.var(x, axis=axis, keepdims=True)
    return (x - m) / jnp.sqrt(v + eps)

def _scatter_add(tgt, idx, src, axis=0):
    return tgt.at[idx].add(src)

def _segment_sum(src, seg, n):
    return jax.ops.segment_sum(src, seg, n)
kernel_name = 'mk_adaln_d1_jaxref_r4_08ee38'

def setup_inputs(seed: int=0):
    np.random.seed(seed)
    _w = jnp.asarray

    def _L0_attn_setup():
        import jax, jax.numpy as jnp
        import numpy as np
        B, T, E, H = (1, 512, 256, 16)
        HD = E // H
        key = jax.random.key(seed)
        ks = jax.random.split(key, 8)
        s = 0.02
        mk = lambda k, sh: jax.random.normal(k, sh, jnp.float32) * s
        return {'x': jax.random.normal(ks[0], (B, T, E), jnp.float32), 'wq': mk(ks[1], (E, E)), 'bq': jnp.zeros((E,), jnp.float32), 'wk': mk(ks[2], (E, E)), 'bk': jnp.zeros((E,), jnp.float32), 'wv': mk(ks[3], (E, E)), 'bv': jnp.zeros((E,), jnp.float32), 'wg': mk(ks[4], (E, E)), 'bg': jnp.zeros((E,), jnp.float32), 'wo': mk(ks[5], (E, E)), 'bo': jnp.zeros((E,), jnp.float32), 'wd': mk(ks[6], (H, E)), 'bd': jnp.zeros((H,), jnp.float32), 'gamma': jnp.ones((E,), jnp.float32), 'beta': jnp.zeros((E,), jnp.float32)}
    _L0_attn_in = _L0_attn_setup()

    def _L0_ffn_setup():
        import jax, jax.numpy as jnp
        import numpy as np
        D, H, O, E, TOPK = (256, 1024, 256, 8, 2)
        B, S = (4, 256)
        key = jax.random.key(seed)
        ks = jax.random.split(key, 12)
        std = 0.02
        return {'hidden_states': jax.random.normal(ks[0], (B, S, D), dtype=jnp.float32), 'norm_weight': jnp.ones((D,), dtype=jnp.float32), 'router_w': jax.random.normal(ks[1], (E, D), dtype=jnp.float32) * std, 'sw1': jax.random.normal(ks[2], (D, H), dtype=jnp.float32) * (1.0 / np.sqrt(D)), 'sb1': jnp.zeros((H,), dtype=jnp.float32), 'sw2': jax.random.normal(ks[3], (H, O), dtype=jnp.float32) * (1.0 / np.sqrt(H)), 'sb2': jnp.zeros((O,), dtype=jnp.float32), 'ew1': jax.random.normal(ks[4], (E, D, H), dtype=jnp.float32) * (1.0 / np.sqrt(D)), 'eb1': jnp.zeros((E, H), dtype=jnp.float32), 'ew2': jax.random.normal(ks[5], (E, H, O), dtype=jnp.float32) * (1.0 / np.sqrt(H)), 'eb2': jnp.zeros((E, O), dtype=jnp.float32)}
    _L0_ffn_in = _L0_ffn_setup()
    _L0_c = _w((lambda *s: np.random.randn(*s).astype(np.float32) * 0.05)(4, 256))
    _L0_wmod = _w((lambda *s: np.random.randn(*s).astype(np.float32) * 0.05)(256, 6 * 256) * 256 ** (-0.5))
    _d = {'L0_attn_x': _L0_attn_in['x'], 'L0_attn_wq': _L0_attn_in['wq'], 'L0_attn_bq': _L0_attn_in['bq'], 'L0_attn_wk': _L0_attn_in['wk'], 'L0_attn_bk': _L0_attn_in['bk'], 'L0_attn_wv': _L0_attn_in['wv'], 'L0_attn_bv': _L0_attn_in['bv'], 'L0_attn_wg': _L0_attn_in['wg'], 'L0_attn_bg': _L0_attn_in['bg'], 'L0_attn_wo': _L0_attn_in['wo'], 'L0_attn_bo': _L0_attn_in['bo'], 'L0_attn_wd': _L0_attn_in['wd'], 'L0_attn_bd': _L0_attn_in['bd'], 'L0_attn_gamma': _L0_attn_in['gamma'], 'L0_attn_beta': _L0_attn_in['beta'], 'L0_ffn_norm_weight': _L0_ffn_in['norm_weight'], 'L0_ffn_router_w': _L0_ffn_in['router_w'], 'L0_ffn_sw1': _L0_ffn_in['sw1'], 'L0_ffn_sb1': _L0_ffn_in['sb1'], 'L0_ffn_sw2': _L0_ffn_in['sw2'], 'L0_ffn_sb2': _L0_ffn_in['sb2'], 'L0_ffn_ew1': _L0_ffn_in['ew1'], 'L0_ffn_eb1': _L0_ffn_in['eb1'], 'L0_ffn_ew2': _L0_ffn_in['ew2'], 'L0_ffn_eb2': _L0_ffn_in['eb2'], 'L0_c': _L0_c, 'L0_wmod': _L0_wmod}
    _x0 = _d['L0_attn_x']
    _d['L0_attn_x'] = jax.random.normal(jax.random.fold_in(jax.random.key(seed), 1), (4, 1024, 256), dtype=_x0.dtype)
    del _x0
    return _d

def reference(L0_attn_x, L0_attn_wq, L0_attn_bq, L0_attn_wk, L0_attn_bk, L0_attn_wv, L0_attn_bv, L0_attn_wg, L0_attn_bg, L0_attn_wo, L0_attn_bo, L0_attn_wd, L0_attn_bd, L0_attn_gamma, L0_attn_beta, L0_ffn_norm_weight, L0_ffn_router_w, L0_ffn_sw1, L0_ffn_sb1, L0_ffn_sw2, L0_ffn_sb2, L0_ffn_ew1, L0_ffn_eb1, L0_ffn_ew2, L0_ffn_eb2, L0_c, L0_wmod):

    def _L0_attn_ref(x, wq, bq, wk, bk, wv, bv, wg, bg, wo, bo, wd, bd, gamma, beta):
        import jax, jax.numpy as jnp
        import numpy as np
        B, T, E, H = (1, 512, 256, 16)
        HD = E // H
        Bx, Tx, Ex = x.shape
        scale = jnp.sqrt(jnp.asarray(HD, jnp.float32))

        def proj(w, b):
            return (x @ w.T + b).reshape(Bx, Tx, H, HD).transpose(0, 2, 1, 3)
        Q, K, V = (proj(wq, bq), proj(wk, bk), proj(wv, bv))
        inv_freq = 1.0 / 10000.0 ** (jnp.arange(0, HD, 2, dtype=jnp.float32) / HD)
        freqs = jnp.arange(Tx, dtype=jnp.float32)[:, None] * inv_freq[None, :]
        emb = jnp.concatenate([freqs, freqs], axis=-1)
        cos, sin = (jnp.cos(emb), jnp.sin(emb))

        def rope(t):
            x1, x2 = (t[..., ::2], t[..., 1::2])
            t_rot = jnp.stack([-x2, x1], axis=-1).reshape(t.shape)
            return t * cos + t_rot * sin
        Q, K = (rope(Q), rope(K))
        scores = jnp.einsum('bhqd,bhkd->bhqk', Q, K) / scale
        pd = jax.nn.sigmoid(x.mean(axis=1) @ wd.T + bd)
        log_decay = jnp.log(1.0 - jnp.exp2(-5.0 - 8.0 * pd))
        idx = jnp.arange(Tx)
        pos_diff = jnp.clip(idx[None, :] - idx[:, None], 0, None).astype(jnp.float32)
        scores = scores + pos_diff[None, None] * log_decay[:, :, None, None]
        attn = jax.nn.softmax(scores, axis=-1)
        out = jnp.einsum('bhqk,bhkd->bhqd', attn, V).transpose(0, 2, 1, 3).reshape(Bx, Tx, Ex)
        og = out.reshape(Bx, Tx, H, HD)
        mu = og.mean(axis=(1, 3), keepdims=True)
        var = ((og - mu) ** 2).mean(axis=(1, 3), keepdims=True)
        on = ((og - mu) / jnp.sqrt(var + 1e-05)).reshape(Bx, Tx, Ex) * gamma + beta
        gate = jax.nn.silu(x @ wg.T + bg)
        return gate * on @ wo.T + bo

    def _L0_ffn_ref(hidden_states, norm_weight, router_w, sw1, sb1, sw2, sb2, ew1, eb1, ew2, eb2):
        import jax, jax.numpy as jnp
        import numpy as np
        D, H, O, E, TOPK = (256, 1024, 256, 8, 2)
        B, S = (4, 256)
        b, s, d = hidden_states.shape
        var = jnp.mean(jnp.square(hidden_states), axis=-1, keepdims=True)
        normed = hidden_states * jax.lax.rsqrt(var + 1e-08) * norm_weight
        shared = jnp.maximum(normed @ sw1 + sb1, 0.0) @ sw2 + sb2
        flat = normed.reshape(-1, d)
        T = flat.shape[0]
        probs = jax.nn.sigmoid(flat @ router_w.T)
        scores, idx = jax.lax.top_k(probs, TOPK)
        w = scores / (jnp.sum(scores, axis=-1, keepdims=True) + 1e-06)
        comb = jnp.zeros((T, E), dtype=flat.dtype)
        comb = comb.at[jnp.arange(T)[:, None], idx].add(w)
        h = jnp.maximum(jnp.einsum('td,edh->teh', flat, ew1) + eb1[None, :, :], 0.0)
        eo = jnp.einsum('teh,eho->teo', h, ew2) + eb2[None, :, :]
        routed = jnp.einsum('teo,te->to', eo, comb)
        return shared + routed.reshape(b, s, -1)
    x = L0_attn_x
    mod = (_silu(L0_c) @ L0_wmod).reshape(L0_c.shape[0], 6, 1, -1)
    sa, ca, ga, sb, cb, gb = (mod[:, 0], mod[:, 1], mod[:, 2], mod[:, 3], mod[:, 4], mod[:, 5])
    ga = (2 * (ga >= 0) - 1) * jnp.maximum(jnp.abs(ga), 0.25)
    gb = (2 * (gb >= 0) - 1) * jnp.maximum(jnp.abs(gb), 0.25)
    h = _layernorm(x, axis=-1) * (1 + ca) + sa
    x = x + ga * _L0_attn_ref(h, L0_attn_wq, L0_attn_bq, L0_attn_wk, L0_attn_bk, L0_attn_wv, L0_attn_bv, L0_attn_wg, L0_attn_bg, L0_attn_wo, L0_attn_bo, L0_attn_wd, L0_attn_bd, L0_attn_gamma, L0_attn_beta)
    h = _layernorm(x, axis=-1) * (1 + cb) + sb
    x = x + gb * _L0_ffn_ref(h, L0_ffn_norm_weight, L0_ffn_router_w, L0_ffn_sw1, L0_ffn_sb1, L0_ffn_sw2, L0_ffn_sb2, L0_ffn_ew1, L0_ffn_eb1, L0_ffn_ew2, L0_ffn_eb2)
    return x

_drawn_inputs = setup_inputs


def setup_inputs(seed=0):
    import zlib

    import numpy as np

    out = dict(_drawn_inputs(seed))
    spreads = {'L0_attn_bq': (0.0, 0.8),
     'L0_attn_bk': (0.0, 0.8),
     'L0_attn_bv': (0.0, 0.296),
     'L0_attn_bg': (0.0, 0.761),
     'L0_attn_bo': (0.0, 0.1),
     'L0_attn_bd': (0.0, 0.8),
     'L0_attn_gamma': (1.0, 0.6),
     'L0_attn_beta': (0.0, 0.8),
     'L0_ffn_norm_weight': (1.0, 0.2),
     'L0_ffn_sb1': (0.0, 0.464),
     'L0_ffn_sb2': (0.0, 0.307),
     'L0_ffn_eb1': (0.0, 0.67),
     'L0_ffn_eb2': (0.0, 0.471)}
    factors = {'L0_attn_wq': 8.0,
     'L0_attn_wk': 8.0,
     'L0_attn_wv': 8.0,
     'L0_attn_wg': 2.878,
     'L0_attn_wo': 2.724,
     'L0_attn_wd': 47.741}
    for name, (base, spread) in spreads.items():
        noise = np.random.default_rng([zlib.crc32(name.encode()), seed]).standard_normal(out[name].shape)
        drawn = base * np.exp(spread * noise) if base else spread * noise
        out[name] = jnp.asarray(drawn.astype(out[name].dtype))
    for name, factor in factors.items():
        out[name] = (out[name] * factor).astype(out[name].dtype)
    return out
```

```python
from contextlib import ExitStack

import numpy as np

import concourse.bass as bass
from concourse import mybir

F32 = mybir.dt.float32
BF16 = mybir.dt.bfloat16
I32 = mybir.dt.int32
U32 = mybir.dt.uint32
ALU = mybir.AluOpType
ACT = mybir.ActivationFunctionType
AX = mybir.AxisListType

P = 128
B, T, E = 4, 1024, 256
H = 16
HD = E // H
NT = B * T // P
TB = T // P
KC = E // P
NE = 8
HID = 1024
HC = HID // P
GH = 4
HG = H // GH
NG = B * HG
QH = T // 512
LN2 = float(np.log(2.0))

Q_PART = [0, 0, 1, 1, 0, 2]
K_PART = [0, 1, 0, 1, 2, 0]
ROWS_QK = 16 * len(Q_PART)
ROW_M = ROWS_QK
ROWS_NEAR = ROWS_QK + 1
N_EXT = 9
ROWS_FAR = ROWS_NEAR + N_EXT

STEPS = 2 * QH * TB
BLOCKS = STEPS // 2
NMAX = GH * TB * 2
MSEQ = NMAX + 1
PRING = 8
MAX_DONE = 27
SLOTS = 2 * B * T + NE * P
NTILE = SLOTS // P


def constants():
    f = np.float32
    k = np.arange(T)
    inv = (1.0 / 10000.0 ** (np.arange(0, HD, 2, dtype=f) / f(HD))).astype(f)
    ang = np.arange(T, dtype=f)[:, None] * inv[None, :]
    ang = np.concatenate([ang, ang], axis=-1).astype(f)
    d = np.arange(P) % HD
    cos = np.cos(ang)[:, d].T.astype(f)
    sin = (np.sin(ang)[:, d] * np.where(d % 2 == 0, -1.0, 1.0)[None, :]).T.astype(f)
    ident = np.eye(P, dtype=f)
    relu = np.maximum(np.arange(P)[:, None] - np.arange(P)[None, :], 0).astype(f)
    before = (np.arange(P)[:, None] < np.arange(P)[None, :]).astype(f)
    same_head = (np.arange(P)[:, None] // HD == np.arange(P)[None, :] // HD).astype(f) / f(HD)
    hi, lo = (k // 8 * 8).astype(f), (k % 8).astype(f)
    one = np.ones(T, f)
    kext = (np.stack([one] + [hi] * 3 + [lo] * 3 + [one] * 3).view(np.uint32) >> 16).astype(np.uint16)
    qrow = np.broadcast_to(k.astype(f), (H, T)).copy()
    eidx = np.broadcast_to(np.tile(np.arange(NE) - NE, NT).astype(f), (P, NT * NE)).copy()
    tile = np.broadcast_to(np.arange(NTILE).astype(f), (P, NTILE)).copy()
    token = (np.arange(NT)[None, :] * P + np.arange(P)[:, None]).astype(np.int32)
    return {"c_cos": cos, "c_sin": np.ascontiguousarray(sin), "c_ident": ident, "c_relu": relu, "c_before": before,
            "c_head": same_head, "c_kext": kext, "c_qrow": qrow, "c_token": token, "c_eidx": eidx, "c_tile": tile}


def max_items(step):
    return min(NMAX, -(-NMAX * (step + 1) // MAX_DONE))


class Chain:

    def __init__(self, eng, sem, alone=None):
        self.eng, self.sem, self.n, self.base, self.alone = eng, sem, 0, 0, alone

    def start(self, base):
        self.base, self.n = base, 0

    def __call__(self, ins):
        self.n += 1
        ins.then_inc(self.sem, 1)
        self.eng.wait_ge(self.sem, self.base + self.n)

    def apart(self, ins):
        self.n += 1
        ins.then_inc(self.sem, 1)
        self.eng.wait_ge(self.sem, self.alone(self.eng, self.base + self.n))


def build(nc, a, out, dbg=None, upto=99):
    ctx = ExitStack()
    with ctx:
        def sb(name, shape, dt=F32):
            return ctx.enter_context(nc.sbuf_tensor(name, shape, dt))

        def sem(name):
            return ctx.enter_context(nc.semaphore(name))

        def dram(name, shape, dt=F32):
            return nc.dram_tensor(name, shape, dt).ap() if not dbg else nc.dram_tensor(name, shape, dt, kind="ExternalOutput").ap()

        qkS = dram("qkS", [B, 2, 3, E, T], BF16)
        qeS = dram("qeS", [B, H, N_EXT, T], BF16)
        vS = dram("vS", [B, P, TB, H * 32])
        gS = dram("gS", [B, E, T])
        oS = dram("oS", [B, E, T])
        ldS = dram("ldS", [B, H])
        sS = dram("sS", [B, H, T])
        rS = dram("rS", [B, H, T])
        nS = dram("nS", [B * T, E])
        tokS = dram("tokS", [SLOTS, 1], I32)
        yS = dram("yS", [SLOTS, E])

        bank = [ctx.enter_context(nc.psum_tensor(f"bank{i}", [P, 512], F32)) for i in range(4, 8)]
        score_ps = [ctx.enter_context(nc.psum_tensor(f"score{i}", [P, 2, 512], F32)) for i in range(2)]
        low = [score_ps[0][:, 0, :], score_ps[0][:, 1, :], score_ps[1][:, 0, :], score_ps[1][:, 1, :]]
        hib = [t[:, :] for t in bank]
        max_ps = hib[0:2]
        out_ps = hib[2:4]

        X = sb("X", [P, NT, E])
        W = sb("W", [P, NE, 2, 2048])
        ident = sb("ident", [P, P])
        ones = sb("ones", [P, P])
        relu_t = sb("relu_t", [P, P])
        head_avg = sb("head_avg", [P, P])
        wT = sb("wT", [P, 5, KC, E])
        rows = sb("rows", [P, 4, B, E])
        modT = sb("modT", [P, 4, B])
        smallT = sb("smallT", [P, 56 + NE * HC])
        fcol = sb("fcol", [P, 12])
        bv_row = sb("bv_row", [P, E])
        bo_row = sb("bo_row", [P, E])
        mv1 = sb("mv1", [P, NT, 2])
        rst1 = sb("rst1", [P, NT])
        st6 = sb("st6", [P, NT, 6])
        tmpA = sb("tmpA", [P, NT])
        tmpB = sb("tmpB", [P, NT])
        LDb = sb("LDb", [P, B * H])

        def region(e, k, n, dt=F32):
            ap = W[:, :, :, :].rearrange("p e w x -> p (e w x)")[:, e * 4096 + k:e * 4096 + k + n]
            return ap if dt == F32 else ap.bitcast(dt)

        stackQ = [region(4 + i, 0, 2048, BF16).rearrange("p (h t) -> p h t", h=GH) for i in range(4)]
        stackK = [region(4 + i, 2048, 2048, BF16).rearrange("p (h t) -> p h t", h=GH) for i in range(4)]

        ctx1 = ExitStack()
        if True:
            with ctx1:
                def sb1(name, shape, dt=F32):
                    return ctx1.enter_context(nc.sbuf_tensor(name, shape, dt))
                wn = region(0, 0, 2560).rearrange("p (w c e) -> p w c e", w=5, c=KC)
                wmod = region(0, 2560, 3072).rearrange("p (c e) -> p c e", c=KC)
                scT = region(1, 1536, 8).rearrange("p (c b) -> p c b", c=KC)
                scB = region(1, 1544, 1024).rearrange("p (c b x) -> p c b x", c=KC, b=B)
                wdn = region(1, 2568, 256)
                rwn = region(1, 2824, 256)
                cn = region(1, 3080, 256)
                cE = region(1, 3336, 8).rearrange("p (c b) -> p c b", c=KC)
                mag = region(1, 3352, 256)
                sgn = region(1, 3608, 256)
                ebn = region(1, 3864, P)
        csT = sb("csT", [P, 2, T])
        cosT, sinT = csT[:, 0, :], csT[:, 1, :]
        sw2 = csT[:, :, :].rearrange("p a (b e) -> p (a b) e", e=E)
        OT = region(4, 0, 2048).rearrange("p (c t) -> p c t", c=KC)
        GT = region(4, 2048, 2048).rearrange("p (c t) -> p c t", c=KC)
        RB = region(5, 0, 2048).rearrange("p (c t) -> p c t", c=KC)
        H2 = region(5, 2048, 2048).rearrange("p (t e) -> p t e", t=TB)
        NTr = region(6, 0, 2048).rearrange("p (c t) -> p c t", c=KC)
        sw1 = region(6, 2048, 2048).rearrange("p (c h) -> p c h", c=KC)
        HT = region(7, 0, 4096).rearrange("p (c t) -> p c t", c=HC)
        GT2 = OT
        U = wT[:, 0:2, :, :].rearrange("p w c e -> p w (c e)")
        sums = wT[:, 2, :, :].rearrange("p c e -> p (c e)").rearrange("p (b x) -> p b x", b=B)
        misc = sb("misc", [P, 4, E])
        qrow = misc[0:H, :, :].rearrange("p k e -> p (k e)")
        gabo, gbsb, sb2_row, nw_row = (misc[:, i, :] for i in range(4))
        sb1c = sb("sb1c", [P, HC])
        st3 = sb("st3", [P, 4, 6])
        mvf = sb("mvf", [P, KC, 2])
        gst = sb("gst", [P, KC, 2])
        q3 = sb("q3", [P, 8, KC])
        stx = sb("stx", [P, TB, 6])
        mvx = sb("mvx", [P, TB, 2])
        q8 = sb("q8", [P, 8, TB])
        LG = sb("LG", [P, NT, NE])
        xh = region(2, 0, 2048).rearrange("p (t e) -> p t e", t=TB)
        hT = region(2, 2048, 2048).rearrange("p (c t) -> p c t", c=KC)
        qs = region(3, 0, 4096).rearrange("p (c t) -> p c t", c=4)
        gz = region(4, 0, 2048).rearrange("p (n t) -> p n t", n=4)
        ge = region(4, 2048, 2048).rearrange("p (n t) -> p n t", n=4)
        Vx = region(5, 0, 4096).rearrange("p (t h c) -> p t h c", t=TB, h=H)
        pb = region(6, 0, 4096 + 2048, BF16).rearrange("p (c k t) -> p c k t", c=4, k=3)
        qe = W[:, 7, 1, :].bitcast(BF16)
        rope_s = region(0, 0, 2048).rearrange("p (k t) -> p k t", k=2)
        rope_1 = region(0, 2048, 2048).rearrange("p (k t) -> p k t", k=2)
        rope_r = region(7, 2048, 2048).rearrange("p (k t) -> p k t", k=2)
        qeb = region(1, 0, 3072, BF16)[0:H].rearrange("p (r t) -> p r t", r=6)
        qc = region(1, 3072, 1024)[0:H]
        hsum = sb("hsum", [P, 4])
        mean2 = sb("mean2", [P, 2])
        bd16 = sb("bd16", [H, 1])
        lt = sb("lt", [H, 16])
        l3 = sb("l3", [H, 3], BF16)
        Pb = [region(0, 1024 * i, 1024).rearrange("p (h t) -> p h t", h=2) for i in range(4)] + \
             [region(1, 1024 * i, 1024).rearrange("p (h t) -> p h t", h=2) for i in range(4)]
        Vst = [region(2, 1024 * i, 1024).rearrange("p (t c) -> p t c", t=TB) for i in range(2)]
        Dec = [region(2, 2048 + 512 * i, 512).rearrange("p (h t) -> p h t", h=GH) for i in range(2)]
        Os = [region(3, 512 * i, 512) for i in range(2)]
        mp = sb("mp", [P, NMAX])
        mc = sb("mc", [P, NMAX // 2])
        mrow = sb("mrow", [NMAX // 2, P], BF16)

        def route(i):
            return region(4, 256 * i, 256).rearrange("p (t e) -> p t e", e=NE)
        PR, MK, OH1, OH2, P2, MM, TOT, EXC, POS = (route(i) for i in range(9))
        CUM = region(4, 2304, 256).rearrange("p (e t) -> p e t", e=NE)
        one32 = region(4, 2560, 32)
        m12 = region(4, 2592, 64).rearrange("p (k t) -> p k t", k=2)
        i12 = region(4, 2656, 64).rearrange("p (k t) -> p k t", k=2)
        sm = region(4, 2720, 32)
        pf = region(4, 2752, 64).rearrange("p (k t) -> p k t", k=2)
        ntf = region(4, 2816, NE)
        nti = region(4, 2824, NE, I32)
        tinc = region(4, 2832, NE)
        tslot = region(4, 2840, NE)
        etf = region(4, 2848, 80)
        eidx = region(5, 0, 256).rearrange("p (t e) -> p t e", e=NE)
        before = region(5, 256, P)
        tile_no = region(5, 384, NTILE)
        zero_t = region(5, 512, P, I32)
        tokn = region(5, 640, P, I32)
        tokf = region(5, 768, P)
        st_words = st6[:, :, :].rearrange("p t s -> p (t s)")
        WG = mv1[:, :, :].rearrange("p t k -> p k t")
        POSI = st_words[:, 72:136].bitcast(I32).rearrange("p (k t) -> p k t", k=2)
        ET = sb("ET", [P, 80], I32)
        TIX = st_words[:, 0:NTILE].bitcast(I32)
        TK = sb("TK", [P, NT], I32)
        GI = sb("GI", [P, 4], I32)
        SC = sb("SC", [P, 3, 4], I32)
        PC = sb("PC", [P, 2, TB], I32)
        Hn = [wT[:, 0:2, :, :].rearrange("p w c e -> p (w c e)"), csT[:, 1, :]]
        Ht = [wT[:, 2:4, :, :].rearrange("p w c e -> p (w c e)"), csT[:, 0, :]]
        Ht = [h.rearrange("p (c t) -> p c t", c=HC) for h in Ht]
        Yt = [wT[:, 4, i, :] for i in range(2)]
        Xg = [misc[:, i, :] for i in range(2)]
        XT = [misc[:, 2 + i, :].rearrange("p (c t) -> p c t", c=KC) for i in range(2)]
        eb2r = rows[:, 0:2, :, :].rearrange("p k b e -> p (k b) e")
        Yg = [[region(0, 256 * (2 * i + k), 256) for k in range(2)] for i in range(4)]
        Vg = [region(1, 256 * i, 256) for i in range(4)]

        s_x = [sem(f"x_loaded{b}") for b in range(B)]
        s_cst = sem("constants_loaded")
        s_ones = sem("ones_set")
        s_wtr = sem("weights_transposed")
        s_wev = sem("weights_copied")
        s_ce = sem("c_exp")
        s_sc = sem("c_silu")
        s_mod = sem("modulation_made")
        s_modc = sem("modulation_copied")
        s_var = sem("variance_ready")
        s_sq = sem("sqrt_done")
        s_dve = sem("dve_chain")
        s_pool = sem("pool_chain")
        s_act = sem("act_chain")
        s_xh = sem("x_normalised")
        s_tr = sem("h_transposed")
        s_hT = sem("h_copied")
        s_proj = sem("projection_made")
        s_qkev = sem("qk_copied")
        s_gexp = sem("gate_exp")
        s_gz = sem("gate_z")
        s_vev = sem("v_copied")
        s_gate = sem("gate_made")
        s_cosm = sem("rope_cos_part")
        s_rr = sem("roped")
        s_p1 = sem("part1")
        s_r1 = sem("rest1")
        s_p2 = sem("part2")
        s_p3 = sem("part3")
        s_pout = sem("parts_stored")
        s_gout = sem("gate_stored")
        s_vout = sem("v_stored")
        s_mean = sem("h_mean")
        s_z16 = sem("decay_logit")
        s_zb = sem("decay_z")
        s_e16 = sem("decay_exp")
        s_pd = sem("decay_pd")
        s_ld = sem("log_decay")
        s_qe = sem("decay_rows")
        s_qeo = sem("decay_rows_stored")
        s_ldo = sem("log_decay_stored")
        s_ldb = sem("log_decay_loaded")
        s_kx = sem("key_rows_loaded")
        s_stk = [sem(f"stack_loaded{i}") for i in range(4)]
        s_vld = [sem(f"v_loaded{i}") for i in range(2)]
        s_mm = sem("max_scores")
        s_mx = sem("max_taken")
        s_mc = sem("max_combined")
        s_mrow = sem("max_row_placed")
        s_s = sem("scores_made")
        s_exp = sem("exp_done")
        s_dect = sem("decay_tables")
        s_dec = sem("decay_applied")
        s_pv = sem("pv_done")
        s_oev = sem("out_copied")
        s_od = [sem(f"out_stored{i}") for i in range(2)]

        s_sums = sem("sums_loaded")
        s_inv = sem("sums_inverted")
        s_ro = sem("inverses_stored")
        s_ot = sem("attention_out_loaded")
        s_rb = sem("inverses_loaded")
        s_sw = sem("shared_weights_loaded")
        s_fst = sem("feature_stats")
        s_gmm = sem("head_stats")
        s_gv = sem("head_variance")
        s_gsq = sem("head_sqrt")
        s_gt = sem("gated")
        s_xbo = sem("x_plus_bias")
        s_wo = sem("wo_made")
        s_woev = sem("wo_copied")
        s_xv = sem("x1_variance")
        s_xsq = sem("x1_sqrt")
        s_h2 = sem("h2_scaled")
        s_h2b = sem("h2_made")
        s_ms = sem("h2_squares")
        s_mv = sem("h2_mean_square")
        s_msq = sem("h2_sqrt")
        s_nd = sem("n_scaled")
        s_n = sem("n_made")
        s_nst = sem("n_stored")
        s_ntr = sem("n_transposed")
        s_nT = sem("n_copied")
        s_lg = sem("logits_made")
        s_lgc = sem("logits_copied")
        s_g1 = sem("shared_up")
        s_relu = sem("shared_relu")
        s_g2 = sem("shared_down")
        s_g2m = sem("shared_scaled")
        s_g2e = sem("shared_added")
        s_c3 = sem("dve_chain3")
        s_xsb = sem("x_plus_shared_bias")
        s_rc = sem("routing_tables_loaded")
        s_wl = sem("expert_weights_loaded")
        s_pe4 = sem("routing_counts")
        s_ex4 = sem("routing_exp")
        s_z4 = sem("slot_table_zeroed")
        s_zt = sem("zero_tile")
        s_m4 = sem("choice_made")
        s_pos = sem("positions_ready")
        s_sc4 = sem("scatter_index_staged")
        s_scat = sem("tokens_scattered")
        s_tokl = sem("slot_tokens_loaded")
        s_tokf = sem("slot_tokens_float")
        s_tokt = sem("slot_tokens_transposed")
        s_tix = sem("slot_tokens_ready")
        s_eb2 = sem("expert_bias_loaded")
        s_gi = sem("gather_index_staged")
        s_gx = [sem(f"tokens_gathered{i}") for i in range(2)]
        s_xtr = sem("x_tile_transposed")
        s_xT = sem("x_tile_copied")
        s_u2 = sem("expert_up_half")
        s_hn = sem("hidden_copied")
        s_htr = sem("hidden_transposed")
        s_hr = sem("hidden_relu")
        s_d = sem("expert_down")
        s_y = sem("y_copied")
        s_yo = [sem(f"y_stored{i}") for i in range(2)]
        s_pc = sem("combine_index_staged")
        s_yg = [sem(f"y_gathered{i}") for i in range(4)]
        s_v1 = sem("combined")
        s_fin = sem("x_final")
        s_out = sem("x_stored")
        s_c5 = sem("dve_chain5")

        block = ctx.enter_context(nc.Block())

        count_reg = {}

        def apart(eng, count):
            if not isinstance(count, int):
                if eng not in count_reg:
                    count_reg[eng] = eng.alloc_register(f"count{len(count_reg)}")
                eng.reg_add(count_reg[eng], count, 0)
                count = count_reg[eng]
            eng.wait_ge(s_ones, 1)
            return count

        def base_of(b):
            return b * HG

        @block.sync
        def _(sp):
            def cst(dst, src):
                sp.dma_start(dst, src).then_inc(s_cst, 16)
                cst.n += 1
            cst.n = 0
            cst(ident[:, :], a["c_ident"])
            for i, w in enumerate(("wq", "wk", "wv", "wg", "wo")):
                cst(wn[:, i, :, :], a["L0_attn_" + w].rearrange("(c p) e -> p c e", p=P))
            cst(cn[0:B, :], a["L0_c"])
            cst(wdn[0:H, :], a["L0_attn_wd"])
            cst(rwn[0:NE, :], a["L0_ffn_router_w"])
            cst(ebn[0:NE * HC, :], a["L0_ffn_eb1"].rearrange("e (c p) -> (e c) p", p=P))
            for b in range(B):
                sp.dma_start(X[:, TB * b:TB * b + TB, :],
                             a["L0_attn_x"][b].rearrange("(t p) e -> p t e", p=P)).then_inc(s_x[b], 16)
            cst(wmod, a["L0_wmod"].rearrange("(c p) e -> p c e", p=P))
            cst(cosT, a["c_cos"])
            cst(sinT, a["c_sin"])
            cst(relu_t[:, :], a["c_relu"])
            cst(head_avg[:, :], a["c_head"])
            cst(qrow, a["c_qrow"])
            for i, w in enumerate(("bq", "bk", "bg", "gamma", "beta")):
                col = (0, 2, 4, 8, 10)[i]
                for c in range(KC):
                    cst(fcol[:, col + c:col + c + 1], a["L0_attn_" + w][P * c:P * c + P].unsqueeze(1))
            cst(bv_row[:, :], a["L0_attn_bv"].unsqueeze(0).broadcast_to([P, E]))
            cst(bo_row[:, :], a["L0_attn_bo"].unsqueeze(0).broadcast_to([P, E]))
            cst(bd16[:, :], a["L0_attn_bd"].unsqueeze(1))
            for c in range(HC):
                cst(sb1c[:, c:c + 1], a["L0_ffn_sb1"][P * c:P * c + P].unsqueeze(1))
            build.n_cst = cst.n

            with sp.Fori(0, B) as b:
                for c in range(4):
                    w, oc = c // 2, c % 2
                    sp.wait_ge(s_p3, 4 * b + c + 1)
                    sp.dma_start(qkS[bass.ds(b, 1), w, :, P * oc:P * oc + P, :].rearrange("o k p t -> p (o k) t"),
                                 pb[:, c, :, :]).then_inc(s_pout, 16)
                sp.wait_ge(s_gate, 4 * b + 4)
                for oc in range(KC):
                    sp.dma_start(gS[bass.ds(b, 1), P * oc:P * oc + P, :].rearrange("o p t -> p (o t)"),
                                 gz[:, 2 * oc:2 * oc + 2, :].rearrange("p n t -> p (n t)")).then_inc(s_gout, 16)
                sp.wait_ge(s_vev, 4 * b + 4)
                sp.dma_start(vS[bass.ds(b, 1), :, :, :].rearrange("o p t c -> p (o t) c"),
                             Vx.rearrange("p t h c -> p t (h c)")).then_inc(s_vout, 16)
                sp.wait_ge(s_ld, b + 1)
                sp.dma_start(ldS[bass.ds(b, 1), :].rearrange("o h -> h o"), lt[:, 8:9]).then_inc(s_ldo, 16)
                sp.wait_ge(s_qe, b + 1)
                for r0, r1, src in ((0, 3, 0), (3, 6, 0), (6, 9, 3)):
                    sp.dma_start(qeS[bass.ds(b, 1), :, r0:r1, :].rearrange("o h r t -> h (o r) t"),
                                 qeb[:, src:src + 3, :]).then_inc(s_qeo, 16)
            sp.wait_ge(s_ldo, 16 * B)
            sp.dma_start(LDb[:, :], ldS.rearrange("b h -> (b h)").unsqueeze(0).broadcast_to([P, B * H])).then_inc(s_ldb, 16)
            sp.wait_ge(s_pout, 64 * B)
            sp.wait_ge(s_gout, 32 * B)
            sp.wait_ge(s_vout, 16 * B)
            sp.wait_ge(s_qeo, 48 * B)
            for i in range(4):
                for h in range(GH):
                    sp.dma_start(stackK[i][ROW_M:ROWS_FAR, h, :], a["c_kext"].bitcast(BF16)).then_inc(s_kx, 16)

            def load_stack(b, hg):
                for j in range(6):
                    for w, part, st in ((0, Q_PART[j], stackQ[hg]), (1, K_PART[j], stackK[hg])):
                        src = qkS[bass.ds(b, 1), w, part, 64 * hg:64 * hg + 64, :].rearrange("o (h d) t -> d (o h) t", d=HD)
                        sp.dma_start(st[16 * j:16 * j + 16, :, :], src).then_inc(s_stk[hg], 16)
                sp.dma_start(stackQ[hg][ROWS_NEAR:ROWS_FAR, :, :],
                             qeS[bass.ds(b, 1), GH * hg:GH * hg + GH, :, :].rearrange("o h r t -> r (o h) t")).then_inc(s_stk[hg], 16)

            def load_v(b, hg):
                sp.dma_start(Vst[hg % 2], vS[bass.ds(b, 1), :, :, P * hg:P * hg + P].rearrange("o p t c -> p (o t) c")).then_inc(s_vld[hg % 2], 16)

            def place_max(g):
                sp.wait_ge(s_mx, MSEQ * (g + 1) + 2)
                st = stackQ[place_max.hg]
                sp.dma_start(st[ROW_M:ROW_M + 1, :, :].rearrange("o h (q t) -> o (h q) t", t=P), mrow[:, :]).then_inc(s_mrow, 16)

            def store_out(b, hg, qh):
                g = base_of(b) + hg
                sp.wait_ge(s_oev, 2 * g + qh + 3)
                for i in range(GH):
                    f0 = (GH * hg + i) * HD
                    sp.dma_start(sS[bass.ds(b, 1), GH * hg + i, 512 * qh:512 * qh + 512],
                                 Os[qh][32 * i + HD:32 * i + HD + 1, :]).then_inc(s_od[qh], 16)
                    sp.dma_start(oS[bass.ds(b, 1), f0:f0 + HD, 512 * qh:512 * qh + 512].rearrange("o p t -> p (o t)"),
                                 Os[qh][32 * i:32 * i + HD, :]).then_inc(s_od[qh], 16)

            def slot(b, hg, last):
                g = base_of(b) + hg
                nxt = hg + 2
                if not last or nxt < HG:
                    if nxt >= 4:
                        load_stack(b + 1, nxt - 4)
                    else:
                        load_stack(b, nxt)
                if not last or hg + 1 < HG:
                    if hg + 1 == HG:
                        load_v(b + 1, 0)
                    else:
                        load_v(b, hg + 1)
                store_out(b, hg, 0)
                if not last or hg + 1 < HG:
                    place_max.hg = (hg + 1) % HG
                    place_max(g + 1)
                store_out(b, hg, 1)

            load_stack(0, 0)
            load_v(0, 0)
            load_stack(0, 1)
            place_max.hg = 0
            place_max(0)

            def guarded(b, last):
                for hg in range(HG):
                    g = base_of(b) + hg
                    sp.wait_ge(s_pv, BLOCKS * g + 4)
                    slot(b, hg, last)
            with sp.Fori(0, B - 1) as b:
                guarded(b, False)
            guarded(B - 1, True)
            for qh in range(QH):
                sp.wait_ge(s_od[qh], 128 * NG)
            sp.dma_start(sums[:, :, :], sS.rearrange("b h (q x) -> (h q) b x", x=P)).then_inc(s_sums, 16)
            sp.dma_start(sw1, a["L0_ffn_sw1"].rearrange("(c p) h -> p c h", p=P)).then_inc(s_sw, 16)
            sp.dma_start(sw2, a["L0_ffn_sw2"].rearrange("(c p) e -> p c e", p=P)).then_inc(s_sw, 16)
            sp.dma_start(sb2_row, a["L0_ffn_sb2"].unsqueeze(0).broadcast_to([P, E])).then_inc(s_sw, 16)
            sp.dma_start(nw_row, a["L0_ffn_norm_weight"].unsqueeze(0).broadcast_to([P, E])).then_inc(s_sw, 16)
            sp.wait_ge(s_inv, 1)
            sp.dma_start(rS.rearrange("b h (q x) -> (h q) b x", x=P), sums[:, :, :]).then_inc(s_ro, 16)
            sp.wait_ge(s_ro, 16)

            def load3(b):
                sp.wait_ge(s_gt, b)
                sp.dma_start(OT, oS[bass.ds(b, 1), :, :].rearrange("o (c p) t -> p (o c) t", p=P)).then_inc(s_ot, 16)
                sp.dma_start(GT, gS[bass.ds(b, 1), :, :].rearrange("o (c p) t -> p (o c) t", p=P)).then_inc(s_ot, 16)
                for h in range(H):
                    sp.dma_start(RB[HD * (h % 8):HD * (h % 8) + HD, h // 8, :],
                                 rS[bass.ds(b, 1), h, :].broadcast_to([HD, T])).then_inc(s_rb, 16)

            def store3(b):
                sp.wait_ge(s_n, b + 1)
                sp.dma_start(nS[bass.ds(b * T, T), :].rearrange("(t p) e -> p t e", p=P), H2).then_inc(s_nst, 16)
            load3(0)
            store3(0)
            with sp.Fori(1, B) as b:
                load3(b)
                store3(b)
            def load_expert(e):
                for k, src in ((0, a["L0_ffn_ew1"][e].rearrange("(c p) h -> p c h", p=P)), (1, a["L0_ffn_ew2"][e].rearrange("(c p) o -> p c o", p=P))):
                    sp.dma_start(W[:, e, k, :].rearrange("p (c h) -> p c h", c=src.shape[1]), src).then_inc(s_wl, 16)

            sp.wait_ge(s_gt, B)
            sp.dma_start(region(5, 0, 256), a["c_eidx"]).then_inc(s_rc, 16)
            sp.dma_start(before, a["c_before"]).then_inc(s_rc, 16)
            sp.dma_start(tile_no, a["c_tile"]).then_inc(s_rc, 16)
            sp.dma_start(TK[:, :], a["c_token"]).then_inc(s_rc, 16)
            for e in range(4):
                load_expert(e)
            sp.wait_ge(s_zt, 1)
            sp.dma_start(tokS.rearrange("(i p) o -> i (p o)", p=P), zero_t[0:NTILE, :]).then_inc(s_z4, 16)
            sp.wait_ge(s_scat, 16 * 2 * NT)
            sp.dma_start(tokn[0:NTILE, :], tokS.rearrange("(i p) o -> i (p o)", p=P)).then_inc(s_tokl, 16)
            sp.wait_ge(s_xsb, B)
            sp.wait_ge(s_woev, 4 * B)
            sp.dma_start(eb2r.rearrange("p e o -> p (e o)"),
                         a["L0_ffn_eb2"].rearrange("e o -> (e o)").unsqueeze(0).broadcast_to([P, NE * E])).then_inc(s_eb2, 16)
            sp.wait_ge(s_tix, 1)
            sp.wait_ge(s_nst, 16 * B)
            load_expert(4)
            load_expert(5)
            sp.wait_ge(s_g2, 4 * B)
            load_expert(6)
            load_expert(7)

            with sp.Fori(0, NTILE // 4) as it:
                for u in range(4):
                    sp.wait_ge(s_y, 4 * it + u + 1)
                    sp.dma_start(yS[bass.ds(it * (4 * P) + u * P, P), :], Yt[u % 2]).then_inc(s_yo[u % 2], 16)
            with sp.Fori(0, B) as b:
                sp.wait_ge(s_fin, TB * b + TB)
                sp.dma_start(out[bass.ds(b, 1), :, :].rearrange("o (t p) e -> p (o t) e", p=P),
                             X[:, bass.ds(b * TB, TB), :]).then_inc(s_out, 16)
            sp.wait_ge(s_out, 16 * B)

        @block.gpsimd
        def _(pool):
            g = nc.gpsimd
            chain = Chain(pool, s_pool, apart)
            g.memset(ones[:, :], 1.0).then_inc(s_ones, 1)
            pool.wait_ge(s_cst, 16 * build.n_cst)
            POOL_CH = 8
            with pool.Fori(0, B) as b:
                chain.start(b * POOL_CH)
                for c in range(4):
                    pool.wait_ge(s_qkev, 8 * b + 2 * c + 2)
                    if c:
                        pool.wait_ge(s_rr, 4 * b + c)
                    g.tensor_tensor(rope_1[:, c % 2, :], qs[:, c, :], cosT, ALU.mult).then_inc(s_cosm, 1)
                    if c:
                        pool.wait_ge(s_p1, 4 * b + c)
                        g.tensor_tensor(rope_r[:, (c - 1) % 2, :], rope_r[:, (c - 1) % 2, :], pb[:, c - 1, 0, :], ALU.subtract).then_inc(s_r1, 1)
                pool.wait_ge(s_p1, 4 * b + 4)
                g.tensor_tensor(rope_r[:, 1, :], rope_r[:, 1, :], pb[:, 3, 0, :], ALU.subtract).then_inc(s_r1, 1)
                pool.wait_ge(s_ld, b + 1)
                pool.wait_ge(s_qeo, apart(pool, 48 * b))
                chain.apart(g.tensor_scalar(qc, qrow, lt[:, 9:10], None, ALU.mult))
                chain(g.tensor_copy(qeb[:, 3, :], qc))
                chain.apart(g.tensor_tensor(qc, qc, qeb[:, 3, :], ALU.subtract))
                chain(g.tensor_copy(qeb[:, 4, :], qc))
                chain.apart(g.tensor_tensor(qeb[:, 5, :], qc, qeb[:, 4, :], ALU.subtract))
                for i in range(3):
                    chain.apart(g.tensor_copy(qeb[:, i, :], l3[:, i:i + 1].to_broadcast([H, T])))
                g.nop().then_inc(s_qe, 1)

            def pool_slot(b, hg):
                gr = base_of(b) + hg
                done = 0
                for s in range(STEPS):
                    qh, kt, hp = s // 16, s % 16 // 2, s % 2
                    if kt // 4 == qh:
                        if s == 0:
                            pool.wait_ge(s_dect, GH * (gr + 1))
                        pool.wait_ge(s_exp, STEPS * gr + s + 3)
                        j = kt % 4
                        blk = Pb[s % PRING][:, :, P * j:P * j + P]
                        g.tensor_tensor(blk, blk, Dec[hg % 2][:, 2 * hp:2 * hp + 2, :], ALU.mult).then_inc(s_dec, 1)
            with pool.Fori(0, B) as b:
                for hg in range(HG):
                    pool_slot(b, hg)

            def pool3(b):
                chain.start(POOL3 + 2 * b)
                bb = bass.ds(b, 1)
                if not isinstance(b, int):
                    pool.wait_ge(s_g2e, apart(pool, 4 * b - 4))
                chain.apart(g.tensor_tensor(gabo, rows[:, 0, bb, :].rearrange("p o e -> p (o e)"), bo_row[:, :], ALU.mult))
                xb = X[:, bass.ds(b * TB, TB), :]
                g.tensor_tensor(xb, xb, gabo.unsqueeze(1).broadcast_to([P, TB, E]), ALU.add).then_inc(s_xbo, 1)
                pool.wait_ge(s_h2, apart(pool, 2 * b + 2))
                g.tensor_tensor(H2, H2, rows[:, 1, bb, :].broadcast_to([P, TB, E]), ALU.add).then_inc(s_h2b, 1)
                chain.apart(g.tensor_tensor(gbsb, rows[:, 3, bb, :].rearrange("p o e -> p (o e)"), sb2_row, ALU.mult))
                g.tensor_tensor(xb, xb, gbsb.unsqueeze(1).broadcast_to([P, TB, E]), ALU.add).then_inc(s_xsb, 1)
                pool.wait_ge(s_nd, b + 1)
                g.tensor_tensor(H2, H2, nw_row.unsqueeze(1).broadcast_to([P, TB, E]), ALU.mult).then_inc(s_n, 1)
            POOL3 = B * POOL_CH
            pool.wait_ge(s_sw, 64)
            pool3(0)
            with pool.Fori(1, B) as b:
                pool3(b)

            pool.wait_ge(s_gt, B)
            g.memset(zero_t, 0).then_inc(s_zt, 1)
            pool.wait_ge(s_z4, 16)
            pool.wait_ge(s_rc, 64)
            pool.wait_ge(s_pos, 1)
            with pool.Fori(0, NT // 4) as it:
                pool.wait_ge(s_scat, apart(pool, 128 * it))
                g.tensor_copy(SC[:, 0:2, :], POSI[:, :, bass.ds(it * 4, 4)]).then_inc(s_sc4, 1)
                g.tensor_copy(SC[:, 2, :], TK[:, bass.ds(it * 4, 4)]).then_inc(s_sc4, 1)
                pool.wait_ge(s_sc4, apart(pool, 2 * it + 2))
                for u in range(4):
                    for k in range(2):
                        g.indirect_dma_start(out=tokS[:, :], out_offset=bass.IndirectOffsetOnAxis(ap=SC[:, k, u:u + 1].bitcast(U32), axis=0),
                                             in_=SC[:, 2, u:u + 1], in_offset=None).then_inc(s_scat, 16)
            pool.wait_ge(s_tix, 1)
            pool.wait_ge(s_nst, 16 * B)
            pool.wait_ge(s_g2, 4 * B)
            with pool.Fori(0, NTILE // 4) as it:
                for u in range(2):
                    pool.wait_ge(s_gx[u], 32 * it)
                pool.wait_ge(s_xtr, 4 * it)
                g.tensor_copy(GI[:, :], TIX[:, bass.ds(it * 4, 4)]).then_inc(s_gi, 1)
                pool.wait_ge(s_gi, apart(pool, it + 1))
                for u in range(4):
                    if u >= 2:
                        pool.wait_ge(s_xtr, apart(pool, 4 * it + u - 1))
                    g.indirect_dma_start(out=Xg[u % 2], out_offset=None, in_=nS[:, :],
                                         in_offset=bass.IndirectOffsetOnAxis(ap=GI[:, u:u + 1].bitcast(U32), axis=0)).then_inc(s_gx[u % 2], 16)
            for i in range(2):
                pool.wait_ge(s_yo[i], 16 * NTILE // 2)
            with pool.Fori(0, B) as b:
                for i in range(4):
                    pool.wait_ge(s_yg[i], 64 * b)
                pool.wait_ge(s_v1, TB * b)
                g.tensor_copy(PC[:, :, :], POSI[:, :, bass.ds(b * TB, TB)]).then_inc(s_pc, 1)
                pool.wait_ge(s_pc, apart(pool, b + 1))
                for t in range(TB):
                    if t >= 4:
                        pool.wait_ge(s_v1, apart(pool, TB * b + t - 3))
                    for k in range(2):
                        g.indirect_dma_start(out=Yg[t % 4][k], out_offset=None, in_=yS[:, :],
                                             in_offset=bass.IndirectOffsetOnAxis(ap=PC[:, k, t:t + 1].bitcast(U32), axis=0)).then_inc(s_yg[t % 4], 16)

        @block.scalar
        def _(act):
            s = nc.scalar
            act.wait_ge(s_wev, 6)
            s.activation(cE, smallT[:, 48:56].rearrange("p (c b) -> p c b", c=KC), ACT.Exp, scale=-1.0).then_inc(s_ce, 1)
            act.wait_ge(s_var, 1)
            s.activation(tmpB[:, :], tmpA[:, :], ACT.Sqrt).then_inc(s_sq, 1)
            with act.Fori(0, B) as b:
                for half in range(2):
                    for fc in range(KC):
                        n = 2 * half + fc
                        act.wait_ge(s_tr, apart(act, 4 * b + n + 1))
                        if n == 0:
                            act.wait_ge(s_proj, 17 * b)
                            act.wait_ge(s_mean, apart(act, b))
                            act.wait_ge(s_modc, 1)
                        s.activation(hT[:, fc, 512 * half:512 * half + 512], low[n][:, :], ACT.Identity,
                                     bias=modT[:, fc, bass.ds(b, 1)], scale=modT[:, 2 + fc, bass.ds(b, 1)],
                                     accum_out=hsum[:, 2 * fc + half:2 * fc + half + 1]).then_inc(s_hT, 1)
                def part1(c):
                    act.wait_ge(s_rr, 4 * b + c + 1)
                    if c == 0:
                        act.wait_ge(s_pout, 64 * b)
                    s.copy(pb[:, c, 0, :], rope_r[:, c % 2, :]).then_inc(s_p1, 1)

                def part2(c):
                    act.wait_ge(s_r1, 4 * b + c + 1)
                    s.copy(pb[:, c, 1, :], rope_r[:, c % 2, :]).then_inc(s_p2, 1)
                for j in range(8):
                    c, half = j // 2, j % 2
                    w, oc = c // 2, c % 2
                    act.wait_ge(s_proj, 17 * b + j + 1)
                    if j == 0:
                        act.wait_ge(s_rr, 4 * b)
                        act.wait_ge(s_cosm, 4 * b)
                    s.activation(qs[:, c, 512 * half:512 * half + 512], hib[j % 4], ACT.Identity,
                                 bias=fcol[:, 2 * w + oc:2 * w + oc + 1], scale=0.25 if w == 0 else 1.0).then_inc(s_qkev, 1)
                    if j == 5:
                        part1(0)
                    if j == 7:
                        part2(0)
                        part1(1)
                for j in range(8, 12):
                    act.wait_ge(s_proj, 17 * b + j + 1)
                    if j == 8:
                        act.wait_ge(s_gate, 4 * b)
                    oc, half = (j - 8) // 2, j % 2
                    s.activation(ge[:, j - 8, :], hib[j % 4], ACT.Exp, bias=fcol[:, 6 + oc:7 + oc], scale=-1.0).then_inc(s_gexp, 1)
                part2(1)
                part1(2)
                part2(2)
                part1(3)
                part2(3)
                act.wait_ge(s_zb, b + 1)
                s.activation(lt[:, 1:2], lt[:, 0:1], ACT.Exp, scale=-1.0).then_inc(s_e16, 1)
                act.wait_ge(s_pd, b + 1)
                s.activation(lt[:, 3:4], lt[:, 2:3], ACT.Exp, scale=-8.0 * LN2).then_inc(s_e16, 1)

            act.wait_ge(s_ldb, 16)
            act.wait_ge(s_pout, 64 * B)
            act.wait_ge(s_qeo, 48 * B)
            act.wait_ge(s_vout, 16 * B)
            act.wait_ge(s_proj, 17 * B)

            def out_copy(gr, qh):
                act.wait_ge(s_pv, BLOCKS * gr + 8 * qh + 8 + 4)
                act.wait_ge(s_od[qh], 128 * gr)
                s.copy(Os[qh], out_ps[qh]).then_inc(s_oev, 1)

            def act_slot(b, hg):
                gr = base_of(b) + hg
                for i in range(GH):
                    hcol = b * H + (GH * hg + i)
                    s.activation(Dec[hg % 2][:, i, :], relu_t[:, :], ACT.Exp, scale=LDb[:, bass.ds(hcol, 1)]).then_inc(s_dect, 1)
                for st in range(STEPS):
                    act.wait_ge(s_s, STEPS * gr + st + 1)
                    act.wait_ge(s_pv, BLOCKS * gr + st // 2 + 1)
                    s.activation(Pb[st % PRING], score_ps[st % 2][:, :, :], ACT.Exp).then_inc(s_exp, 1)
                    if st == 19:
                        out_copy(gr, 0)
                out_copy(gr, 1)
            act.nop().then_inc(s_exp, 2)
            act.nop().then_inc(s_oev, 2)
            with act.Fori(0, B) as b:
                for hg in range(HG):
                    if hg < 2:
                        act.wait_ge(s_dec, apart(act, 16 * base_of(b)))
                    else:
                        act.wait_ge(s_dec, apart(act, 16 * (base_of(b) + hg - 1)))
                    act_slot(b, hg)

            def act3(b):
                act.wait_ge(s_gv, b + 1)
                s.activation(q3[:, 2, :], q3[:, 1, :], ACT.Sqrt).then_inc(s_gsq, 1)
                act.wait_ge(s_xv, b + 1)
                s.activation(q8[:, 1, :], q8[:, 0, :], ACT.Sqrt).then_inc(s_xsq, 1)
                act.wait_ge(s_h2b, b + 1)
                for t in range(TB):
                    ins = s.activation(U[:, 0, E * (t % 2):E * (t % 2) + E], H2[:, t, :], ACT.Square, accum_out=q8[:, 2, t:t + 1])
                    if t % 2 == 1:
                        ins.then_inc(s_ms, 1)
                        act.wait_ge(s_ms, 4 * b + t // 2 + 1)
                act.wait_ge(s_mv, b + 1)
                s.activation(q8[:, 4, :], q8[:, 3, :], ACT.Sqrt).then_inc(s_msq, 1)

            def act_shared(b):
                for half in range(2):
                    for hc in range(HC):
                        n = HC * half + hc
                        act.wait_ge(s_g1, 16 * b + n + 1)
                        if hc == 0:
                            act.wait_ge(s_g2, 4 * b + 2 * half)
                        s.activation(HT[:, hc, :], hib[n % 2], ACT.Relu, bias=sb1c[:, hc:hc + 1]).then_inc(s_relu, 1)

            def act3b(b):
                for n in range(4):
                    act.wait_ge(s_ntr, 4 * b + n + 1)
                    half, fc = n // 2, n % 2
                    s.copy(NTr[:, fc, 512 * half:512 * half + 512], low[n]).then_inc(s_nT, 1)
            act3(0)
            act3b(0)
            with act.Fori(1, B) as b:
                act3(b)
                act_shared(b - 1)
                act3b(b)
            act.wait_ge(s_lgc, B)
            act.wait_ge(s_wo, 4 * B)
            s.activation(PR.rearrange("p t e -> p (t e)"), LG[:, :, :].rearrange("p t e -> p (t e)"), ACT.Exp, scale=-1.0).then_inc(s_ex4, 1)
            act_shared(B - 1)

            def x_copy(i, it, u):
                act.wait_ge(s_xtr, i + 1)
                if not (isinstance(i, int) and i < 2):
                    act.wait_ge(s_u2, 2 * i - 2)
                s.copy(XT[u % 2].rearrange("p c t -> p (c t)"), hib[2 + u % 2][:, 0:KC * P]).then_inc(s_xT, 1)

            def relu(i, u, e):
                act.wait_ge(s_htr, apart(act, i + 1))
                if not (isinstance(i, int) and i < 2):
                    act.wait_ge(s_d, apart(act, i - 1))
                for hc in range(HC):
                    s.activation(Ht[u % 2][:, hc, :], low[2 + hc // 4][:, P * (hc % 4):P * (hc % 4) + P], ACT.Relu,
                                 bias=smallT[:, bass.ds(e * HC + 56 + hc, 1)]).then_inc(s_hr, 1)

            def act5(it, first, last):
                for u in range(4):
                    i = 4 * it + u
                    e = act.value_load(ET[0:1, bass.ds(i, 1)], min_val=0, max_val=NE - 1)
                    if not last or u + 2 < 4:
                        x_copy(i + 2, it, u + 2)
                    relu(i, u, e)
            act.wait_ge(s_pos, 1)
            x_copy(0, 0, 0)
            x_copy(1, 0, 1)
            act5(0, True, False)
            with act.Fori(1, NTILE // 4 - 1) as it:
                act5(it, False, False)
            act5(NTILE // 4 - 1, False, True)

        @block.vector
        def _(dve):
            v = nc.vector
            chain = Chain(dve, s_dve)
            dve.wait_ge(s_cst, 16 * build.n_cst)
            for i in range(5):
                dve.wait_ge(s_wtr, i + 1)
                v.tensor_copy(wT[:, i, :, :].rearrange("p c e -> p (c e)"), (low + hib)[i]).then_inc(s_wev, 1)
            dve.wait_ge(s_wtr, 6)
            v.tensor_copy(smallT[:, :], hib[1][:, 0:56 + NE * HC]).then_inc(s_wev, 1)
            chain(v.tensor_scalar(fcol[:, 0:2], fcol[:, 0:2], 0.25, None, ALU.mult))
            chain(v.tensor_scalar(fcol[:, 6:8], fcol[:, 4:6], -1.0, None, ALU.mult))
            dve.wait_ge(s_ce, 1)
            chain(v.tensor_scalar(cE, cE, 1.0, None, ALU.add))
            chain(v.reciprocal(cE, cE))
            chain(v.tensor_tensor(scT, smallT[:, 48:56].rearrange("p (c b) -> p c b", c=KC), cE, ALU.mult))
            dve.wait_ge(s_ones, 1)
            for c in range(KC):
                for b in range(B):
                    v.tensor_scalar(scB[:, c, b, :], ones[:, :], scT[:, c, b:b + 1], None, ALU.mult).then_inc(s_sc, 1)
            dve.wait_ge(s_mod, 1)
            v.tensor_copy(modT[:, 0:2, :], hib[2][:, 0:8].rearrange("p (n b) -> p n b", n=2)).then_inc(s_dve, 1)
            chain.n += 1
            v.tensor_scalar(modT[:, 2:4, :], hib[2][:, 8:16].rearrange("p (n b) -> p n b", n=2), 1.0, None, ALU.add).then_inc(s_modc, 1)
            for n in range(8):
                b, half = n // 2, n % 2
                dve.wait_ge(s_mod, n + 2)
                v.tensor_copy(rows[:, 2 * half:2 * half + 2, b, :], low[n % 4].rearrange("p (k e) -> p k e", k=2)).then_inc(s_modc, 1)
            dve.wait_ge(s_modc, 9)
            chain(v.tensor_scalar(rows[:, 2, :, :], rows[:, 2, :, :], 1.0, None, ALU.add))
            for b in range(B):
                for k in (0, 3):
                    gr = rows[:, k, b, :]
                    chain(v.scalar_tensor_tensor(mag, gr, -1.0, gr, ALU.mult, ALU.max))
                    chain(v.tensor_scalar(sgn, gr, 0.0, 2.0, ALU.is_ge, ALU.mult))
                    chain(v.tensor_scalar(mag, mag, 0.25, None, ALU.max))
                    chain(v.scalar_tensor_tensor(gr, sgn, -1.0, mag, ALU.add, ALU.mult))
            for t in range(NT):
                if t % TB == 0:
                    dve.wait_ge(s_x[t // TB], 16)
                ins = v.bn_stats(st6[:, t, :], X[:, t, :])
            chain(ins)
            for t in range(NT):
                ins = v.bn_aggr(mv1[:, t, :], st6[:, t, :])
            chain(ins)
            v.tensor_scalar(tmpA[:, :], mv1[:, :, 1], 1e-5, None, ALU.add).then_inc(s_var, 1)
            dve.wait_ge(s_sq, 1)
            chain(v.reciprocal(rst1[:, :], tmpB[:, :]))
            chain(v.tensor_tensor(tmpB[:, :], rst1[:, :], rst1[:, :], ALU.mult))
            chain(v.tensor_tensor(tmpB[:, :], tmpB[:, :], tmpA[:, :], ALU.mult))
            chain(v.tensor_scalar(tmpB[:, :], tmpB[:, :], -0.5, 1.5, ALU.mult, ALU.add))
            chain(v.tensor_tensor(rst1[:, :], rst1[:, :], tmpB[:, :], ALU.mult))
            chain(v.memset(Vx[:, :, :, HD:32], 1.0))
            dve.wait_ge(s_mod, 9)
            base1 = chain.n
            PER1 = [None]

            def batch(b, per):
                chain.start(base1 + b * per)
                for t in range(TB):
                    tt = b * TB + t
                    if t == 0:
                        dve.wait_ge(s_tr, 4 * b)
                    v.tensor_scalar(xh[:, t, :], X[:, bass.ds(tt, 1), :].rearrange("p o e -> p (o e)"),
                                    mv1[:, bass.ds(tt, 1), 0], rst1[:, bass.ds(tt, 1)],
                                    ALU.subtract, ALU.mult).then_inc(s_xh, 1)
                dve.wait_ge(s_hT, 4 * b + 4)
                chain(v.tensor_tensor(mean2[:, :], hsum[:, 0:4:2], hsum[:, 1:4:2], ALU.add))
                v.tensor_scalar(mean2[:, :], mean2[:, :], 1.0 / T, None, ALU.mult).then_inc(s_mean, 1)

                def rest2(c):
                    dve.wait_ge(s_p2, 4 * b + c + 1)
                    v.tensor_tensor(pb[:, c, 2, :], rope_r[:, c % 2, :], pb[:, c, 1, :], ALU.subtract).then_inc(s_p3, 1)

                for c in range(4):
                    dve.wait_ge(s_qkev, apart(dve, 8 * b + 2 * c + 2))
                    chain(v.stream_shuffle(rope_s[:, c % 2, :], qs[:, c, :], [i ^ 1 for i in range(32)]))
                    chain(v.tensor_tensor(rope_s[:, c % 2, :], rope_s[:, c % 2, :], sinT, ALU.mult))
                    dve.wait_ge(s_cosm, 4 * b + c + 1)
                    if c >= 2:
                        rest2(c - 2)
                        dve.wait_ge(s_p3, 4 * b + c - 1)
                    else:
                        dve.wait_ge(s_p3, 4 * b)
                    v.tensor_tensor(rope_r[:, c % 2, :], rope_1[:, c % 2, :], rope_s[:, c % 2, :], ALU.add).then_inc(s_rr, 1)
                for n in range(4):
                    dve.wait_ge(s_gexp, 4 * b + n + 1)
                    if n == 0:
                        dve.wait_ge(s_gout, 32 * b)
                    v.tensor_scalar(gz[:, n, :], hib[n], fcol[:, 4 + n // 2:5 + n // 2], None, ALU.add).then_inc(s_gz, 1)
                    chain(v.tensor_scalar(ge[:, n, :], ge[:, n, :], 1.0, None, ALU.add))
                    chain(v.reciprocal(ge[:, n, :], ge[:, n, :]))
                    dve.wait_ge(s_gz, 4 * b + n + 1)
                    v.tensor_tensor(gz[:, n, :], gz[:, n, :], ge[:, n, :], ALU.mult).then_inc(s_gate, 1)
                for n in range(4):
                    dve.wait_ge(s_proj, 17 * b + 12 + n + 1)
                    if n == 0:
                        dve.wait_ge(s_vout, 16 * b)
                    for k in range(2):
                        ins = v.tensor_tensor(Vx[:, 2 * n + k, :, 0:HD], hib[n][:, E * k:E * k + E].rearrange("p (h d) -> p h d", h=H),
                                              bv_row[:, :].rearrange("p (h d) -> p h d", h=H), ALU.add)
                    ins.then_inc(s_vev, 1)
                dve.wait_ge(s_proj, 17 * b + 17)
                dve.wait_ge(s_ldo, 16 * b)
                dve.wait_ge(s_qe, b)
                v.tensor_tensor(lt[:, 0:1], hib[0][0:H, 0:1], bd16[:, :], ALU.add).then_inc(s_zb, 1)
                dve.wait_ge(s_e16, 2 * b + 1)
                chain(v.tensor_scalar(lt[:, 4:5], lt[:, 1:2], 1.0, None, ALU.add))
                v.reciprocal(lt[:, 2:3], lt[:, 4:5]).then_inc(s_pd, 1)
                dve.wait_ge(s_e16, 2 * b + 2)
                chain(v.tensor_scalar(lt[:, 5:6], lt[:, 3:4], -2.0 ** -5, 1.0, ALU.mult, ALU.add))
                chain(v.tensor_scalar(lt[:, 6:7], lt[:, 5:6], -1.0, 1.0, ALU.mult, ALU.add))
                chain(v.tensor_scalar(lt[:, 7:8], lt[:, 6:7], 1.0 / 7, 1.0 / 6, ALU.mult, ALU.add))
                for k in (5, 4, 3, 2, 1):
                    chain(v.tensor_scalar(lt[:, 7:8], lt[:, 7:8], lt[:, 6:7], 1.0 / k, ALU.mult, ALU.add))
                chain(v.tensor_tensor(lt[:, 9:10], lt[:, 7:8], lt[:, 6:7], ALU.mult))
                chain(v.tensor_scalar(lt[:, 8:9], lt[:, 9:10], -1.0, None, ALU.mult))
                chain(v.tensor_copy(l3[:, 0:1], lt[:, 8:9]))
                chain(v.tensor_tensor(lt[:, 10:11], lt[:, 8:9], l3[:, 0:1], ALU.subtract))
                chain(v.tensor_copy(l3[:, 1:2], lt[:, 10:11]))
                v.tensor_tensor(l3[:, 2:3], lt[:, 10:11], l3[:, 1:2], ALU.subtract).then_inc(s_ld, 1)
                rest2(2)
                rest2(3)
                return chain.n
            per1 = 1 + 8 + 8 + 1 + 3 + 5 + 2 + 3
            with dve.Fori(0, B) as b:
                got = batch(b, per1)
                assert got == per1, got
            build.dve_stage1 = base1 + B * per1
            chain.start(build.dve_stage1)

            def take_max(gr, x):
                dve.wait_ge(s_mm, MSEQ * gr + x + 1)
                if x == 0:
                    dve.wait_ge(s_mc, gr)
                v.tensor_reduce(mp[:, x:x + 1], max_ps[x % 2], AX.X, ALU.max).then_inc(s_mx, 1)

            def combine(gr):
                dve.wait_ge(s_mx, MSEQ * gr + NMAX + 2)
                v.tensor_reduce(mc[:, :], mp[:, :].rearrange("p (x k) -> p x k", k=2), AX.X, ALU.max).then_inc(s_mc, 1)
                dve.wait_ge(s_mm, MSEQ * (gr + 1))
                dve.wait_ge(s_mrow, 16 * gr)
                v.tensor_scalar(mrow[:, :], max_ps[0][0:NMAX // 2, 0:P], -1.0, None, ALU.mult).then_inc(s_mx, 1)

            dve.nop().then_inc(s_mx, 2)
            for x in range(NMAX):
                take_max(0, x)
            combine(0)
            def dve_slot(b, hg, last):
                gr = base_of(b) + hg
                nxt = not last or hg + 1 < HG
                done = 0
                for st in range(STEPS):
                    if nxt:
                        while done < max_items(st):
                            take_max(gr + 1, done)
                            done += 1
                if nxt:
                    combine(gr + 1)
            with dve.Fori(0, B - 1) as b:
                for hg in range(HG):
                    dve_slot(b, hg, False)
            for hg in range(HG):
                dve_slot(B - 1, hg, True)

            dve.wait_ge(s_sums, 16)
            v.reciprocal(sums[:, :, :], sums[:, :, :]).then_inc(s_inv, 1)
            ch3 = Chain(dve, s_c3, apart)

            def newton(r, w, y, x):
                ch3(v.reciprocal(r, y))
                ch3(v.tensor_tensor(w, r, r, ALU.mult))
                ch3(v.tensor_tensor(w, w, x, ALU.mult))
                ch3(v.tensor_scalar(w, w, -0.5, 1.5, ALU.mult, ALU.add))
                ch3(v.tensor_tensor(r, r, w, ALU.mult))

            def dve3(b, per):
                ch3.start(b * per)
                dve.wait_ge(s_ot, 32 * b + 32)
                dve.wait_ge(s_rb, 256 * b + 256)
                ch3(v.tensor_tensor(OT, OT, RB, ALU.mult))
                for n in range(4):
                    ins = v.bn_stats(st3[:, n, :], OT[:, n // 2, 512 * (n % 2):512 * (n % 2) + 512])
                ch3.apart(ins)
                for c in range(KC):
                    ins = v.bn_aggr(mvf[:, c, :], st3[:, 2 * c:2 * c + 2, :].rearrange("p n s -> p (n s)"))
                ch3(ins)
                ch3(v.tensor_tensor(q3[:, 0, :], mvf[:, :, 0], mvf[:, :, 0], ALU.mult))
                v.tensor_tensor(mvf[:, :, 1], mvf[:, :, 1], q3[:, 0, :], ALU.add).then_inc(s_fst, 1)
                dve.wait_ge(s_gmm, b + 1)
                ch3(v.tensor_copy(gst[:, :, :].rearrange("p c k -> p (c k)"), hib[2][:, 0:4]))
                ch3(v.tensor_tensor(q3[:, 0, :], gst[:, :, 0], gst[:, :, 0], ALU.mult))
                ch3(v.tensor_tensor(q3[:, 1, :], gst[:, :, 1], q3[:, 0, :], ALU.subtract))
                v.tensor_scalar(q3[:, 1, :], q3[:, 1, :], 1e-5, None, ALU.add).then_inc(s_gv, 1)
                dve.wait_ge(s_gsq, b + 1)
                newton(q3[:, 3, :], q3[:, 4, :], q3[:, 2, :], q3[:, 1, :])
                ch3(v.tensor_tensor(q3[:, 3, :], q3[:, 3, :], fcol[:, 8:10], ALU.mult))
                ch3(v.tensor_tensor(q3[:, 4, :], q3[:, 3, :], gst[:, :, 0], ALU.mult))
                ch3(v.tensor_tensor(q3[:, 4, :], fcol[:, 10:12], q3[:, 4, :], ALU.subtract))
                for c in range(KC):
                    ins = v.tensor_scalar(OT[:, c, :], OT[:, c, :], q3[:, 3, c:c + 1], q3[:, 4, c:c + 1], ALU.mult, ALU.add)
                ch3(ins)
                dve.wait_ge(s_wo, 4 * b)
                v.tensor_tensor(GT2, OT, GT, ALU.mult).then_inc(s_gt, 1)
                dve.wait_ge(s_xbo, b + 1)
                dve.wait_ge(s_ms, 4 * b)
                for n in range(4):
                    dve.wait_ge(s_wo, 4 * b + n + 1)
                    u = U[:, n % 2, :].rearrange("p (t e) -> p t e", t=2)
                    v.tensor_tensor(u, low[n][:, :].rearrange("p (t e) -> p t e", t=2),
                                    rows[:, 0, bass.ds(b, 1), :].broadcast_to([P, 2, E]), ALU.mult).then_inc(s_woev, 1)
                    dve.wait_ge(s_woev, 4 * b + n + 1)
                    xx = X[:, bass.ds(b * TB + 2 * n, 2), :]
                    ch3.apart(v.tensor_tensor(xx, xx, u, ALU.add))
                for t in range(TB):
                    ins = v.bn_stats(stx[:, t, :], X[:, bass.ds(b * TB + t, 1), :].rearrange("p o e -> p (o e)"))
                ch3.apart(ins)
                for t in range(TB):
                    ins = v.bn_aggr(mvx[:, t, :], stx[:, t, :])
                ch3(ins)
                v.tensor_scalar(q8[:, 0, :], mvx[:, :, 1], 1e-5, None, ALU.add).then_inc(s_xv, 1)
                dve.wait_ge(s_xsq, b + 1)
                newton(q8[:, 5, :], q8[:, 6, :], q8[:, 1, :], q8[:, 0, :])
                dve.wait_ge(s_nst, 16 * b)
                dve.wait_ge(s_ntr, 4 * b)
                for t in range(TB):
                    ins = v.tensor_scalar(H2[:, t, :], X[:, bass.ds(b * TB + t, 1), :].rearrange("p o e -> p (o e)"),
                                          mvx[:, t, 0:1], q8[:, 5, t:t + 1], ALU.subtract, ALU.mult)
                ins.then_inc(s_h2, 1)
                dve.wait_ge(s_h2, 2 * b + 1)
                v.tensor_tensor(H2, H2, rows[:, 2, bass.ds(b, 1), :].broadcast_to([P, TB, E]), ALU.mult).then_inc(s_h2, 1)
                dve.wait_ge(s_ms, 4 * b + 4)
                v.tensor_scalar(q8[:, 3, :], q8[:, 2, :], 1.0 / E, 1e-8, ALU.mult, ALU.add).then_inc(s_mv, 1)
                dve.wait_ge(s_msq, b + 1)
                newton(q8[:, 5, :], q8[:, 6, :], q8[:, 4, :], q8[:, 3, :])
                for t in range(TB):
                    ins = v.tensor_scalar(H2[:, t, :], H2[:, t, :], q8[:, 5, t:t + 1], None, ALU.mult)
                ins.then_inc(s_nd, 1)
                return ch3.n

            def dve_shared(b):
                dve.wait_ge(s_xsb, b + 1)
                for n in range(4):
                    dve.wait_ge(s_g2, 4 * b + n + 1)
                    u = U[:, n % 2, :].rearrange("p (t e) -> p t e", t=2)
                    v.tensor_tensor(u, hib[2 + n % 2].rearrange("p (t e) -> p t e", t=2),
                                    rows[:, 3, bass.ds(b, 1), :].broadcast_to([P, 2, E]), ALU.mult).then_inc(s_g2m, 1)
                    dve.wait_ge(s_g2m, 4 * b + n + 1)
                    xx = X[:, bass.ds(b * TB + 2 * n, 2), :]
                    v.tensor_tensor(xx, xx, u, ALU.add).then_inc(s_g2e, 1)

            def dve3b(b):
                dve.wait_ge(s_lg, b + 1)
                v.tensor_copy(LG[:, bass.ds(b * TB, TB), :].rearrange("p t e -> p (t e)"), hib[3][:, 0:TB * NE]).then_inc(s_lgc, 1)
            per3 = 4 + 3 + 5 + 3 + 1 + 4 + 2 + 5 + 5
            got = dve3(0, per3)
            assert got == per3, got
            dve3b(0)
            with dve.Fori(1, B) as b:
                dve3(b, per3)
                dve_shared(b - 1)
                dve3b(b)
            c5 = Chain(dve, s_c5)
            dve.wait_ge(s_rc, 64)
            dve.wait_ge(s_ex4, 1)
            flat = "p t e -> p (t e)"
            c5(v.tensor_scalar(PR.rearrange(flat), PR.rearrange(flat), 1.0, None, ALU.add))
            c5(v.reciprocal(PR.rearrange(flat), PR.rearrange(flat)))
            src = PR
            for k, OH in ((0, OH1), (1, OH2)):
                m, ix = m12[:, k, :], i12[:, k, :]
                c5(v.tensor_reduce(m, src, AX.X, ALU.max))
                c5(v.tensor_tensor(MK, src, m.unsqueeze(2).broadcast_to([P, NT, NE]), ALU.is_equal))
                c5(v.tensor_tensor(MK, MK, eidx, ALU.mult))
                c5(v.tensor_reduce(ix, MK, AX.X, ALU.min))
                c5(v.tensor_tensor(OH, eidx, ix.unsqueeze(2).broadcast_to([P, NT, NE]), ALU.is_equal))
                if k == 0:
                    c5(v.scalar_tensor_tensor(P2.rearrange(flat), OH.rearrange(flat), -2.0, PR.rearrange(flat), ALU.mult, ALU.add))
                    src = P2
            v.tensor_tensor(MM.rearrange(flat), OH1.rearrange(flat), OH2.rearrange(flat), ALU.add).then_inc(s_m4, 1)
            c5(v.tensor_tensor(sm, m12[:, 0, :], m12[:, 1, :], ALU.add))
            c5(v.tensor_scalar(sm, sm, 1e-6, None, ALU.add))
            c5(v.reciprocal(sm, sm))
            for k in range(2):
                c5(v.tensor_tensor(WG[:, k, :], m12[:, k, :], sm, ALU.mult))
            c5(v.memset(one32, 1.0))
            dve.wait_ge(s_pe4, 1)
            c5(v.tensor_copy(TOT.rearrange(flat), low[1][:, 0:NT * NE]))
            for e in range(NE):
                ins = v.tensor_tensor_scan(CUM[:, e, :], one32, TOT[:, :, e], 0.0, ALU.mult, ALU.add)
            c5(ins)
            c5(v.tensor_tensor(EXC, CUM.rearrange("p e t -> p t e"), TOT, ALU.subtract))
            c5(v.tensor_scalar(nti, CUM[:, :, NT - 1], 1.0 / P, (P - 1) / P - 0.5 + 0.5 / P, ALU.mult, ALU.add))
            c5(v.tensor_copy(ntf, nti))
            c5(v.tensor_tensor_scan(tinc, one32[:, 0:NE], ntf, 0.0, ALU.mult, ALU.add))
            c5(v.tensor_tensor(tslot, tinc, ntf, ALU.subtract))
            c5(v.tensor_scalar(tslot, tslot, float(P), None, ALU.mult))
            c5(v.tensor_tensor(EXC, EXC, tslot.unsqueeze(1).broadcast_to([P, NT, NE]), ALU.add))
            c5(v.tensor_tensor(POS.rearrange(flat), low[0][:, 0:NT * NE], EXC.rearrange(flat), ALU.add))
            for k, OH in ((0, OH1), (1, OH2)):
                c5(v.tensor_tensor(MK, OH, POS, ALU.mult))
                c5(v.tensor_reduce(pf[:, k, :], MK, AX.X, ALU.add))
            c5(v.tensor_copy(POSI, pf))
            c5(v.tensor_scalar(etf[:, 0:NTILE], tile_no, tinc[:, 0:1], None, ALU.is_ge))
            for e in range(1, NE - 1):
                c5(v.scalar_tensor_tensor(etf[:, 0:NTILE], tile_no, tinc[:, e:e + 1], etf[:, 0:NTILE], ALU.is_ge, ALU.add))
            v.tensor_copy(ET[:, 0:NTILE], etf[:, 0:NTILE]).then_inc(s_pos, 1)
            dve_shared(B - 1)
            dve.wait_ge(s_tokl, 16)
            v.tensor_copy(tokf[0:NTILE, :], tokn[0:NTILE, :]).then_inc(s_tokf, 1)
            dve.wait_ge(s_tokt, 1)
            v.tensor_copy(TIX, low[2][:, 0:NTILE]).then_inc(s_tix, 1)

            def hidden(i, u):
                for half in range(2):
                    dve.wait_ge(s_u2, 2 * i + half + 1)
                    if half == 0 and not (isinstance(i, int) and i < 2):
                        dve.wait_ge(s_htr, i - 1)
                    v.tensor_copy(Hn[u % 2][:, 512 * half:512 * half + 512], low[half]).then_inc(s_hn, 1)

            def result(i, it, u, e):
                dve.wait_ge(s_d, i + 1)
                if u >= 2:
                    dve.wait_ge(s_yo[u % 2], 32 * it + 16)
                else:
                    dve.wait_ge(s_yo[u % 2], 32 * it)
                v.tensor_tensor(Yt[u % 2], hib[u % 2][:, 0:E], eb2r[:, bass.ds(e, 1), :].rearrange("p o e -> p (o e)"), ALU.add).then_inc(s_y, 1)

            def dve5(it, last):
                for u in range(4):
                    i = 4 * it + u
                    e = dve.value_load(ET[0:1, bass.ds(i, 1)], min_val=0, max_val=NE - 1)
                    if not last or u + 1 < 4:
                        hidden(i + 1, u + 1)
                    result(i, it, u, e)
            dve.wait_ge(s_pos, 1)
            dve.wait_ge(s_eb2, 16)
            hidden(0, 0)
            dve5(0, False)
            with dve.Fori(1, NTILE // 4 - 1) as it:
                dve5(it, False)
            dve5(NTILE // 4 - 1, True)

            base6 = c5.n
            with dve.Fori(0, B) as b:
                c5.start(base6 + b * 2 * TB)
                for t in range(TB):
                    tt = b * TB + t
                    y0, y1, vv = Yg[t % 4][0], Yg[t % 4][1], Vg[t % 4]
                    dve.wait_ge(s_yg[t % 4], 64 * b + (64 if t >= 4 else 32))
                    c5(v.tensor_scalar(vv, y0, WG[:, 0, bass.ds(tt, 1)], None, ALU.mult))
                    ins = v.scalar_tensor_tensor(vv, y1, WG[:, 1, bass.ds(tt, 1)], vv, ALU.mult, ALU.add)
                    ins.then_inc(s_v1, 1)
                    dve.wait_ge(s_v1, TB * b + t + 1)
                    c5(v.tensor_tensor(vv, vv, rows[:, 3, bass.ds(b, 1), :].rearrange("p o e -> p (o e)"), ALU.mult))
                    xx = X[:, bass.ds(tt, 1), :].rearrange("p o e -> p (o e)")
                    v.tensor_tensor(xx, xx, vv, ALU.add).then_inc(s_fin, 1)

        @block.tensor
        def _(pe):
            t = nc.tensor
            pe.wait_ge(s_cst, 16 * build.n_cst)
            banks = low + hib
            for i in range(5):
                for ic in range(KC):
                    for oc in range(KC):
                        ins = t.transpose(banks[i][:, E * ic + P * oc:E * ic + P * oc + P], wn[:, i, oc, P * ic:P * ic + P], ident[:, :])
                ins.then_inc(s_wtr, 1)
            for src, n, col in ((wdn, H, 0), (rwn, NE, 32), (cn, B, 48)):
                for c in range(KC):
                    ins = t.transpose(hib[1][:, col + n * c:col + n * c + n], src[0:n, P * c:P * c + P], ident[0:n, 0:n])
            ins = t.transpose(hib[1][:, 56:56 + NE * HC], ebn[0:NE * HC, :], ident[0:NE * HC, 0:NE * HC])
            ins.then_inc(s_wtr, 1)
            pe.wait_ge(s_sc, 8)
            pe.wait_ge(s_wev, 6)
            for n in range(4):
                for c in range(KC):
                    ins = t.matmul(hib[2][:, 4 * n:4 * n + 4], wmod[:, c, P * n:P * n + P], scT[:, c, :], start=c == 0, stop=c == KC - 1)
            ins.then_inc(s_mod, 1)
            for n in range(8):
                b, half = n // 2, n % 2
                if n >= 4:
                    pe.wait_ge(s_modc, n - 4 + 2)
                for c in range(KC):
                    ins = t.matmul(low[n % 4], scB[:, c, b, :], wmod[:, c, 512 + 512 * half:1024 + 512 * half], start=c == 0, stop=c == KC - 1)
                ins.then_inc(s_mod, 1)
            pe.wait_ge(s_modc, 9)

            def project(b, j):
                dst = hib[j % 4]
                if j < 12:
                    w, oc, half = (0, 1, 3)[j // 4], j % 4 // 2, j % 2
                    for c in range(KC):
                        ins = t.matmul(dst, wT[:, w, c, P * oc:P * oc + P], hT[:, c, 512 * half:512 * half + 512], start=c == 0, stop=c == KC - 1)
                elif j < 16:
                    for k in range(2):
                        tt = 2 * (j - 12) + k
                        for c in range(KC):
                            ins = t.matmul(dst[:, E * k:E * k + E], hT[:, c, P * tt:P * tt + P], wT[:, 2, c, :], start=c == 0, stop=c == KC - 1)
                else:
                    for c in range(KC):
                        ins = t.matmul(dst[0:H, 0:1], smallT[:, H * c:H * c + H], mean2[:, c:c + 1], start=c == 0, stop=c == KC - 1)
                ins.then_inc(s_proj, 1)

            with pe.Fori(0, B) as b:
                for half in range(2):
                    for fc in range(KC):
                        n = 2 * half + fc
                        for k in range(4):
                            tt = 4 * half + k
                            pe.wait_ge(s_xh, TB * b + tt + 1)
                            if n == 0 and k == 0:
                                pe.wait_ge(s_hT, 4 * b)
                            ins = t.transpose(low[n][:, P * k:P * k + P], xh[:, tt, P * fc:P * fc + P], ident[:, :])
                        ins.then_inc(s_tr, 1)
                for j in range(17):
                    if j == 0:
                        pe.wait_ge(s_hT, 4 * b + 4)
                        pe.wait_ge(s_vev, 4 * b)
                        pe.wait_ge(s_zb, b)
                    elif 4 <= j < 12:
                        pe.wait_ge(s_qkev, 8 * b + j - 3)
                    elif 12 <= j < 16:
                        pe.wait_ge(s_gz, 4 * b + j - 11)
                    elif j == 16:
                        pe.wait_ge(s_vev, 4 * b + 1)
                        pe.wait_ge(s_mean, b + 1)
                    project(b, j)

            pe.wait_ge(s_hT, 4 * B)
            pe.wait_ge(s_vev, 4 * B)
            pe.wait_ge(s_zb, B)
            pe.wait_ge(s_kx, 16 * 16)
            pe.nop().then_inc(s_pv, 4)

            def max_scores(gr, hg, x, uses):
                h, qt, kh = x // 16, x % 16 // 2, x % 2
                if x == 0:
                    pe.wait_ge(s_stk[hg], 16 * 13 * uses)
                    pe.wait_ge(s_mx, MSEQ * gr + 2)
                else:
                    pe.wait_ge(s_mx, MSEQ * gr + x + 1)
                t.matmul(max_ps[x % 2], stackQ[hg][0:ROWS_QK, h, P * qt:P * qt + P],
                         stackK[hg][0:ROWS_QK, h, 512 * kh:512 * kh + 512], start=True, stop=True).then_inc(s_mm, 1)

            def max_turn(gr):
                pe.wait_ge(s_mc, gr + 1)
                t.transpose(max_ps[0][0:NMAX // 2, 0:P], mc[:, :], ident[:, :]).then_inc(s_mm, 1)

            def scores(gr, hg, st):
                qh, kt, hp = st // 16, st % 16 // 2, st % 2
                far = P * min(max(kt - 4 * qh, 0), 4)
                pe.wait_ge(s_exp, STEPS * gr + st + 1)
                for k in range(2):
                    h = 2 * hp + k
                    key = slice(P * kt, P * kt + P)
                    for c0, c1, rws in ((0, far, ROWS_FAR), (far, 512, ROWS_NEAR)):
                        if c1 > c0:
                            ins = t.matmul(score_ps[st % 2][:, k, c0:c1], stackK[hg][0:rws, h, key],
                                           stackQ[hg][0:rws, h, 512 * qh + c0:512 * qh + c1], start=True, stop=True)
                ins.then_inc(s_s, 1)

            def weigh(gr, hg, blk):
                qh, kt = blk // TB, blk % TB
                if kt == 0:
                    pe.wait_ge(s_oev, 2 * gr + qh + 1)
                if kt // 4 == qh:
                    pe.wait_ge(s_dec, 16 * gr + (2 * kt + 2 if qh == 0 else 8 + 2 * (kt - 4) + 2))
                else:
                    pe.wait_ge(s_exp, STEPS * gr + 2 * blk + 4)
                for i in range(GH):
                    ins = t.matmul(out_ps[qh][32 * i:32 * i + 32, :], Vst[hg % 2][:, kt, 32 * i:32 * i + 32],
                                   Pb[(2 * blk + i // 2) % PRING][:, i % 2, :], start=kt == 0, stop=kt == TB - 1,
                                   tile_position=(0, 32 * i))
                ins.then_inc(s_pv, 1)

            def pe_slot(b, hg, last):
                gr = base_of(b) + hg
                nxt = not last or hg + 1 < HG
                nhg = (hg + 1) % HG
                uses = b + 1 if hg + 1 < HG else b + 2
                pe.wait_ge(s_mrow, 16 * (gr + 1))
                pe.wait_ge(s_vld[hg % 2], 16 * (2 * b + hg // 2 + 1))
                done = 0
                for st in range(STEPS):
                    scores(gr, hg, st)
                    if nxt:
                        while done < max_items(st):
                            max_scores(gr + 1, nhg, done, uses)
                            done += 1
                        if st == MAX_DONE + 1:
                            max_turn(gr + 1)
                    if st % 2 == 1 and st >= 3:
                        weigh(gr, hg, st // 2 - 1)
                weigh(gr, hg, BLOCKS - 1)

            for x in range(NMAX):
                max_scores(0, 0, x, 1)
            max_turn(0)
            with pe.Fori(0, B - 1) as b:
                for hg in range(HG):
                    pe_slot(b, hg, False)
            for hg in range(HG):
                pe_slot(B - 1, hg, True)

            def pe3(b):
                pe.wait_ge(s_fst, b + 1)
                t.matmul(hib[2][:, 0:4], head_avg[:, :], mvf[:, :, :].rearrange("p c k -> p (c k)"), start=True, stop=True).then_inc(s_gmm, 1)
                pe.wait_ge(s_gt, b + 1)
                for n in range(4):
                    if n == 0:
                        pe.wait_ge(s_nT, 4 * b)
                    for k in range(2):
                        tt = 2 * n + k
                        for c in range(KC):
                            ins = t.matmul(low[n][:, E * k:E * k + E], OT[:, c, P * tt:P * tt + P], wT[:, 4, c, :], start=c == 0, stop=c == KC - 1)
                    ins.then_inc(s_wo, 1)

            def pe_shared(b):
                pe.wait_ge(s_sw, 64)
                pe.wait_ge(s_gv, b + 1)
                for half in range(2):
                    for hc in range(HC):
                        n = HC * half + hc
                        if n >= 2:
                            pe.wait_ge(s_relu, 16 * b + n - 1)
                        else:
                            pe.wait_ge(s_relu, 16 * b)
                        for c in range(KC):
                            ins = t.matmul(hib[n % 2], sw1[:, c, P * hc:P * hc + P], NTr[:, c, 512 * half:512 * half + 512], start=c == 0, stop=c == KC - 1)
                        ins.then_inc(s_g1, 1)
                    pe.wait_ge(s_relu, 16 * b + 8 * half + 8)
                    for m in range(2):
                        n = 2 * half + m
                        if n == 0:
                            pe.wait_ge(s_gv, b + 1)
                            pe.wait_ge(s_g2m, 4 * b)
                            pe.wait_ge(s_lgc, b + 1)
                        elif n >= 2:
                            pe.wait_ge(s_g2m, 4 * b + n - 1)
                        for k in range(2):
                            for hc in range(HC):
                                ins = t.matmul(hib[2 + n % 2][:, E * k:E * k + E], HT[:, hc, P * (2 * m + k):P * (2 * m + k) + P], sw2[:, hc, :],
                                               start=hc == 0, stop=hc == HC - 1)
                        ins.then_inc(s_g2, 1)

            def pe3b(b):
                pe.wait_ge(s_n, b + 1)
                pe.wait_ge(s_woev, 4 * b + 4)
                for n in range(4):
                    half, fc = n // 2, n % 2
                    for k in range(4):
                        ins = t.transpose(low[n][:, P * k:P * k + P], H2[:, 4 * half + k, P * fc:P * fc + P], ident[:, :])
                    ins.then_inc(s_ntr, 1)
                pe.wait_ge(s_nT, 4 * b + 4)
                pe.wait_ge(s_g2m, 4 * b)
                for tt in range(TB):
                    for c in range(KC):
                        ins = t.matmul(hib[3][:, NE * tt:NE * tt + NE], NTr[:, c, P * tt:P * tt + P], smallT[:, 32 + NE * c:32 + NE * c + NE],
                                       start=c == 0, stop=c == KC - 1)
                ins.then_inc(s_lg, 1)

            pe.wait_ge(s_mx, MSEQ * NG + 2)
            pe.wait_ge(s_oev, 2 * NG + 2)
            pe.wait_ge(s_exp, STEPS * NG + 2)
            pe3(0)
            pe3b(0)
            with pe.Fori(1, B) as b:
                pe3(b)
                pe_shared(b - 1)
                pe3b(b)
            pe.wait_ge(s_m4, 1)
            pe.wait_ge(s_nT, 4 * B)
            mm = MM.rearrange("p t e -> p (t e)")
            t.matmul(low[0][:, 0:NT * NE], before, mm, start=True, stop=True)
            t.matmul(low[1][:, 0:NT * NE], ones[:, :], mm, start=True, stop=True).then_inc(s_pe4, 1)
            pe_shared(B - 1)
            pe.wait_ge(s_tokf, 1)
            t.transpose(low[2][:, 0:NTILE], tokf[0:NTILE, :], ident[0:NTILE, 0:NTILE]).then_inc(s_tokt, 1)

            def x_turn(i, it, u):
                pe.wait_ge(s_gx[u % 2], 32 * it + (16 if u % 4 < 2 else 32))
                if not (isinstance(i, int) and i < 2):
                    pe.wait_ge(s_xT, i - 1)
                for c in range(KC):
                    ins = t.transpose(hib[2 + u % 2][:, P * c:P * c + P], Xg[u % 2][:, P * c:P * c + P], ident[:, :])
                ins.then_inc(s_xtr, 1)

            def up(i, u, e):
                pe.wait_ge(s_xT, i + 1)
                for half in range(2):
                    if isinstance(i, int) and i == 0:
                        pass
                    else:
                        pe.wait_ge(s_hn, 2 * i + half - 1)
                    for c in range(KC):
                        ins = t.matmul(low[half], XT[u % 2][:, c, :], W[:, bass.ds(e, 1), 0, 1024 * c + 512 * half:1024 * c + 512 * half + 512].rearrange("p o x -> p (o x)"),
                                       start=c == 0, stop=c == KC - 1)
                    ins.then_inc(s_u2, 1)

            def hidden_turn(i, u):
                if isinstance(i, int) and i == 0:
                    pass
                else:
                    pe.wait_ge(s_hr, HC * i)
                for hc in range(HC):
                    if hc % 4 == 0:
                        pe.wait_ge(s_hn, 2 * i + hc // 4 + 1)
                    ins = t.transpose(low[2 + hc // 4][:, P * (hc % 4):P * (hc % 4) + P], Hn[u % 2][:, P * hc:P * hc + P], ident[:, :])
                ins.then_inc(s_htr, 1)

            def down(i, u, e):
                if not (isinstance(i, int) and i < 2):
                    pe.wait_ge(s_y, i - 1)
                for hc in range(HC):
                    pe.wait_ge(s_hr, HC * i + hc + 1)
                    ins = t.matmul(hib[u % 2][:, 0:E], Ht[u % 2][:, hc, :], W[:, bass.ds(e, 1), 1, E * hc:E * hc + E].rearrange("p o x -> p (o x)"),
                                   start=hc == 0, stop=hc == HC - 1)
                ins.then_inc(s_d, 1)

            def expert_of(i):
                return pe.value_load(ET[0:1, bass.ds(i, 1)], min_val=0, max_val=NE - 1)

            def pe5(it, last):
                e = [expert_of(4 * it + u) for u in range(4 if last else 5)]
                for u in range(4):
                    i = 4 * it + u
                    if not last or u + 2 < 4:
                        x_turn(i + 2, it + (u + 2) // 4, (u + 2) % 4)
                    if not last or u + 1 < 4:
                        up(i + 1, u + 1, e[u + 1])
                    hidden_turn(i, u)
                    down(i, u, e[u])
            pe.wait_ge(s_pos, 1)
            pe.wait_ge(s_wl, 32 * NE)
            pe.wait_ge(s_g2e, 4 * B)
            pe.wait_ge(s_tix, 1)
            x_turn(0, 0, 0)
            x_turn(1, 0, 1)
            up(0, 0, expert_of(0))
            pe5(0, False)
            with pe.Fori(1, NTILE // 4 - 1) as it:
                pe5(it, False)
            pe5(NTILE // 4 - 1, True)


def names():
    return ["L0_attn_x", "L0_attn_wq", "L0_attn_bq", "L0_attn_wk", "L0_attn_bk", "L0_attn_wv", "L0_attn_bv",
            "L0_attn_wg", "L0_attn_bg", "L0_attn_wo", "L0_attn_bo", "L0_attn_wd", "L0_attn_bd", "L0_attn_gamma",
            "L0_attn_beta", "L0_ffn_norm_weight", "L0_ffn_router_w", "L0_ffn_sw1", "L0_ffn_sb1", "L0_ffn_sw2",
            "L0_ffn_sb2", "L0_ffn_ew1", "L0_ffn_eb1", "L0_ffn_ew2", "L0_ffn_eb2", "L0_c", "L0_wmod"]

def kernel(**inputs):
    import concourse.bacc as bacc
    from concourse.bass_utils import run_bass_kernel_spmd

    nc = bacc.Bacc("TRN2", target_bir_lowering=False, num_devices=1)
    given = {name: np.ascontiguousarray(inputs[name]) for name in names()}
    given.update(constants())
    handles = {name: nc.dram_tensor(f"in_{name}_dram", x.shape, mybir.dt.from_np(x.dtype), kind="ExternalInput").ap()
               for name, x in given.items()}
    out = nc.dram_tensor("out_0_dram", (B, T, E), F32, kind="ExternalOutput").ap()
    build(nc, handles, out)
    done = run_bass_kernel_spmd(nc, [{f"in_{name}_dram": x for name, x in given.items()}], core_ids=[0])
    return done.results[0]["out_0_dram"]
```

```python
from contextlib import ExitStack

import numpy as np

import concourse.bass as bass
from concourse import mybir

F32 = mybir.dt.float32
BF16 = mybir.dt.bfloat16
I32 = mybir.dt.int32
U32 = mybir.dt.uint32
ALU = mybir.AluOpType
ACT = mybir.ActivationFunctionType
AX = mybir.AxisListType

P = 128
B, T, E = 4, 1024, 256
H = 16
HD = E // H
NT = B * T // P
TB = T // P
KC = E // P
NE = 8
HID = 1024
HC = HID // P
GH = 4
HG = H // GH
NG = B * HG
QH = T // 512
LN2 = float(np.log(2.0))

Q_PART = [0, 0, 1, 1, 0, 2]
K_PART = [0, 1, 0, 1, 2, 0]
ROWS_QK = 16 * len(Q_PART)
ROW_M = ROWS_QK
ROWS_NEAR = ROWS_QK + 1
N_EXT = 9
ROWS_FAR = ROWS_NEAR + N_EXT

STEPS = 2 * QH * TB
BLOCKS = STEPS // 2
NMAX = GH * TB * 2
MSEQ = NMAX + 1
PRING = 8
PLACES = 4 * BLOCKS - 5
OPEN = 1
SLOTS = 2 * B * T + NE * P
NTILE = SLOTS // P


def constants():
    f = np.float32
    k = np.arange(T)
    inv = (1.0 / 10000.0 ** (np.arange(0, HD, 2, dtype=f) / f(HD))).astype(f)
    ang = np.arange(T, dtype=f)[:, None] * inv[None, :]
    ang = np.concatenate([ang, ang], axis=-1).astype(f)
    d = np.arange(P) % HD
    cos = np.cos(ang)[:, d].T.astype(f)
    sin = (np.sin(ang)[:, d] * np.where(d % 2 == 0, -1.0, 1.0)[None, :]).T.astype(f)
    ident = np.eye(P, dtype=f)
    relu = np.maximum(np.arange(P)[:, None] - np.arange(P)[None, :], 0).astype(f)
    before = (np.arange(P)[:, None] < np.arange(P)[None, :]).astype(f)
    same_head = (np.arange(P)[:, None] // HD == np.arange(P)[None, :] // HD).astype(f) / f(HD)
    hi, lo = (k // 8 * 8).astype(f), (k % 8).astype(f)
    one = np.ones(T, f)
    kext = (np.stack([one] + [hi] * 3 + [lo] * 3 + [one] * 3).view(np.uint32) >> 16).astype(np.uint16)
    qrow = np.broadcast_to(k.astype(f), (H, T)).copy()
    eidx = np.broadcast_to(np.tile(np.arange(NE) - NE, NT).astype(f), (P, NT * NE)).copy()
    tile = np.broadcast_to(np.arange(NTILE).astype(f), (P, NTILE)).copy()
    token = (np.arange(NT)[None, :] * P + np.arange(P)[:, None]).astype(np.int32)
    return {"c_cos": cos, "c_sin": np.ascontiguousarray(sin), "c_ident": ident, "c_relu": relu, "c_before": before,
            "c_head": same_head, "c_kext": kext, "c_qrow": qrow, "c_token": token, "c_eidx": eidx, "c_tile": tile}


def max_items(place):
    return min(NMAX, -(-NMAX * (place + 1) // PLACES))


class Chain:

    def __init__(self, eng, sem, alone=None):
        self.eng, self.sem, self.n, self.base, self.alone = eng, sem, 0, 0, alone

    def start(self, base):
        self.base, self.n = base, 0

    def __call__(self, ins):
        self.n += 1
        ins.then_inc(self.sem, 1)
        self.eng.wait_ge(self.sem, self.base + self.n)

    def apart(self, ins):
        self.n += 1
        ins.then_inc(self.sem, 1)
        self.eng.wait_ge(self.sem, self.alone(self.eng, self.base + self.n))


def build(nc, a, out, dbg=None, upto=99):
    ctx = ExitStack()
    with ctx:
        def sb(name, shape, dt=F32):
            return ctx.enter_context(nc.sbuf_tensor(name, shape, dt))

        def sem(name):
            return ctx.enter_context(nc.semaphore(name))

        def dram(name, shape, dt=F32):
            return nc.dram_tensor(name, shape, dt).ap() if not dbg else nc.dram_tensor(name, shape, dt, kind="ExternalOutput").ap()

        qkS = dram("qkS", [B, 2, 3, E, T], BF16)
        qeS = dram("qeS", [B, H, N_EXT, T], BF16)
        vS = dram("vS", [B, P, TB, H * 32])
        gS = dram("gS", [B, E, T])
        oS = dram("oS", [B, E, T])
        ldS = dram("ldS", [B, H])
        sS = dram("sS", [B, H, T])
        rS = dram("rS", [B, H, T])
        nS = dram("nS", [B * T, E])
        tokS = dram("tokS", [SLOTS, 1], I32)
        yS = dram("yS", [SLOTS, E])

        bank = [ctx.enter_context(nc.psum_tensor(f"bank{i}", [P, 512], F32)) for i in range(4, 8)]
        score_ps = [ctx.enter_context(nc.psum_tensor(f"score{i}", [P, 2, 512], F32)) for i in range(2)]
        low = [score_ps[0][:, 0, :], score_ps[0][:, 1, :], score_ps[1][:, 0, :], score_ps[1][:, 1, :]]
        hib = [t[:, :] for t in bank]
        max_ps = hib[0:2]
        out_ps = hib[2:4]

        X = sb("X", [P, NT, E])
        W = sb("W", [P, NE, 2, 2048])
        ident = sb("ident", [P, P])
        ones = sb("ones", [P, P])
        relu_t = sb("relu_t", [P, P])
        head_avg = sb("head_avg", [P, P])
        wT = sb("wT", [P, 5, KC, E])
        rows = sb("rows", [P, 4, B, E])
        modT = sb("modT", [P, 4, B])
        smallT = sb("smallT", [P, 56 + NE * HC])
        fcol = sb("fcol", [P, 12])
        bv_row = sb("bv_row", [P, E])
        bo_row = sb("bo_row", [P, E])
        mv1 = sb("mv1", [P, NT, 2])
        rst1 = sb("rst1", [P, NT])
        st6 = sb("st6", [P, NT, 6])
        tmpA = sb("tmpA", [P, NT])
        tmpB = sb("tmpB", [P, NT])
        LDb = sb("LDb", [P, B * H])

        def region(e, k, n, dt=F32):
            ap = W[:, :, :, :].rearrange("p e w x -> p (e w x)")[:, e * 4096 + k:e * 4096 + k + n]
            return ap if dt == F32 else ap.bitcast(dt)

        stackQ = [region(4 + i, 0, 2048, BF16).rearrange("p (h t) -> p h t", h=GH) for i in range(4)]
        stackK = [region(4 + i, 2048, 2048, BF16).rearrange("p (h t) -> p h t", h=GH) for i in range(4)]

        ctx1 = ExitStack()
        if True:
            with ctx1:
                def sb1(name, shape, dt=F32):
                    return ctx1.enter_context(nc.sbuf_tensor(name, shape, dt))
                wn = region(0, 0, 2560).rearrange("p (w c e) -> p w c e", w=5, c=KC)
                wmod = region(0, 2560, 3072).rearrange("p (c e) -> p c e", c=KC)
                scT = region(1, 1536, 8).rearrange("p (c b) -> p c b", c=KC)
                scB = region(1, 1544, 1024).rearrange("p (c b x) -> p c b x", c=KC, b=B)
                wdn = region(1, 2568, 256)
                rwn = region(1, 2824, 256)
                cn = region(1, 3080, 256)
                cE = region(1, 3336, 8).rearrange("p (c b) -> p c b", c=KC)
                mag = region(1, 3352, 256)
                sgn = region(1, 3608, 256)
                ebn = region(1, 3864, P)
        csT = sb("csT", [P, 2, T])
        cosT, sinT = csT[:, 0, :], csT[:, 1, :]
        sw2 = csT[:, :, :].rearrange("p a (b e) -> p (a b) e", e=E)
        OT = region(4, 0, 2048).rearrange("p (c t) -> p c t", c=KC)
        GT = region(4, 2048, 2048).rearrange("p (c t) -> p c t", c=KC)
        RB = region(5, 0, 2048).rearrange("p (c t) -> p c t", c=KC)
        H2 = region(5, 2048, 2048).rearrange("p (t e) -> p t e", t=TB)
        NTr = region(6, 0, 2048).rearrange("p (c t) -> p c t", c=KC)
        sw1 = region(6, 2048, 2048).rearrange("p (c h) -> p c h", c=KC)
        HT = region(7, 0, 4096).rearrange("p (c t) -> p c t", c=HC)
        GT2 = OT
        U = wT[:, 0:2, :, :].rearrange("p w c e -> p w (c e)")
        sums = wT[:, 2, :, :].rearrange("p c e -> p (c e)").rearrange("p (b x) -> p b x", b=B)
        misc = sb("misc", [P, 4, E])
        qrow = misc[0:H, :, :].rearrange("p k e -> p (k e)")
        gabo, gbsb, sb2_row, nw_row = (misc[:, i, :] for i in range(4))
        sb1c = sb("sb1c", [P, HC])
        st3 = sb("st3", [P, 4, 6])
        mvf = sb("mvf", [P, KC, 2])
        gst = sb("gst", [P, KC, 2])
        q3 = sb("q3", [P, 8, KC])
        stx = sb("stx", [P, TB, 6])
        mvx = sb("mvx", [P, TB, 2])
        q8 = sb("q8", [P, 8, TB])
        LG = sb("LG", [P, NT, NE])
        xh = region(2, 0, 2048).rearrange("p (t e) -> p t e", t=TB)
        hT = region(2, 2048, 2048).rearrange("p (c t) -> p c t", c=KC)
        qs = region(3, 0, 4096).rearrange("p (c t) -> p c t", c=4)
        gz = region(4, 0, 2048).rearrange("p (n t) -> p n t", n=4)
        ge = region(4, 2048, 2048).rearrange("p (n t) -> p n t", n=4)
        Vx = region(5, 0, 4096).rearrange("p (t h c) -> p t h c", t=TB, h=H)
        pb = region(6, 0, 4096 + 2048, BF16).rearrange("p (c k t) -> p c k t", c=4, k=3)
        qe = W[:, 7, 1, :].bitcast(BF16)
        rope_s = region(0, 0, 2048).rearrange("p (k t) -> p k t", k=2)
        rope_1 = region(0, 2048, 2048).rearrange("p (k t) -> p k t", k=2)
        rope_r = region(7, 2048, 2048).rearrange("p (k t) -> p k t", k=2)
        qeb = region(1, 0, 3072, BF16)[0:H].rearrange("p (r t) -> p r t", r=6)
        qc = region(1, 3072, 1024)[0:H]
        hsum = sb("hsum", [P, 4])
        mean2 = sb("mean2", [P, 2])
        bd16 = sb("bd16", [H, 1])
        lt = sb("lt", [H, 16])
        l3 = sb("l3", [H, 3], BF16)
        Pb = [region(0, 1024 * i, 1024).rearrange("p (h t) -> p h t", h=2) for i in range(4)] + \
             [region(1, 1024 * i, 1024).rearrange("p (h t) -> p h t", h=2) for i in range(4)]
        Vst = [region(2, 1024 * i, 1024).rearrange("p (t c) -> p t c", t=TB) for i in range(2)]
        Dec = [region(2, 2048 + 512 * i, 512).rearrange("p (h t) -> p h t", h=GH) for i in range(2)]
        Os = [region(3, 512 * i, 512) for i in range(2)]
        mp = sb("mp", [P, NMAX])
        mc = sb("mc", [P, NMAX // 2])
        mrow = sb("mrow", [NMAX // 2, P], BF16)

        def route(i):
            return region(4, 256 * i, 256).rearrange("p (t e) -> p t e", e=NE)
        PR, MK, OH1, OH2, P2, MM, TOT, EXC, POS = (route(i) for i in range(9))
        CUM = region(4, 2304, 256).rearrange("p (e t) -> p e t", e=NE)
        one32 = region(4, 2560, 32)
        m12 = region(4, 2592, 64).rearrange("p (k t) -> p k t", k=2)
        i12 = region(4, 2656, 64).rearrange("p (k t) -> p k t", k=2)
        sm = region(4, 2720, 32)
        pf = region(4, 2752, 64).rearrange("p (k t) -> p k t", k=2)
        ntf = region(4, 2816, NE)
        nti = region(4, 2824, NE, I32)
        tinc = region(4, 2832, NE)
        tslot = region(4, 2840, NE)
        etf = region(4, 2848, 80)
        eidx = region(5, 0, 256).rearrange("p (t e) -> p t e", e=NE)
        before = region(5, 256, P)
        tile_no = region(5, 384, NTILE)
        zero_t = region(5, 512, P, I32)
        tokn = region(5, 640, P, I32)
        tokf = region(5, 768, P)
        st_words = st6[:, :, :].rearrange("p t s -> p (t s)")
        WG = mv1[:, :, :].rearrange("p t k -> p k t")
        POSI = st_words[:, 72:136].bitcast(I32).rearrange("p (k t) -> p k t", k=2)
        ET = sb("ET", [P, 80], I32)
        TIX = st_words[:, 0:NTILE].bitcast(I32)
        TK = sb("TK", [P, NT], I32)
        GI = sb("GI", [P, 4], I32)
        SC = sb("SC", [P, 3, 4], I32)
        PC = sb("PC", [P, 2, TB], I32)
        Hn = [wT[:, 0:2, :, :].rearrange("p w c e -> p (w c e)"), csT[:, 1, :]]
        Ht = [wT[:, 2:4, :, :].rearrange("p w c e -> p (w c e)"), csT[:, 0, :]]
        Ht = [h.rearrange("p (c t) -> p c t", c=HC) for h in Ht]
        Yt = [wT[:, 4, i, :] for i in range(2)]
        Xg = [misc[:, i, :] for i in range(2)]
        XT = [misc[:, 2 + i, :].rearrange("p (c t) -> p c t", c=KC) for i in range(2)]
        eb2r = rows[:, 0:2, :, :].rearrange("p k b e -> p (k b) e")
        Yg = [[region(0, 256 * (2 * i + k), 256) for k in range(2)] for i in range(4)]
        Vg = [region(1, 256 * i, 256) for i in range(4)]

        s_x = [sem(f"x_loaded{b}") for b in range(B)]
        s_cst = sem("constants_loaded")
        s_ones = sem("ones_set")
        s_wtr = sem("weights_transposed")
        s_wev = sem("weights_copied")
        s_ce = sem("c_exp")
        s_sc = sem("c_silu")
        s_mod = sem("modulation_made")
        s_modc = sem("modulation_copied")
        s_var = sem("variance_ready")
        s_sq = sem("sqrt_done")
        s_dve = sem("dve_chain")
        s_pool = sem("pool_chain")
        s_act = sem("act_chain")
        s_xh = sem("x_normalised")
        s_tr = sem("h_transposed")
        s_hT = sem("h_copied")
        s_proj = sem("projection_made")
        s_qkev = sem("qk_copied")
        s_gexp = sem("gate_exp")
        s_gz = sem("gate_z")
        s_vev = sem("v_copied")
        s_gate = sem("gate_made")
        s_cosm = sem("rope_cos_part")
        s_rr = sem("roped")
        s_p1 = sem("part1")
        s_r1 = sem("rest1")
        s_p2 = sem("part2")
        s_p3 = sem("part3")
        s_pout = sem("parts_stored")
        s_gout = sem("gate_stored")
        s_vout = sem("v_stored")
        s_mean = sem("h_mean")
        s_z16 = sem("decay_logit")
        s_zb = sem("decay_z")
        s_e16 = sem("decay_exp")
        s_pd = sem("decay_pd")
        s_ld = sem("log_decay")
        s_qe = sem("decay_rows")
        s_qeo = sem("decay_rows_stored")
        s_ldo = sem("log_decay_stored")
        s_ldb = sem("log_decay_loaded")
        s_kx = sem("key_rows_loaded")
        s_stk = [sem(f"stack_loaded{i}") for i in range(4)]
        s_vld = [sem(f"v_loaded{i}") for i in range(2)]
        s_mm = sem("max_scores")
        s_mx = sem("max_taken")
        s_mc = sem("max_combined")
        s_mrow = sem("max_row_placed")
        s_s = sem("scores_made")
        s_exp = sem("exp_done")
        s_dect = sem("decay_tables")
        s_dec = sem("decay_applied")
        s_pv = sem("pv_done")
        s_oev = sem("out_copied")
        s_od = [sem(f"out_stored{i}") for i in range(2)]

        s_sums = sem("sums_loaded")
        s_inv = sem("sums_inverted")
        s_ro = sem("inverses_stored")
        s_ot = sem("attention_out_loaded")
        s_rb = sem("inverses_loaded")
        s_sw = sem("shared_weights_loaded")
        s_fst = sem("feature_stats")
        s_gmm = sem("head_stats")
        s_gst = sem("head_stats_copied")
        s_gt = sem("gated")
        s_xbo = sem("x_plus_bias")
        s_wo = sem("wo_made")
        s_woev = sem("wo_copied")
        s_h2 = sem("h2_made")
        s_n = sem("n_made")
        s_nst = sem("n_stored")
        s_ntr = sem("n_transposed")
        s_nT = sem("n_copied")
        s_lg = sem("logits_made")
        s_lgc = sem("logits_copied")
        s_g1 = sem("shared_up")
        s_relu = sem("shared_relu")
        s_g2 = sem("shared_down")
        s_g2m = sem("shared_scaled")
        s_g2e = sem("shared_added")
        s_c3 = sem("front_a_chain")
        s_c3b = sem("front_b_chain")
        s_c3c = sem("tail_chain")
        s_xsb = sem("x_plus_shared_bias")
        s_rc = sem("routing_tables_loaded")
        s_wl = sem("expert_weights_loaded")
        s_pe4 = sem("routing_counts")
        s_ex4 = sem("routing_exp")
        s_z4 = sem("slot_table_zeroed")
        s_zt = sem("zero_tile")
        s_m4 = sem("choice_made")
        s_pos = sem("positions_ready")
        s_sc4 = sem("scatter_index_staged")
        s_scat = sem("tokens_scattered")
        s_tokl = sem("slot_tokens_loaded")
        s_tokf = sem("slot_tokens_float")
        s_tokt = sem("slot_tokens_transposed")
        s_tix = sem("slot_tokens_ready")
        s_eb2 = sem("expert_bias_loaded")
        s_gi = sem("gather_index_staged")
        s_gx = [sem(f"tokens_gathered{i}") for i in range(2)]
        s_xtr = sem("x_tile_transposed")
        s_xT = sem("x_tile_copied")
        s_u2 = sem("expert_up_half")
        s_hn = sem("hidden_copied")
        s_htr = sem("hidden_transposed")
        s_hr = sem("hidden_relu")
        s_d = sem("expert_down")
        s_y = sem("y_copied")
        s_yo = [sem(f"y_stored{i}") for i in range(2)]
        s_pc = sem("combine_index_staged")
        s_yg = [sem(f"y_gathered{i}") for i in range(4)]
        s_v1 = sem("combined")
        s_fin = sem("x_final")
        s_out = sem("x_stored")
        s_c5 = sem("dve_chain5")

        block = ctx.enter_context(nc.Block())

        count_reg = {}

        def apart(eng, count):
            if not isinstance(count, int):
                if eng not in count_reg:
                    count_reg[eng] = eng.alloc_register(f"count{len(count_reg)}")
                eng.reg_add(count_reg[eng], count, 0)
                count = count_reg[eng]
            eng.wait_ge(s_ones, 1)
            return count

        def base_of(b):
            return b * HG

        @block.sync
        def _(sp):
            for opened in (s_ldo, s_pout, s_gout, s_vout, s_qeo, s_od[0], s_od[1], s_mrow):
                sp.nop().then_inc(opened, OPEN)
            def cst(dst, src):
                sp.dma_start(dst, src).then_inc(s_cst, 16)
                cst.n += 1
            cst.n = 0
            cst(ident[:, :], a["c_ident"])
            for i, w in enumerate(("wq", "wk", "wv", "wg", "wo")):
                cst(wn[:, i, :, :], a["L0_attn_" + w].rearrange("(c p) e -> p c e", p=P))
            cst(cn[0:B, :], a["L0_c"])
            cst(wdn[0:H, :], a["L0_attn_wd"])
            cst(rwn[0:NE, :], a["L0_ffn_router_w"])
            cst(ebn[0:NE * HC, :], a["L0_ffn_eb1"].rearrange("e (c p) -> (e c) p", p=P))
            for b in range(B):
                sp.dma_start(X[:, TB * b:TB * b + TB, :],
                             a["L0_attn_x"][b].rearrange("(t p) e -> p t e", p=P)).then_inc(s_x[b], 16)
            cst(wmod, a["L0_wmod"].rearrange("(c p) e -> p c e", p=P))
            cst(cosT, a["c_cos"])
            cst(sinT, a["c_sin"])
            cst(relu_t[:, :], a["c_relu"])
            cst(head_avg[:, :], a["c_head"])
            cst(qrow, a["c_qrow"])
            for i, w in enumerate(("bq", "bk", "bg", "gamma", "beta")):
                col = (0, 2, 4, 8, 10)[i]
                for c in range(KC):
                    cst(fcol[:, col + c:col + c + 1], a["L0_attn_" + w][P * c:P * c + P].unsqueeze(1))
            cst(bv_row[:, :], a["L0_attn_bv"].unsqueeze(0).broadcast_to([P, E]))
            cst(bo_row[:, :], a["L0_attn_bo"].unsqueeze(0).broadcast_to([P, E]))
            cst(bd16[:, :], a["L0_attn_bd"].unsqueeze(1))
            for c in range(HC):
                cst(sb1c[:, c:c + 1], a["L0_ffn_sb1"][P * c:P * c + P].unsqueeze(1))
            build.n_cst = cst.n

            with sp.Fori(0, B) as b:
                for c in range(4):
                    w, oc = c // 2, c % 2
                    sp.wait_ge(s_p3, OPEN + 4 * b + c + 1)
                    sp.dma_start(qkS[bass.ds(b, 1), w, :, P * oc:P * oc + P, :].rearrange("o k p t -> p (o k) t"),
                                 pb[:, c, :, :]).then_inc(s_pout, 16)
                sp.wait_ge(s_gate, OPEN + 4 * b + 4)
                for oc in range(KC):
                    sp.dma_start(gS[bass.ds(b, 1), P * oc:P * oc + P, :].rearrange("o p t -> p (o t)"),
                                 gz[:, 2 * oc:2 * oc + 2, :].rearrange("p n t -> p (n t)")).then_inc(s_gout, 16)
                sp.wait_ge(s_vev, OPEN + 4 * b + 4)
                sp.dma_start(vS[bass.ds(b, 1), :, :, :].rearrange("o p t c -> p (o t) c"),
                             Vx.rearrange("p t h c -> p t (h c)")).then_inc(s_vout, 16)
                sp.wait_ge(s_ld, b + 1)
                sp.dma_start(ldS[bass.ds(b, 1), :].rearrange("o h -> h o"), lt[:, 8:9]).then_inc(s_ldo, 16)
                sp.wait_ge(s_qe, OPEN + b + 1)
                for r0, r1, src in ((0, 3, 0), (3, 6, 0), (6, 9, 3)):
                    sp.dma_start(qeS[bass.ds(b, 1), :, r0:r1, :].rearrange("o h r t -> h (o r) t"),
                                 qeb[:, src:src + 3, :]).then_inc(s_qeo, 16)
            sp.wait_ge(s_ldo, OPEN + 16 * B)
            sp.dma_start(LDb[:, :], ldS.rearrange("b h -> (b h)").unsqueeze(0).broadcast_to([P, B * H])).then_inc(s_ldb, 16)
            sp.wait_ge(s_pout, OPEN + 64 * B)
            sp.wait_ge(s_gout, OPEN + 32 * B)
            sp.wait_ge(s_vout, OPEN + 16 * B)
            sp.wait_ge(s_qeo, OPEN + 48 * B)
            for i in range(4):
                for h in range(GH):
                    sp.dma_start(stackK[i][ROW_M:ROWS_FAR, h, :], a["c_kext"].bitcast(BF16)).then_inc(s_kx, 16)

            def load_stack(b, hg):
                for j in range(6):
                    for w, part, st in ((0, Q_PART[j], stackQ[hg]), (1, K_PART[j], stackK[hg])):
                        src = qkS[bass.ds(b, 1), w, part, 64 * hg:64 * hg + 64, :].rearrange("o (h d) t -> d (o h) t", d=HD)
                        sp.dma_start(st[16 * j:16 * j + 16, :, :], src).then_inc(s_stk[hg], 16)
                sp.dma_start(stackQ[hg][ROWS_NEAR:ROWS_FAR, :, :],
                             qeS[bass.ds(b, 1), GH * hg:GH * hg + GH, :, :].rearrange("o h r t -> r (o h) t")).then_inc(s_stk[hg], 16)

            def load_v(b, hg):
                sp.dma_start(Vst[hg % 2], vS[bass.ds(b, 1), :, :, P * hg:P * hg + P].rearrange("o p t c -> p (o t) c")).then_inc(s_vld[hg % 2], 16)

            def place_max(g):
                sp.wait_ge(s_mx, MSEQ * (g + 1) + 2)
                st = stackQ[place_max.hg]
                sp.dma_start(st[ROW_M:ROW_M + 1, :, :].rearrange("o h (q t) -> o (h q) t", t=P), mrow[:, :]).then_inc(s_mrow, 16)

            def store_out(b, hg, qh):
                g = base_of(b) + hg
                sp.wait_ge(s_oev, 2 * g + qh + 3)
                for i in range(GH):
                    f0 = (GH * hg + i) * HD
                    sp.dma_start(sS[bass.ds(b, 1), GH * hg + i, 512 * qh:512 * qh + 512],
                                 Os[qh][32 * i + HD:32 * i + HD + 1, :]).then_inc(s_od[qh], 16)
                    sp.dma_start(oS[bass.ds(b, 1), f0:f0 + HD, 512 * qh:512 * qh + 512].rearrange("o p t -> p (o t)"),
                                 Os[qh][32 * i:32 * i + HD, :]).then_inc(s_od[qh], 16)

            def slot(b, hg, last):
                g = base_of(b) + hg
                nxt = hg + 2
                if not last or nxt < HG:
                    if nxt >= 4:
                        load_stack(b + 1, nxt - 4)
                    else:
                        load_stack(b, nxt)
                if not last or hg + 1 < HG:
                    if hg + 1 == HG:
                        load_v(b + 1, 0)
                    else:
                        load_v(b, hg + 1)
                store_out(b, hg, 0)
                if not last or hg + 1 < HG:
                    place_max.hg = (hg + 1) % HG
                    place_max(g + 1)
                store_out(b, hg, 1)

            load_stack(0, 0)
            load_v(0, 0)
            load_stack(0, 1)
            place_max.hg = 0
            place_max(0)

            def load_sums(b0, b1):
                sp.dma_start(sums[:, b0:b1, :], sS[b0:b1, :, :].rearrange("b h (q x) -> (h q) b x", x=P)).then_inc(s_sums, 16)

            def store_inverses(b0, b1, count):
                sp.dma_start(rS[b0:b1, :, :].rearrange("b h (q x) -> (h q) b x", x=P), sums[:, b0:b1, :]).then_inc(s_ro, 16)
                sp.wait_ge(s_ro, count)

            def load3(b):
                sp.dma_start(OT, oS[bass.ds(b, 1), :, :].rearrange("o (c p) t -> p (o c) t", p=P)).then_inc(s_ot, 16)
                for h in range(H):
                    sp.dma_start(RB[HD * (h % 8):HD * (h % 8) + HD, h // 8, :],
                                 rS[bass.ds(b, 1), h, :].broadcast_to([HD, T])).then_inc(s_rb, 16)
                sp.dma_start(GT, gS[bass.ds(b, 1), :, :].rearrange("o (c p) t -> p (o c) t", p=P)).then_inc(s_ot, 16)

            def guarded(b, last):
                for hg in range(HG):
                    g = base_of(b) + hg
                    sp.wait_ge(s_pv, BLOCKS * g + 4)
                    if last and hg == 2:
                        for qh in range(QH):
                            sp.wait_ge(s_od[qh], OPEN + 128 * (NG - 2))
                        load_sums(0, B - 1)
                    if last and hg == 3:
                        sp.wait_ge(s_inv, 1)
                        store_inverses(0, B - 1, 16)
                        load3(0)
                        sp.dma_start(sw1, a["L0_ffn_sw1"].rearrange("(c p) h -> p c h", p=P)).then_inc(s_sw, 16)
                        sp.dma_start(sw2, a["L0_ffn_sw2"].rearrange("(c p) e -> p c e", p=P)).then_inc(s_sw, 16)
                        sp.dma_start(sb2_row, a["L0_ffn_sb2"].unsqueeze(0).broadcast_to([P, E])).then_inc(s_sw, 16)
                        sp.dma_start(nw_row, a["L0_ffn_norm_weight"].unsqueeze(0).broadcast_to([P, E])).then_inc(s_sw, 16)
                    slot(b, hg, last)
            with sp.Fori(0, B - 1) as b:
                guarded(b, False)
            guarded(B - 1, True)
            def body3(b, last):
                if not last:
                    sp.wait_ge(s_wo, 4 * b + 4)
                    load3(b + 1)
                sp.wait_ge(s_n, b + 1)
                sp.dma_start(nS[bass.ds(b * T, T), :].rearrange("(t p) e -> p t e", p=P), H2).then_inc(s_nst, 16)
            body3(0, False)
            for qh in range(QH):
                sp.wait_ge(s_od[qh], OPEN + 128 * NG)
            load_sums(B - 1, B)
            sp.wait_ge(s_inv, 2)
            store_inverses(B - 1, B, 32)
            with sp.Fori(1, B - 1) as b:
                body3(b, False)
            body3(B - 1, True)
            def load_expert(e):
                for k, src in ((0, a["L0_ffn_ew1"][e].rearrange("(c p) h -> p c h", p=P)), (1, a["L0_ffn_ew2"][e].rearrange("(c p) o -> p c o", p=P))):
                    sp.dma_start(W[:, e, k, :].rearrange("p (c h) -> p c h", c=src.shape[1]), src).then_inc(s_wl, 16)

            sp.wait_ge(s_gt, B)
            sp.dma_start(region(5, 0, 256), a["c_eidx"]).then_inc(s_rc, 16)
            sp.dma_start(before, a["c_before"]).then_inc(s_rc, 16)
            sp.dma_start(tile_no, a["c_tile"]).then_inc(s_rc, 16)
            sp.dma_start(TK[:, :], a["c_token"]).then_inc(s_rc, 16)
            for e in range(4):
                load_expert(e)
            sp.wait_ge(s_zt, 1)
            sp.dma_start(tokS.rearrange("(i p) o -> i (p o)", p=P), zero_t[0:NTILE, :]).then_inc(s_z4, 16)
            sp.wait_ge(s_scat, 16 * 2 * NT)
            sp.dma_start(tokn[0:NTILE, :], tokS.rearrange("(i p) o -> i (p o)", p=P)).then_inc(s_tokl, 16)
            sp.wait_ge(s_xsb, B)
            sp.wait_ge(s_woev, 4 * B)
            sp.dma_start(eb2r.rearrange("p e o -> p (e o)"),
                         a["L0_ffn_eb2"].rearrange("e o -> (e o)").unsqueeze(0).broadcast_to([P, NE * E])).then_inc(s_eb2, 16)
            sp.wait_ge(s_tix, 1)
            sp.wait_ge(s_nst, 16 * B)
            load_expert(4)
            load_expert(5)
            sp.wait_ge(s_g2, OPEN + 4 * B)
            load_expert(6)
            load_expert(7)

            with sp.Fori(0, NTILE // 4) as it:
                for u in range(4):
                    sp.wait_ge(s_y, 4 * it + u + 1)
                    sp.dma_start(yS[bass.ds(it * (4 * P) + u * P, P), :], Yt[u % 2]).then_inc(s_yo[u % 2], 16)
            with sp.Fori(0, B) as b:
                sp.wait_ge(s_fin, TB * b + TB)
                sp.dma_start(out[bass.ds(b, 1), :, :].rearrange("o (t p) e -> p (o t) e", p=P),
                             X[:, bass.ds(b * TB, TB), :]).then_inc(s_out, 16)
            sp.wait_ge(s_out, 16 * B)

        @block.gpsimd
        def _(pool):
            g = nc.gpsimd
            for opened in (s_cosm, s_dec, s_qe):
                pool.nop().then_inc(opened, OPEN)
            chain = Chain(pool, s_pool, apart)
            g.memset(ones[:, :], 1.0).then_inc(s_ones, 1)
            pool.wait_ge(s_cst, 16 * build.n_cst)
            POOL_CH = 8
            with pool.Fori(0, B) as b:
                chain.start(b * POOL_CH)
                for c in range(4):
                    pool.wait_ge(s_qkev, 8 * b + 2 * c + 2)
                    if c:
                        pool.wait_ge(s_rr, OPEN + 4 * b + c)
                    g.tensor_tensor(rope_1[:, c % 2, :], qs[:, c, :], cosT, ALU.mult).then_inc(s_cosm, 1)
                    if c:
                        pool.wait_ge(s_p1, 4 * b + c)
                        g.tensor_tensor(rope_r[:, (c - 1) % 2, :], rope_r[:, (c - 1) % 2, :], pb[:, c - 1, 0, :], ALU.subtract).then_inc(s_r1, 1)
                pool.wait_ge(s_p1, 4 * b + 4)
                g.tensor_tensor(rope_r[:, 1, :], rope_r[:, 1, :], pb[:, 3, 0, :], ALU.subtract).then_inc(s_r1, 1)
                pool.wait_ge(s_ld, b + 1)
                pool.wait_ge(s_qeo, apart(pool, OPEN + 48 * b))
                chain.apart(g.tensor_scalar(qc, qrow, lt[:, 9:10], None, ALU.mult))
                chain(g.tensor_copy(qeb[:, 3, :], qc))
                chain.apart(g.tensor_tensor(qc, qc, qeb[:, 3, :], ALU.subtract))
                chain(g.tensor_copy(qeb[:, 4, :], qc))
                chain.apart(g.tensor_tensor(qeb[:, 5, :], qc, qeb[:, 4, :], ALU.subtract))
                for i in range(3):
                    chain.apart(g.tensor_copy(qeb[:, i, :], l3[:, i:i + 1].to_broadcast([H, T])))
                g.nop().then_inc(s_qe, 1)

            def pool_slot(b, hg):
                gr = base_of(b) + hg
                done = 0
                for s in range(STEPS):
                    qh, kt, hp = s // 16, s % 16 // 2, s % 2
                    if kt // 4 == qh:
                        if s == 0:
                            pool.wait_ge(s_dect, GH * (gr + 1))
                        pool.wait_ge(s_exp, STEPS * gr + s + 3)
                        j = kt % 4
                        blk = Pb[s % PRING][:, :, P * j:P * j + P]
                        g.tensor_tensor(blk, blk, Dec[hg % 2][:, 2 * hp:2 * hp + 2, :], ALU.mult).then_inc(s_dec, 1)
            with pool.Fori(0, B) as b:
                for hg in range(HG):
                    pool_slot(b, hg)

            def pool3(b):
                chain.start(POOL3 + 2 * b)
                bb = bass.ds(b, 1)
                if not isinstance(b, int):
                    pool.wait_ge(s_g2e, apart(pool, OPEN + 4 * b - 4))
                chain.apart(g.tensor_tensor(gabo, rows[:, 0, bb, :].rearrange("p o e -> p (o e)"), bo_row[:, :], ALU.mult))
                xb = X[:, bass.ds(b * TB, TB), :]
                g.tensor_tensor(xb, xb, gabo.unsqueeze(1).broadcast_to([P, TB, E]), ALU.add).then_inc(s_xbo, 1)
                pool.wait_ge(s_h2, b + 1)
                chain.apart(g.tensor_tensor(gbsb, rows[:, 3, bb, :].rearrange("p o e -> p (o e)"), sb2_row, ALU.mult))
                g.tensor_tensor(xb, xb, gbsb.unsqueeze(1).broadcast_to([P, TB, E]), ALU.add).then_inc(s_xsb, 1)
            POOL3 = B * POOL_CH
            pool.wait_ge(s_sw, 64)
            pool3(0)
            with pool.Fori(1, B) as b:
                pool3(b)

            pool.wait_ge(s_gt, B)
            g.memset(zero_t, 0).then_inc(s_zt, 1)
            pool.wait_ge(s_z4, 16)
            pool.wait_ge(s_rc, 64)
            pool.wait_ge(s_pos, 1)
            with pool.Fori(0, NT // 4) as it:
                g.tensor_copy(SC[:, 0:2, :], POSI[:, :, bass.ds(it * 4, 4)]).then_inc(s_sc4, 1)
                g.tensor_copy(SC[:, 2, :], TK[:, bass.ds(it * 4, 4)]).then_inc(s_sc4, 1)
                pool.wait_ge(s_sc4, apart(pool, 2 * it + 2))
                for u in range(4):
                    for k in range(2):
                        g.indirect_dma_start(out=tokS[:, :], out_offset=bass.IndirectOffsetOnAxis(ap=SC[:, k, u:u + 1].bitcast(U32), axis=0),
                                             in_=SC[:, 2, u:u + 1], in_offset=None).then_inc(s_scat, 16)
                pool.wait_ge(s_scat, 128 * it + 128)
            pool.wait_ge(s_tix, 1)
            pool.wait_ge(s_nst, 16 * B)
            pool.wait_ge(s_g2, OPEN + 4 * B)
            with pool.Fori(0, NTILE // 4) as it:
                pool.wait_ge(s_xtr, OPEN + 4 * it)
                g.tensor_copy(GI[:, :], TIX[:, bass.ds(it * 4, 4)]).then_inc(s_gi, 1)
                pool.wait_ge(s_gi, apart(pool, it + 1))
                for u in range(4):
                    if u >= 2:
                        pool.wait_ge(s_xtr, apart(pool, OPEN + 4 * it + u - 1))
                    g.indirect_dma_start(out=Xg[u % 2], out_offset=None, in_=nS[:, :],
                                         in_offset=bass.IndirectOffsetOnAxis(ap=GI[:, u:u + 1].bitcast(U32), axis=0)).then_inc(s_gx[u % 2], 16)
            for i in range(2):
                pool.wait_ge(s_yo[i], 16 * NTILE // 2)
            with pool.Fori(0, B) as b:
                pool.wait_ge(s_v1, OPEN + TB * b)
                g.tensor_copy(PC[:, :, :], POSI[:, :, bass.ds(b * TB, TB)]).then_inc(s_pc, 1)
                pool.wait_ge(s_pc, apart(pool, b + 1))
                for t in range(TB):
                    if t >= 4:
                        pool.wait_ge(s_v1, apart(pool, OPEN + TB * b + t - 3))
                    for k in range(2):
                        g.indirect_dma_start(out=Yg[t % 4][k], out_offset=None, in_=yS[:, :],
                                             in_offset=bass.IndirectOffsetOnAxis(ap=PC[:, k, t:t + 1].bitcast(U32), axis=0)).then_inc(s_yg[t % 4], 16)

        @block.scalar
        def _(act):
            s = nc.scalar
            for opened in (s_relu, s_hT):
                act.nop().then_inc(opened, OPEN)
            act.wait_ge(s_wev, 6)
            s.activation(cE, smallT[:, 48:56].rearrange("p (c b) -> p c b", c=KC), ACT.Exp, scale=-1.0).then_inc(s_ce, 1)
            act.wait_ge(s_var, 1)
            s.activation(tmpB[:, :], tmpA[:, :], ACT.Sqrt).then_inc(s_sq, 1)
            with act.Fori(0, B) as b:
                for half in range(2):
                    for fc in range(KC):
                        n = 2 * half + fc
                        act.wait_ge(s_tr, apart(act, OPEN + 4 * b + n + 1))
                        if n == 0:
                            act.wait_ge(s_proj, OPEN + 17 * b)
                            act.wait_ge(s_mean, apart(act, OPEN + b))
                            act.wait_ge(s_modc, 1)
                        s.activation(hT[:, fc, 512 * half:512 * half + 512], low[n][:, :], ACT.Identity,
                                     bias=modT[:, fc, bass.ds(b, 1)], scale=modT[:, 2 + fc, bass.ds(b, 1)],
                                     accum_out=hsum[:, 2 * fc + half:2 * fc + half + 1]).then_inc(s_hT, 1)
                def part1(c):
                    act.wait_ge(s_rr, OPEN + 4 * b + c + 1)
                    if c == 0:
                        act.wait_ge(s_pout, OPEN + 64 * b)
                    s.copy(pb[:, c, 0, :], rope_r[:, c % 2, :]).then_inc(s_p1, 1)

                def part2(c):
                    act.wait_ge(s_r1, 4 * b + c + 1)
                    s.copy(pb[:, c, 1, :], rope_r[:, c % 2, :]).then_inc(s_p2, 1)
                for j in range(8):
                    c, half = j // 2, j % 2
                    w, oc = c // 2, c % 2
                    act.wait_ge(s_proj, OPEN + 17 * b + j + 1)
                    if j == 0:
                        act.wait_ge(s_rr, OPEN + 4 * b)
                        act.wait_ge(s_cosm, OPEN + 4 * b)
                    s.activation(qs[:, c, 512 * half:512 * half + 512], hib[j % 4], ACT.Identity,
                                 bias=fcol[:, 2 * w + oc:2 * w + oc + 1], scale=0.25 if w == 0 else 1.0).then_inc(s_qkev, 1)
                    if j == 5:
                        part1(0)
                    if j == 7:
                        part2(0)
                        part1(1)
                for j in range(8, 12):
                    act.wait_ge(s_proj, OPEN + 17 * b + j + 1)
                    if j == 8:
                        act.wait_ge(s_gate, OPEN + 4 * b)
                    oc, half = (j - 8) // 2, j % 2
                    s.activation(ge[:, j - 8, :], hib[j % 4], ACT.Exp, bias=fcol[:, 6 + oc:7 + oc], scale=-1.0).then_inc(s_gexp, 1)
                part2(1)
                part1(2)
                part2(2)
                part1(3)
                part2(3)
                act.wait_ge(s_zb, OPEN + b + 1)
                s.activation(lt[:, 1:2], lt[:, 0:1], ACT.Exp, scale=-1.0).then_inc(s_e16, 1)
                act.wait_ge(s_pd, b + 1)
                s.activation(lt[:, 3:4], lt[:, 2:3], ACT.Exp, scale=-8.0 * LN2).then_inc(s_e16, 1)

            act.wait_ge(s_ldb, 16)
            act.wait_ge(s_pout, OPEN + 64 * B)
            act.wait_ge(s_qeo, OPEN + 48 * B)
            act.wait_ge(s_vout, OPEN + 16 * B)
            act.wait_ge(s_proj, OPEN + 17 * B)

            def out_copy(gr, qh):
                act.wait_ge(s_pv, BLOCKS * gr + 8 * qh + 8 + 4)
                act.wait_ge(s_od[qh], OPEN + 128 * gr)
                s.copy(Os[qh], out_ps[qh]).then_inc(s_oev, 1)

            def act_slot(b, hg):
                gr = base_of(b) + hg
                for i in range(GH):
                    hcol = b * H + (GH * hg + i)
                    s.activation(Dec[hg % 2][:, i, :], relu_t[:, :], ACT.Exp, scale=LDb[:, bass.ds(hcol, 1)]).then_inc(s_dect, 1)
                for st in range(STEPS):
                    act.wait_ge(s_s, STEPS * gr + st + 1)
                    act.wait_ge(s_pv, BLOCKS * gr + st // 2 + 1)
                    s.activation(Pb[st % PRING], score_ps[st % 2][:, :, :], ACT.Exp).then_inc(s_exp, 1)
                    if st == 19:
                        out_copy(gr, 0)
                out_copy(gr, 1)
            act.nop().then_inc(s_exp, 2)
            act.nop().then_inc(s_oev, 2)
            with act.Fori(0, B) as b:
                for hg in range(HG):
                    if hg < 2:
                        act.wait_ge(s_dec, apart(act, OPEN + 16 * base_of(b)))
                    else:
                        act.wait_ge(s_dec, apart(act, OPEN + 16 * (base_of(b) + hg - 1)))
                    act_slot(b, hg)

            def act_shared(b):
                for half in range(2):
                    for hc in range(HC):
                        n = HC * half + hc
                        act.wait_ge(s_g1, 16 * b + n + 1)
                        if hc == 0:
                            act.wait_ge(s_g2, OPEN + 4 * b + 2 * half)
                        s.activation(HT[:, hc, :], hib[n % 2], ACT.Relu, bias=sb1c[:, hc:hc + 1]).then_inc(s_relu, 1)

            def act3b(b):
                for n in range(4):
                    act.wait_ge(s_ntr, 4 * b + n + 1)
                    half, fc = n // 2, n % 2
                    s.copy(NTr[:, fc, 512 * half:512 * half + 512], low[n]).then_inc(s_nT, 1)
            act3b(0)
            with act.Fori(1, B) as b:
                act_shared(b - 1)
                act3b(b)
            act.wait_ge(s_lgc, B)
            act.wait_ge(s_wo, 4 * B)
            s.activation(PR.rearrange("p t e -> p (t e)"), LG[:, :, :].rearrange("p t e -> p (t e)"), ACT.Exp, scale=-1.0).then_inc(s_ex4, 1)
            act_shared(B - 1)

            def x_copy(i, it, u):
                act.wait_ge(s_xtr, OPEN + i + 1)
                if not (isinstance(i, int) and i < 2):
                    act.wait_ge(s_u2, 2 * i - 2)
                s.copy(XT[u % 2].rearrange("p c t -> p (c t)"), hib[2 + u % 2][:, 0:KC * P]).then_inc(s_xT, 1)

            def relu(i, u, e):
                act.wait_ge(s_htr, apart(act, i + 1))
                if not (isinstance(i, int) and i < 2):
                    act.wait_ge(s_d, apart(act, i - 1))
                for hc in range(HC):
                    s.activation(Ht[u % 2][:, hc, :], low[2 + hc // 4][:, P * (hc % 4):P * (hc % 4) + P], ACT.Relu,
                                 bias=smallT[:, bass.ds(e * HC + 56 + hc, 1)]).then_inc(s_hr, 1)

            def act5(it, first, last):
                for u in range(4):
                    i = 4 * it + u
                    e = act.value_load(ET[0:1, bass.ds(i, 1)], min_val=0, max_val=NE - 1)
                    if not last or u + 2 < 4:
                        x_copy(i + 2, it, u + 2)
                    relu(i, u, e)
            act.wait_ge(s_pos, 1)
            x_copy(0, 0, 0)
            x_copy(1, 0, 1)
            act5(0, True, False)
            with act.Fori(1, NTILE // 4 - 1) as it:
                act5(it, False, False)
            act5(NTILE // 4 - 1, False, True)

        @block.vector
        def _(dve):
            v = nc.vector
            for opened in (s_p3, s_gate, s_vev, s_rr, s_g2e, s_v1, s_mean, s_zb, s_g2m, s_mc):
                dve.nop().then_inc(opened, OPEN)
            chain = Chain(dve, s_dve)
            dve.wait_ge(s_cst, 16 * build.n_cst)
            for i in range(5):
                dve.wait_ge(s_wtr, i + 1)
                v.tensor_copy(wT[:, i, :, :].rearrange("p c e -> p (c e)"), (low + hib)[i]).then_inc(s_wev, 1)
            dve.wait_ge(s_wtr, 6)
            v.tensor_copy(smallT[:, :], hib[1][:, 0:56 + NE * HC]).then_inc(s_wev, 1)
            chain(v.tensor_scalar(fcol[:, 0:2], fcol[:, 0:2], 0.25, None, ALU.mult))
            chain(v.tensor_scalar(fcol[:, 6:8], fcol[:, 4:6], -1.0, None, ALU.mult))
            dve.wait_ge(s_ce, 1)
            chain(v.tensor_scalar(cE, cE, 1.0, None, ALU.add))
            chain(v.reciprocal(cE, cE))
            chain(v.tensor_tensor(scT, smallT[:, 48:56].rearrange("p (c b) -> p c b", c=KC), cE, ALU.mult))
            dve.wait_ge(s_ones, 1)
            for c in range(KC):
                for b in range(B):
                    v.tensor_scalar(scB[:, c, b, :], ones[:, :], scT[:, c, b:b + 1], None, ALU.mult).then_inc(s_sc, 1)
            dve.wait_ge(s_mod, 1)
            v.tensor_copy(modT[:, 0:2, :], hib[2][:, 0:8].rearrange("p (n b) -> p n b", n=2)).then_inc(s_dve, 1)
            chain.n += 1
            v.tensor_scalar(modT[:, 2:4, :], hib[2][:, 8:16].rearrange("p (n b) -> p n b", n=2), 1.0, None, ALU.add).then_inc(s_modc, 1)
            for n in range(8):
                b, half = n // 2, n % 2
                dve.wait_ge(s_mod, n + 2)
                v.tensor_copy(rows[:, 2 * half:2 * half + 2, b, :], low[n % 4].rearrange("p (k e) -> p k e", k=2)).then_inc(s_modc, 1)
            dve.wait_ge(s_modc, 9)
            chain(v.tensor_scalar(rows[:, 2, :, :], rows[:, 2, :, :], 1.0, None, ALU.add))
            for b in range(B):
                for k in (0, 3):
                    gr = rows[:, k, b, :]
                    chain(v.scalar_tensor_tensor(mag, gr, -1.0, gr, ALU.mult, ALU.max))
                    chain(v.tensor_scalar(sgn, gr, 0.0, 2.0, ALU.is_ge, ALU.mult))
                    chain(v.tensor_scalar(mag, mag, 0.25, None, ALU.max))
                    chain(v.scalar_tensor_tensor(gr, sgn, -1.0, mag, ALU.add, ALU.mult))
            for t in range(NT):
                if t % TB == 0:
                    dve.wait_ge(s_x[t // TB], 16)
                ins = v.bn_stats(st6[:, t, :], X[:, t, :])
            chain(ins)
            for t in range(NT):
                ins = v.bn_aggr(mv1[:, t, :], st6[:, t, :])
            chain(ins)
            v.tensor_scalar(tmpA[:, :], mv1[:, :, 1], 1e-5, None, ALU.add).then_inc(s_var, 1)
            dve.wait_ge(s_sq, 1)
            chain(v.reciprocal(rst1[:, :], tmpB[:, :]))
            chain(v.tensor_tensor(tmpB[:, :], rst1[:, :], rst1[:, :], ALU.mult))
            chain(v.tensor_tensor(tmpB[:, :], tmpB[:, :], tmpA[:, :], ALU.mult))
            chain(v.tensor_scalar(tmpB[:, :], tmpB[:, :], -0.5, 1.5, ALU.mult, ALU.add))
            chain(v.tensor_tensor(rst1[:, :], rst1[:, :], tmpB[:, :], ALU.mult))
            chain(v.memset(Vx[:, :, :, HD:32], 1.0))
            dve.wait_ge(s_mod, 9)
            base1 = chain.n
            PER1 = [None]

            def batch(b, per):
                chain.start(base1 + b * per)
                for t in range(TB):
                    tt = b * TB + t
                    if t == 0:
                        dve.wait_ge(s_tr, OPEN + 4 * b)
                    v.tensor_scalar(xh[:, t, :], X[:, bass.ds(tt, 1), :].rearrange("p o e -> p (o e)"),
                                    mv1[:, bass.ds(tt, 1), 0], rst1[:, bass.ds(tt, 1)],
                                    ALU.subtract, ALU.mult).then_inc(s_xh, 1)
                dve.wait_ge(s_hT, OPEN + 4 * b + 4)
                chain(v.tensor_tensor(mean2[:, :], hsum[:, 0:4:2], hsum[:, 1:4:2], ALU.add))
                v.tensor_scalar(mean2[:, :], mean2[:, :], 1.0 / T, None, ALU.mult).then_inc(s_mean, 1)

                def rest2(c):
                    dve.wait_ge(s_p2, 4 * b + c + 1)
                    v.tensor_tensor(pb[:, c, 2, :], rope_r[:, c % 2, :], pb[:, c, 1, :], ALU.subtract).then_inc(s_p3, 1)

                for c in range(4):
                    dve.wait_ge(s_qkev, apart(dve, 8 * b + 2 * c + 2))
                    chain(v.stream_shuffle(rope_s[:, c % 2, :], qs[:, c, :], [i ^ 1 for i in range(32)]))
                    chain(v.tensor_tensor(rope_s[:, c % 2, :], rope_s[:, c % 2, :], sinT, ALU.mult))
                    dve.wait_ge(s_cosm, OPEN + 4 * b + c + 1)
                    if c >= 2:
                        rest2(c - 2)
                        dve.wait_ge(s_p3, OPEN + 4 * b + c - 1)
                    else:
                        dve.wait_ge(s_p3, OPEN + 4 * b)
                    v.tensor_tensor(rope_r[:, c % 2, :], rope_1[:, c % 2, :], rope_s[:, c % 2, :], ALU.add).then_inc(s_rr, 1)
                for n in range(4):
                    dve.wait_ge(s_gexp, 4 * b + n + 1)
                    if n == 0:
                        dve.wait_ge(s_gout, OPEN + 32 * b)
                    v.tensor_scalar(gz[:, n, :], hib[n], fcol[:, 4 + n // 2:5 + n // 2], None, ALU.add).then_inc(s_gz, 1)
                    chain(v.tensor_scalar(ge[:, n, :], ge[:, n, :], 1.0, None, ALU.add))
                    chain(v.reciprocal(ge[:, n, :], ge[:, n, :]))
                    dve.wait_ge(s_gz, 4 * b + n + 1)
                    v.tensor_tensor(gz[:, n, :], gz[:, n, :], ge[:, n, :], ALU.mult).then_inc(s_gate, 1)
                for n in range(4):
                    dve.wait_ge(s_proj, OPEN + 17 * b + 12 + n + 1)
                    if n == 0:
                        dve.wait_ge(s_vout, OPEN + 16 * b)
                    for k in range(2):
                        ins = v.tensor_tensor(Vx[:, 2 * n + k, :, 0:HD], hib[n][:, E * k:E * k + E].rearrange("p (h d) -> p h d", h=H),
                                              bv_row[:, :].rearrange("p (h d) -> p h d", h=H), ALU.add)
                    ins.then_inc(s_vev, 1)
                dve.wait_ge(s_proj, OPEN + 17 * b + 17)
                dve.wait_ge(s_ldo, OPEN + 16 * b)
                dve.wait_ge(s_qe, OPEN + b)
                v.tensor_tensor(lt[:, 0:1], hib[0][0:H, 0:1], bd16[:, :], ALU.add).then_inc(s_zb, 1)
                dve.wait_ge(s_e16, 2 * b + 1)
                chain(v.tensor_scalar(lt[:, 4:5], lt[:, 1:2], 1.0, None, ALU.add))
                v.reciprocal(lt[:, 2:3], lt[:, 4:5]).then_inc(s_pd, 1)
                dve.wait_ge(s_e16, 2 * b + 2)
                chain(v.tensor_scalar(lt[:, 5:6], lt[:, 3:4], -2.0 ** -5, 1.0, ALU.mult, ALU.add))
                chain(v.tensor_scalar(lt[:, 6:7], lt[:, 5:6], -1.0, 1.0, ALU.mult, ALU.add))
                chain(v.tensor_scalar(lt[:, 7:8], lt[:, 6:7], 1.0 / 7, 1.0 / 6, ALU.mult, ALU.add))
                for k in (5, 4, 3, 2, 1):
                    chain(v.tensor_scalar(lt[:, 7:8], lt[:, 7:8], lt[:, 6:7], 1.0 / k, ALU.mult, ALU.add))
                chain(v.tensor_tensor(lt[:, 9:10], lt[:, 7:8], lt[:, 6:7], ALU.mult))
                chain(v.tensor_scalar(lt[:, 8:9], lt[:, 9:10], -1.0, None, ALU.mult))
                chain(v.tensor_copy(l3[:, 0:1], lt[:, 8:9]))
                chain(v.tensor_tensor(lt[:, 10:11], lt[:, 8:9], l3[:, 0:1], ALU.subtract))
                chain(v.tensor_copy(l3[:, 1:2], lt[:, 10:11]))
                v.tensor_tensor(l3[:, 2:3], lt[:, 10:11], l3[:, 1:2], ALU.subtract).then_inc(s_ld, 1)
                rest2(2)
                rest2(3)
                return chain.n
            per1 = 1 + 8 + 8 + 1 + 3 + 5 + 2 + 3
            with dve.Fori(0, B) as b:
                got = batch(b, per1)
                assert got == per1, got
            build.dve_stage1 = base1 + B * per1
            chain.start(build.dve_stage1)

            def take_max(gr, x):
                dve.wait_ge(s_mm, MSEQ * gr + x + 1)
                if x == 0:
                    dve.wait_ge(s_mc, OPEN + gr)
                v.tensor_reduce(mp[:, x:x + 1], max_ps[x % 2], AX.X, ALU.max).then_inc(s_mx, 1)

            def combine(gr):
                dve.wait_ge(s_mx, MSEQ * gr + NMAX + 2)
                v.tensor_reduce(mc[:, :], mp[:, :].rearrange("p (x k) -> p x k", k=2), AX.X, ALU.max).then_inc(s_mc, 1)
                dve.wait_ge(s_mm, MSEQ * (gr + 1))
                dve.wait_ge(s_mrow, OPEN + 16 * gr)
                v.tensor_scalar(mrow[:, :], max_ps[0][0:NMAX // 2, 0:P], -1.0, None, ALU.mult).then_inc(s_mx, 1)

            dve.nop().then_inc(s_mx, 2)
            for x in range(NMAX):
                take_max(0, x)
            combine(0)
            def dve_slot(b, hg, last):
                gr = base_of(b) + hg
                if not last or hg + 1 < HG:
                    for x in range(NMAX):
                        take_max(gr + 1, x)
                    combine(gr + 1)
            with dve.Fori(0, B - 1) as b:
                for hg in range(HG):
                    dve_slot(b, hg, False)
            for hg in range(HG):
                dve_slot(B - 1, hg, True)

            def invert(b0, b1, count):
                dve.wait_ge(s_sums, count)
                v.reciprocal(sums[:, b0:b1, :], sums[:, b0:b1, :]).then_inc(s_inv, 1)
            ch3 = Chain(dve, s_c3, apart)

            def rsqrt(r, w, x):
                ri, xi = r.bitcast(I32), x.bitcast(I32)
                ch3(v.tensor_scalar(ri, xi, 1, None, ALU.logical_shift_right))
                ch3(v.tensor_scalar(ri, ri, -1.0, float(0x5f3759df), ALU.mult, ALU.add))
                for _ in range(3):
                    ch3(v.scalar_tensor_tensor(w, r, -0.5, r, ALU.mult, ALU.mult))
                    ch3(v.tensor_tensor(w, w, x, ALU.mult))
                    ch3(v.scalar_tensor_tensor(r, w, 1.5, r, ALU.add, ALU.mult))

            def front_a(b):
                ch3.start(FRONT_A * b)
                dve.wait_ge(s_ot, 32 * b + 32)
                dve.wait_ge(s_rb, 256 * b + 256)
                ch3(v.tensor_tensor(OT, OT, RB, ALU.mult))
                for n in range(4):
                    ins = v.bn_stats(st3[:, n, :], OT[:, n // 2, 512 * (n % 2):512 * (n % 2) + 512])
                ch3.apart(ins)
                for c in range(KC):
                    ins = v.bn_aggr(mvf[:, c, :], st3[:, 2 * c:2 * c + 2, :].rearrange("p n s -> p (n s)"))
                ch3(ins)
                ch3(v.tensor_tensor(q3[:, 0, :], mvf[:, :, 0], mvf[:, :, 0], ALU.mult))
                v.tensor_tensor(mvf[:, :, 1], mvf[:, :, 1], q3[:, 0, :], ALU.add).then_inc(s_fst, 1)
                assert ch3.n == FRONT_A

            def front_b(b):
                ch3.sem = s_c3b
                ch3.start(FRONT_B * b)
                dve.wait_ge(s_gmm, b + 1)
                v.tensor_copy(gst[:, :, :].rearrange("p c k -> p (c k)"), hib[0][:, 0:4]).then_inc(s_gst, 1)
                dve.wait_ge(s_gst, b + 1)
                ch3(v.tensor_tensor(q3[:, 0, :], gst[:, :, 0], gst[:, :, 0], ALU.mult))
                ch3(v.tensor_tensor(q3[:, 1, :], gst[:, :, 1], q3[:, 0, :], ALU.subtract))
                ch3(v.tensor_scalar(q3[:, 1, :], q3[:, 1, :], 1e-5, None, ALU.add))
                rsqrt(q3[:, 3, :], q3[:, 4, :], q3[:, 1, :])
                ch3(v.tensor_tensor(q3[:, 3, :], q3[:, 3, :], fcol[:, 8:10], ALU.mult))
                ch3(v.tensor_tensor(q3[:, 4, :], q3[:, 3, :], gst[:, :, 0], ALU.mult))
                ch3(v.tensor_tensor(q3[:, 4, :], fcol[:, 10:12], q3[:, 4, :], ALU.subtract))
                for c in range(KC):
                    ins = v.tensor_scalar(OT[:, c, :], OT[:, c, :], q3[:, 3, c:c + 1], q3[:, 4, c:c + 1], ALU.mult, ALU.add)
                ch3(ins)
                v.tensor_tensor(GT2, OT, GT, ALU.mult).then_inc(s_gt, 1)
                assert ch3.n == FRONT_B
                ch3.sem = s_c3

            def tail(b):
                ch3.sem = s_c3c
                ch3.start(TAIL * b)
                dve.wait_ge(s_xbo, b + 1)
                for n in range(4):
                    dve.wait_ge(s_wo, 4 * b + n + 1)
                    u = U[:, n % 2, :].rearrange("p (t e) -> p t e", t=2)
                    v.tensor_tensor(u, low[n][:, :].rearrange("p (t e) -> p t e", t=2),
                                    rows[:, 0, bass.ds(b, 1), :].broadcast_to([P, 2, E]), ALU.mult).then_inc(s_woev, 1)
                    dve.wait_ge(s_woev, 4 * b + n + 1)
                    xx = X[:, bass.ds(b * TB + 2 * n, 2), :]
                    ins = v.tensor_tensor(xx, xx, u, ALU.add)
                    if n < 3:
                        ch3(ins)
                ch3.apart(ins)
                for t in range(TB):
                    ins = v.bn_stats(stx[:, t, :], X[:, bass.ds(b * TB + t, 1), :].rearrange("p o e -> p (o e)"))
                ch3.apart(ins)
                for t in range(TB):
                    ins = v.bn_aggr(mvx[:, t, :], stx[:, t, :])
                ch3(ins)
                ch3(v.tensor_scalar(q8[:, 0, :], mvx[:, :, 1], 1e-5, None, ALU.add))
                rsqrt(q8[:, 5, :], q8[:, 6, :], q8[:, 0, :])
                dve.wait_ge(s_nst, 16 * b)
                dve.wait_ge(s_ntr, 4 * b)
                cb, sbr = (rows[:, k, bass.ds(b, 1), :].rearrange("p o e -> p (o e)") for k in (2, 1))
                for t in range(TB):
                    ins = v.scalar_tensor_tensor(H2[:, t, :], X[:, bass.ds(b * TB + t, 1), :].rearrange("p o e -> p (o e)"),
                                                 mvx[:, t, 0:1], cb, ALU.subtract, ALU.mult)
                ins.then_inc(s_h2, 1)
                dve.wait_ge(s_h2, b + 1)
                for t in range(TB):
                    ins = v.scalar_tensor_tensor(H2[:, t, :], H2[:, t, :], q8[:, 5, t:t + 1], sbr, ALU.mult, ALU.add)
                ch3.apart(ins)
                for t in range(TB):
                    ins = v.bn_stats(stx[:, t, :], H2[:, t, :])
                ch3.apart(ins)
                for t in range(TB):
                    ins = v.bn_aggr(mvx[:, t, :], stx[:, t, :])
                ch3(ins)
                ch3(v.tensor_tensor(q8[:, 1, :], mvx[:, :, 0], mvx[:, :, 0], ALU.mult))
                ch3(v.tensor_tensor(q8[:, 1, :], q8[:, 1, :], mvx[:, :, 1], ALU.add))
                ch3(v.tensor_scalar(q8[:, 3, :], q8[:, 1, :], 1e-8, None, ALU.add))
                rsqrt(q8[:, 5, :], q8[:, 6, :], q8[:, 3, :])
                for t in range(TB):
                    ins = v.scalar_tensor_tensor(H2[:, t, :], H2[:, t, :], q8[:, 5, t:t + 1], nw_row, ALU.mult, ALU.mult)
                ins.then_inc(s_n, 1)
                assert ch3.n == TAIL
                ch3.sem = s_c3

            def dve_shared(b, n0, n1):
                dve.wait_ge(s_xsb, b + 1)
                for n in range(n0, n1):
                    dve.wait_ge(s_g2, OPEN + 4 * b + n + 1)
                    u = U[:, n % 2, :].rearrange("p (t e) -> p t e", t=2)
                    v.tensor_tensor(u, hib[2 + n % 2].rearrange("p (t e) -> p t e", t=2),
                                    rows[:, 3, bass.ds(b, 1), :].broadcast_to([P, 2, E]), ALU.mult).then_inc(s_g2m, 1)
                    dve.wait_ge(s_g2m, OPEN + 4 * b + n + 1)
                    xx = X[:, bass.ds(b * TB + 2 * n, 2), :]
                    v.tensor_tensor(xx, xx, u, ALU.add).then_inc(s_g2e, 1)

            def dve3b(b):
                dve.wait_ge(s_lg, b + 1)
                v.tensor_copy(LG[:, bass.ds(b * TB, TB), :].rearrange("p t e -> p (t e)"), hib[3][:, 0:TB * NE]).then_inc(s_lgc, 1)
            RSQRT = 2 + 3 * 3
            FRONT_A, FRONT_B, TAIL = 4, 3 + RSQRT + 3 + 1, 3 + 3 + 1 + RSQRT + 2 + 1 + 3 + RSQRT
            invert(0, B - 1, 16)
            front_a(0)
            front_b(0)
            dve.wait_ge(s_sw, 64)
            tail(0)
            invert(B - 1, B, 32)
            front_a(1)
            front_b(1)
            dve3b(0)
            with dve.Fori(1, B - 1) as b:
                tail(b)
                dve_shared(b - 1, 0, 2)
                front_a(b + 1)
                dve_shared(b - 1, 2, 4)
                front_b(b + 1)
                dve3b(b)
            tail(B - 1)
            dve_shared(B - 2, 0, 4)
            dve3b(B - 1)
            c5 = Chain(dve, s_c5)
            dve.wait_ge(s_rc, 64)
            dve.wait_ge(s_ex4, 1)
            flat = "p t e -> p (t e)"
            c5(v.tensor_scalar(PR.rearrange(flat), PR.rearrange(flat), 1.0, None, ALU.add))
            c5(v.reciprocal(PR.rearrange(flat), PR.rearrange(flat)))
            src = PR
            for k, OH in ((0, OH1), (1, OH2)):
                m, ix = m12[:, k, :], i12[:, k, :]
                c5(v.tensor_reduce(m, src, AX.X, ALU.max))
                c5(v.tensor_tensor(MK, src, m.unsqueeze(2).broadcast_to([P, NT, NE]), ALU.is_equal))
                c5(v.tensor_tensor(MK, MK, eidx, ALU.mult))
                c5(v.tensor_reduce(ix, MK, AX.X, ALU.min))
                c5(v.tensor_tensor(OH, eidx, ix.unsqueeze(2).broadcast_to([P, NT, NE]), ALU.is_equal))
                if k == 0:
                    c5(v.scalar_tensor_tensor(P2.rearrange(flat), OH.rearrange(flat), -2.0, PR.rearrange(flat), ALU.mult, ALU.add))
                    src = P2
            v.tensor_tensor(MM.rearrange(flat), OH1.rearrange(flat), OH2.rearrange(flat), ALU.add).then_inc(s_m4, 1)
            c5(v.tensor_tensor(sm, m12[:, 0, :], m12[:, 1, :], ALU.add))
            c5(v.tensor_scalar(sm, sm, 1e-6, None, ALU.add))
            c5(v.reciprocal(sm, sm))
            for k in range(2):
                c5(v.tensor_tensor(WG[:, k, :], m12[:, k, :], sm, ALU.mult))
            c5(v.memset(one32, 1.0))
            dve.wait_ge(s_pe4, 1)
            c5(v.tensor_copy(TOT.rearrange(flat), low[1][:, 0:NT * NE]))
            for e in range(NE):
                ins = v.tensor_tensor_scan(CUM[:, e, :], one32, TOT[:, :, e], 0.0, ALU.mult, ALU.add)
            c5(ins)
            c5(v.tensor_tensor(EXC, CUM.rearrange("p e t -> p t e"), TOT, ALU.subtract))
            c5(v.tensor_scalar(nti, CUM[:, :, NT - 1], 1.0 / P, (P - 1) / P - 0.5 + 0.5 / P, ALU.mult, ALU.add))
            c5(v.tensor_copy(ntf, nti))
            c5(v.tensor_tensor_scan(tinc, one32[:, 0:NE], ntf, 0.0, ALU.mult, ALU.add))
            c5(v.tensor_tensor(tslot, tinc, ntf, ALU.subtract))
            c5(v.tensor_scalar(tslot, tslot, float(P), None, ALU.mult))
            c5(v.tensor_tensor(EXC, EXC, tslot.unsqueeze(1).broadcast_to([P, NT, NE]), ALU.add))
            c5(v.tensor_tensor(POS.rearrange(flat), low[0][:, 0:NT * NE], EXC.rearrange(flat), ALU.add))
            for k, OH in ((0, OH1), (1, OH2)):
                c5(v.tensor_tensor(MK, OH, POS, ALU.mult))
                c5(v.tensor_reduce(pf[:, k, :], MK, AX.X, ALU.add))
            c5(v.tensor_copy(POSI, pf))
            c5(v.tensor_scalar(etf[:, 0:NTILE], tile_no, tinc[:, 0:1], None, ALU.is_ge))
            for e in range(1, NE - 1):
                c5(v.scalar_tensor_tensor(etf[:, 0:NTILE], tile_no, tinc[:, e:e + 1], etf[:, 0:NTILE], ALU.is_ge, ALU.add))
            v.tensor_copy(ET[:, 0:NTILE], etf[:, 0:NTILE]).then_inc(s_pos, 1)
            dve_shared(B - 1, 0, 4)
            dve.wait_ge(s_tokl, 16)
            v.tensor_copy(tokf[0:NTILE, :], tokn[0:NTILE, :]).then_inc(s_tokf, 1)
            dve.wait_ge(s_tokt, 1)
            v.tensor_copy(TIX, low[2][:, 0:NTILE]).then_inc(s_tix, 1)

            def hidden(i, u):
                for half in range(2):
                    dve.wait_ge(s_u2, 2 * i + half + 1)
                    if half == 0 and not (isinstance(i, int) and i < 2):
                        dve.wait_ge(s_htr, i - 1)
                    v.tensor_copy(Hn[u % 2][:, 512 * half:512 * half + 512], low[half]).then_inc(s_hn, 1)

            def result(i, it, u, e):
                dve.wait_ge(s_d, i + 1)
                if u >= 2:
                    dve.wait_ge(s_yo[u % 2], 32 * it + 16)
                else:
                    dve.wait_ge(s_yo[u % 2], 32 * it)
                v.tensor_tensor(Yt[u % 2], hib[u % 2][:, 0:E], eb2r[:, bass.ds(e, 1), :].rearrange("p o e -> p (o e)"), ALU.add).then_inc(s_y, 1)

            def dve5(it, last):
                for u in range(4):
                    i = 4 * it + u
                    e = dve.value_load(ET[0:1, bass.ds(i, 1)], min_val=0, max_val=NE - 1)
                    if not last or u + 1 < 4:
                        hidden(i + 1, u + 1)
                    result(i, it, u, e)
            dve.wait_ge(s_pos, 1)
            dve.wait_ge(s_eb2, 16)
            hidden(0, 0)
            dve5(0, False)
            with dve.Fori(1, NTILE // 4 - 1) as it:
                dve5(it, False)
            dve5(NTILE // 4 - 1, True)

            base6 = c5.n
            with dve.Fori(0, B) as b:
                c5.start(base6 + b * 2 * TB)
                for t in range(TB):
                    tt = b * TB + t
                    y0, y1, vv = Yg[t % 4][0], Yg[t % 4][1], Vg[t % 4]
                    dve.wait_ge(s_yg[t % 4], 64 * b + (64 if t >= 4 else 32))
                    c5(v.tensor_scalar(vv, y0, WG[:, 0, bass.ds(tt, 1)], None, ALU.mult))
                    ins = v.scalar_tensor_tensor(vv, y1, WG[:, 1, bass.ds(tt, 1)], vv, ALU.mult, ALU.add)
                    ins.then_inc(s_v1, 1)
                    dve.wait_ge(s_v1, OPEN + TB * b + t + 1)
                    c5(v.tensor_tensor(vv, vv, rows[:, 3, bass.ds(b, 1), :].rearrange("p o e -> p (o e)"), ALU.mult))
                    xx = X[:, bass.ds(tt, 1), :].rearrange("p o e -> p (o e)")
                    v.tensor_tensor(xx, xx, vv, ALU.add).then_inc(s_fin, 1)

        @block.tensor
        def _(pe):
            t = nc.tensor
            for opened in (s_g2, s_xtr, s_tr, s_proj):
                pe.nop().then_inc(opened, OPEN)
            pe.wait_ge(s_cst, 16 * build.n_cst)
            banks = low + hib
            for i in range(5):
                for ic in range(KC):
                    for oc in range(KC):
                        ins = t.transpose(banks[i][:, E * ic + P * oc:E * ic + P * oc + P], wn[:, i, oc, P * ic:P * ic + P], ident[:, :])
                ins.then_inc(s_wtr, 1)
            for src, n, col in ((wdn, H, 0), (rwn, NE, 32), (cn, B, 48)):
                for c in range(KC):
                    ins = t.transpose(hib[1][:, col + n * c:col + n * c + n], src[0:n, P * c:P * c + P], ident[0:n, 0:n])
            ins = t.transpose(hib[1][:, 56:56 + NE * HC], ebn[0:NE * HC, :], ident[0:NE * HC, 0:NE * HC])
            ins.then_inc(s_wtr, 1)
            pe.wait_ge(s_sc, 8)
            pe.wait_ge(s_wev, 6)
            for n in range(4):
                for c in range(KC):
                    ins = t.matmul(hib[2][:, 4 * n:4 * n + 4], wmod[:, c, P * n:P * n + P], scT[:, c, :], start=c == 0, stop=c == KC - 1)
            ins.then_inc(s_mod, 1)
            for n in range(8):
                b, half = n // 2, n % 2
                if n >= 4:
                    pe.wait_ge(s_modc, n - 4 + 2)
                for c in range(KC):
                    ins = t.matmul(low[n % 4], scB[:, c, b, :], wmod[:, c, 512 + 512 * half:1024 + 512 * half], start=c == 0, stop=c == KC - 1)
                ins.then_inc(s_mod, 1)
            pe.wait_ge(s_modc, 9)

            def project(b, j):
                dst = hib[j % 4]
                if j < 12:
                    w, oc, half = (0, 1, 3)[j // 4], j % 4 // 2, j % 2
                    for c in range(KC):
                        ins = t.matmul(dst, wT[:, w, c, P * oc:P * oc + P], hT[:, c, 512 * half:512 * half + 512], start=c == 0, stop=c == KC - 1)
                elif j < 16:
                    for k in range(2):
                        tt = 2 * (j - 12) + k
                        for c in range(KC):
                            ins = t.matmul(dst[:, E * k:E * k + E], hT[:, c, P * tt:P * tt + P], wT[:, 2, c, :], start=c == 0, stop=c == KC - 1)
                else:
                    for c in range(KC):
                        ins = t.matmul(dst[0:H, 0:1], smallT[:, H * c:H * c + H], mean2[:, c:c + 1], start=c == 0, stop=c == KC - 1)
                ins.then_inc(s_proj, 1)

            with pe.Fori(0, B) as b:
                for half in range(2):
                    for fc in range(KC):
                        n = 2 * half + fc
                        for k in range(4):
                            tt = 4 * half + k
                            pe.wait_ge(s_xh, TB * b + tt + 1)
                            if n == 0 and k == 0:
                                pe.wait_ge(s_hT, OPEN + 4 * b)
                            ins = t.transpose(low[n][:, P * k:P * k + P], xh[:, tt, P * fc:P * fc + P], ident[:, :])
                        ins.then_inc(s_tr, 1)
                for j in range(17):
                    if j == 0:
                        pe.wait_ge(s_hT, OPEN + 4 * b + 4)
                        pe.wait_ge(s_vev, OPEN + 4 * b)
                        pe.wait_ge(s_zb, OPEN + b)
                    elif 4 <= j < 12:
                        pe.wait_ge(s_qkev, 8 * b + j - 3)
                    elif 12 <= j < 16:
                        pe.wait_ge(s_gz, 4 * b + j - 11)
                    elif j == 16:
                        pe.wait_ge(s_vev, OPEN + 4 * b + 1)
                        pe.wait_ge(s_mean, OPEN + b + 1)
                    project(b, j)

            pe.wait_ge(s_hT, OPEN + 4 * B)
            pe.wait_ge(s_vev, OPEN + 4 * B)
            pe.wait_ge(s_zb, OPEN + B)
            pe.wait_ge(s_kx, 16 * 16)
            pe.nop().then_inc(s_pv, 4)

            def max_scores(gr, hg, x, uses):
                h, qt, kh = x // 16, x % 16 // 2, x % 2
                if x == 0:
                    pe.wait_ge(s_stk[hg], 16 * 13 * uses)
                    pe.wait_ge(s_mx, MSEQ * gr + 2)
                else:
                    pe.wait_ge(s_mx, MSEQ * gr + x + 1)
                t.matmul(max_ps[x % 2], stackQ[hg][0:ROWS_QK, h, P * qt:P * qt + P],
                         stackK[hg][0:ROWS_QK, h, 512 * kh:512 * kh + 512], start=True, stop=True).then_inc(s_mm, 1)

            def max_turn(gr):
                pe.wait_ge(s_mc, OPEN + gr + 1)
                t.transpose(max_ps[0][0:NMAX // 2, 0:P], mc[:, :], ident[:, :]).then_inc(s_mm, 1)

            def scores(gr, hg, st):
                qh, kt, hp = st // 16, st % 16 // 2, st % 2
                far = P * min(max(kt - 4 * qh, 0), 4)
                pe.wait_ge(s_exp, STEPS * gr + st + 1)
                for k in range(2):
                    h = 2 * hp + k
                    key = slice(P * kt, P * kt + P)
                    for c0, c1, rws in ((0, far, ROWS_FAR), (far, 512, ROWS_NEAR)):
                        if c1 > c0:
                            ins = t.matmul(score_ps[st % 2][:, k, c0:c1], stackK[hg][0:rws, h, key],
                                           stackQ[hg][0:rws, h, 512 * qh + c0:512 * qh + c1], start=True, stop=True)
                ins.then_inc(s_s, 1)

            def weigh(gr, hg, blk):
                qh, kt = blk // TB, blk % TB
                if kt == 0:
                    pe.wait_ge(s_oev, 2 * gr + qh + 1)
                if kt // 4 == qh:
                    pe.wait_ge(s_dec, OPEN + 16 * gr + (2 * kt + 2 if qh == 0 else 8 + 2 * (kt - 4) + 2))
                else:
                    pe.wait_ge(s_exp, STEPS * gr + 2 * blk + 4)
                for i in range(GH):
                    ins = t.matmul(out_ps[qh][32 * i:32 * i + 32, :], Vst[hg % 2][:, kt, 32 * i:32 * i + 32],
                                   Pb[(2 * blk + i // 2) % PRING][:, i % 2, :], start=kt == 0, stop=kt == TB - 1,
                                   tile_position=(0, 32 * i))
                ins.then_inc(s_pv, 1)

            def head_stats(b):
                pe.wait_ge(s_fst, b + 1)
                t.matmul(hib[0][:, 0:4], head_avg[:, :], mvf[:, :, :].rearrange("p c k -> p (c k)"), start=True, stop=True).then_inc(s_gmm, 1)

            def pe_slot(b, hg, last):
                gr = base_of(b) + hg
                nxt = not last or hg + 1 < HG
                nhg = (hg + 1) % HG
                uses = b + 1 if hg + 1 < HG else b + 2
                pe.wait_ge(s_mrow, OPEN + 16 * (gr + 1))
                pe.wait_ge(s_vld[hg % 2], 16 * (2 * b + hg // 2 + 1))
                done = [0]

                def max_here(place):
                    while nxt and done[0] < max_items(place):
                        max_scores(gr + 1, nhg, done[0], uses)
                        done[0] += 1
                for blk in range(BLOCKS):
                    max_here(4 * blk)
                    scores(gr, hg, 2 * blk)
                    max_here(4 * blk + 1)
                    if nxt and blk == BLOCKS - 1:
                        max_turn(gr + 1)
                    if not nxt and blk == BLOCKS - 4:
                        pe.wait_ge(s_mx, MSEQ * NG + 2)
                        head_stats(0)
                    scores(gr, hg, 2 * blk + 1)
                    max_here(4 * blk + 2)
                    max_here(4 * blk + 3)
                    if blk:
                        weigh(gr, hg, blk - 1)
                weigh(gr, hg, BLOCKS - 1)

            for x in range(NMAX):
                max_scores(0, 0, x, 1)
            max_turn(0)
            with pe.Fori(0, B - 1) as b:
                for hg in range(HG):
                    pe_slot(b, hg, False)
            for hg in range(HG):
                pe_slot(B - 1, hg, True)

            def pe3(b):
                pe.wait_ge(s_gt, b + 1)
                for n in range(4):
                    if n == 0:
                        pe.wait_ge(s_nT, 4 * b)
                    for k in range(2):
                        tt = 2 * n + k
                        for c in range(KC):
                            ins = t.matmul(low[n][:, E * k:E * k + E], OT[:, c, P * tt:P * tt + P], wT[:, 4, c, :], start=c == 0, stop=c == KC - 1)
                    ins.then_inc(s_wo, 1)

            def pe_shared(b):
                pe.wait_ge(s_sw, 64)
                pe.wait_ge(s_gst, b + 2 if not isinstance(b, int) else B)
                for half in range(2):
                    for hc in range(HC):
                        n = HC * half + hc
                        if n >= 2:
                            pe.wait_ge(s_relu, OPEN + 16 * b + n - 1)
                        else:
                            pe.wait_ge(s_relu, OPEN + 16 * b)
                        for c in range(KC):
                            ins = t.matmul(hib[n % 2], sw1[:, c, P * hc:P * hc + P], NTr[:, c, 512 * half:512 * half + 512], start=c == 0, stop=c == KC - 1)
                        ins.then_inc(s_g1, 1)
                    pe.wait_ge(s_relu, OPEN + 16 * b + 8 * half + 8)
                    for m in range(2):
                        n = 2 * half + m
                        if n == 0:
                            pe.wait_ge(s_g2m, OPEN + 4 * b)
                            pe.wait_ge(s_lgc, b + 1)
                        elif n >= 2:
                            pe.wait_ge(s_g2m, OPEN + 4 * b + n - 1)
                        for k in range(2):
                            for hc in range(HC):
                                ins = t.matmul(hib[2 + n % 2][:, E * k:E * k + E], HT[:, hc, P * (2 * m + k):P * (2 * m + k) + P], sw2[:, hc, :],
                                               start=hc == 0, stop=hc == HC - 1)
                        ins.then_inc(s_g2, 1)

            def pe3b(b):
                pe.wait_ge(s_n, b + 1)
                pe.wait_ge(s_woev, 4 * b + 4)
                for n in range(4):
                    half, fc = n // 2, n % 2
                    for k in range(4):
                        ins = t.transpose(low[n][:, P * k:P * k + P], H2[:, 4 * half + k, P * fc:P * fc + P], ident[:, :])
                    ins.then_inc(s_ntr, 1)
                pe.wait_ge(s_nT, 4 * b + 4)
                pe.wait_ge(s_g2m, OPEN + 4 * b)
                for tt in range(TB):
                    for c in range(KC):
                        ins = t.matmul(hib[3][:, NE * tt:NE * tt + NE], NTr[:, c, P * tt:P * tt + P], smallT[:, 32 + NE * c:32 + NE * c + NE],
                                       start=c == 0, stop=c == KC - 1)
                ins.then_inc(s_lg, 1)

            pe.wait_ge(s_oev, 2 * NG + 2)
            pe.wait_ge(s_exp, STEPS * NG + 2)
            pe3(0)
            pe3b(0)
            head_stats(1)
            with pe.Fori(1, B - 1) as b:
                pe3(b)
                pe_shared(b - 1)
                head_stats(b + 1)
                pe3b(b)
            pe3(B - 1)
            pe_shared(B - 2)
            pe3b(B - 1)
            pe.wait_ge(s_m4, 1)
            pe.wait_ge(s_nT, 4 * B)
            mm = MM.rearrange("p t e -> p (t e)")
            t.matmul(low[0][:, 0:NT * NE], before, mm, start=True, stop=True)
            t.matmul(low[1][:, 0:NT * NE], ones[:, :], mm, start=True, stop=True).then_inc(s_pe4, 1)
            pe_shared(B - 1)
            pe.wait_ge(s_tokf, 1)
            t.transpose(low[2][:, 0:NTILE], tokf[0:NTILE, :], ident[0:NTILE, 0:NTILE]).then_inc(s_tokt, 1)

            def x_turn(i, it, u):
                pe.wait_ge(s_gx[u % 2], 32 * it + (16 if u % 4 < 2 else 32))
                if not (isinstance(i, int) and i < 2):
                    pe.wait_ge(s_xT, i - 1)
                for c in range(KC):
                    ins = t.transpose(hib[2 + u % 2][:, P * c:P * c + P], Xg[u % 2][:, P * c:P * c + P], ident[:, :])
                ins.then_inc(s_xtr, 1)

            def up(i, u, e):
                pe.wait_ge(s_xT, i + 1)
                for half in range(2):
                    if isinstance(i, int) and i == 0:
                        pass
                    else:
                        pe.wait_ge(s_hn, 2 * i + half - 1)
                    for c in range(KC):
                        ins = t.matmul(low[half], XT[u % 2][:, c, :], W[:, bass.ds(e, 1), 0, 1024 * c + 512 * half:1024 * c + 512 * half + 512].rearrange("p o x -> p (o x)"),
                                       start=c == 0, stop=c == KC - 1)
                    ins.then_inc(s_u2, 1)

            def hidden_turn(i, u):
                if isinstance(i, int) and i == 0:
                    pass
                else:
                    pe.wait_ge(s_hr, HC * i)
                for hc in range(HC):
                    if hc % 4 == 0:
                        pe.wait_ge(s_hn, 2 * i + hc // 4 + 1)
                    ins = t.transpose(low[2 + hc // 4][:, P * (hc % 4):P * (hc % 4) + P], Hn[u % 2][:, P * hc:P * hc + P], ident[:, :])
                ins.then_inc(s_htr, 1)

            def down(i, u, e):
                if not (isinstance(i, int) and i < 2):
                    pe.wait_ge(s_y, i - 1)
                for hc in range(HC):
                    pe.wait_ge(s_hr, HC * i + hc + 1)
                    ins = t.matmul(hib[u % 2][:, 0:E], Ht[u % 2][:, hc, :], W[:, bass.ds(e, 1), 1, E * hc:E * hc + E].rearrange("p o x -> p (o x)"),
                                   start=hc == 0, stop=hc == HC - 1)
                ins.then_inc(s_d, 1)

            def expert_of(i):
                return pe.value_load(ET[0:1, bass.ds(i, 1)], min_val=0, max_val=NE - 1)

            def pe5(it, last):
                e = [expert_of(4 * it + u) for u in range(4 if last else 5)]
                for u in range(4):
                    i = 4 * it + u
                    if not last or u + 2 < 4:
                        x_turn(i + 2, it + (u + 2) // 4, (u + 2) % 4)
                    if not last or u + 1 < 4:
                        up(i + 1, u + 1, e[u + 1])
                    hidden_turn(i, u)
                    down(i, u, e[u])
            pe.wait_ge(s_pos, 1)
            pe.wait_ge(s_wl, 32 * NE)
            pe.wait_ge(s_g2e, OPEN + 4 * B)
            pe.wait_ge(s_tix, 1)
            x_turn(0, 0, 0)
            x_turn(1, 0, 1)
            up(0, 0, expert_of(0))
            pe5(0, False)
            with pe.Fori(1, NTILE // 4 - 1) as it:
                pe5(it, False)
            pe5(NTILE // 4 - 1, True)


def names():
    return ["L0_attn_x", "L0_attn_wq", "L0_attn_bq", "L0_attn_wk", "L0_attn_bk", "L0_attn_wv", "L0_attn_bv",
            "L0_attn_wg", "L0_attn_bg", "L0_attn_wo", "L0_attn_bo", "L0_attn_wd", "L0_attn_bd", "L0_attn_gamma",
            "L0_attn_beta", "L0_ffn_norm_weight", "L0_ffn_router_w", "L0_ffn_sw1", "L0_ffn_sb1", "L0_ffn_sw2",
            "L0_ffn_sb2", "L0_ffn_ew1", "L0_ffn_eb1", "L0_ffn_ew2", "L0_ffn_eb2", "L0_c", "L0_wmod"]

def kernel(**inputs):
    import concourse.bacc as bacc
    from concourse.bass_utils import run_bass_kernel_spmd

    nc = bacc.Bacc("TRN2", target_bir_lowering=False, num_devices=1)
    given = {name: np.ascontiguousarray(inputs[name]) for name in names()}
    given.update(constants())
    handles = {name: nc.dram_tensor(f"in_{name}_dram", x.shape, mybir.dt.from_np(x.dtype), kind="ExternalInput").ap()
               for name, x in given.items()}
    out = nc.dram_tensor("out_0_dram", (B, T, E), F32, kind="ExternalOutput").ap()
    build(nc, handles, out)
    done = run_bass_kernel_spmd(nc, [{f"in_{name}_dram": x for name, x in given.items()}], core_ids=[0])
    return done.results[0]["out_0_dram"]
```

```python
from contextlib import ExitStack

import numpy as np

import concourse.bass as bass
from concourse import mybir

F32 = mybir.dt.float32
BF16 = mybir.dt.bfloat16
I32 = mybir.dt.int32
U32 = mybir.dt.uint32
ALU = mybir.AluOpType
ACT = mybir.ActivationFunctionType
AX = mybir.AxisListType

P = 128
B, T, E = 4, 1024, 256
H = 16
HD = E // H
NT = B * T // P
TB = T // P
KC = E // P
NE = 8
HID = 1024
HC = HID // P
GH = 4
HG = H // GH
NG = B * HG
QH = T // 512
LN2 = float(np.log(2.0))

Q_PART = [0, 0, 1, 1, 0, 2]
K_PART = [0, 1, 0, 1, 2, 0]
ROWS_QK = 16 * len(Q_PART)
ROW_M = ROWS_QK
ROWS_NEAR = ROWS_QK + 1
N_EXT = 9
ROWS_FAR = ROWS_NEAR + N_EXT

STEPS = 2 * QH * TB
BLOCKS = STEPS // 2
NMAX = GH * TB * 2
MSEQ = NMAX + 1
PRING = 8
STATS_BLOCK, WO_BLOCK = 3, 6
TURN_BLOCK = BLOCKS - 2
PLACES = 4 * BLOCKS - 9
OPEN = 1
SLOTS = 2 * B * T + NE * P
NTILE = SLOTS // P


def constants():
    f = np.float32
    k = np.arange(T)
    inv = (1.0 / 10000.0 ** (np.arange(0, HD, 2, dtype=f) / f(HD))).astype(f)
    ang = np.arange(T, dtype=f)[:, None] * inv[None, :]
    ang = np.concatenate([ang, ang], axis=-1).astype(f)
    d = np.arange(P) % HD
    cos = np.cos(ang)[:, d].T.astype(f)
    sin = (np.sin(ang)[:, d] * np.where(d % 2 == 0, -1.0, 1.0)[None, :]).T.astype(f)
    ident = np.eye(P, dtype=f)
    relu = np.maximum(np.arange(P)[:, None] - np.arange(P)[None, :], 0).astype(f)
    before = (np.arange(P)[:, None] < np.arange(P)[None, :]).astype(f)
    same_head = (np.arange(P)[:, None] // HD == np.arange(P)[None, :] // HD).astype(f) / f(HD)
    hi, lo = (k // 8 * 8).astype(f), (k % 8).astype(f)
    one = np.ones(T, f)
    kext = (np.stack([one] + [hi] * 3 + [lo] * 3 + [one] * 3).view(np.uint32) >> 16).astype(np.uint16)
    qrow = (np.arange(P)[:, None] % TB * P + np.arange(P)[None, :]).astype(f)
    eidx = np.broadcast_to(np.tile(np.arange(NE) - NE, NT).astype(f), (P, NT * NE)).copy()
    tile = np.broadcast_to(np.arange(NTILE).astype(f), (P, NTILE)).copy()
    lane = np.broadcast_to(np.arange(P).astype(f), (P, P)).copy()
    place = np.broadcast_to((np.arange(2 * NT) + 1).astype(f), (P, 2 * NT)).copy()
    part = np.arange(P).astype(f)[:, None].copy()
    spare = (np.arange(NTILE)[None, :] * P + np.arange(P)[:, None] + P + 2 * B * T).astype(f)
    return {"c_cos": cos, "c_sin": np.ascontiguousarray(sin), "c_ident": ident, "c_relu": relu, "c_before": before,
            "c_head": same_head, "c_kext": kext, "c_qrow": qrow, "c_eight": (np.arange(P)[None, :] // TB == np.arange(H)[:, None]).astype(f), "c_lane": lane, "c_place": place, "c_part": part, "c_spare": spare, "c_eidx": eidx, "c_tile": tile}


ORDER = list(range(8)) + [16] + list(range(8, 16))
PROJECTED = {j: n + 1 for n, j in enumerate(ORDER)}


def max_items(place):
    return min(NMAX, -(-NMAX * (place + 1) // PLACES))


class Chain:

    def __init__(self, eng, sem, alone=None):
        self.eng, self.sem, self.n, self.base, self.alone = eng, sem, 0, 0, alone

    def start(self, base):
        self.base, self.n = base, 0

    def __call__(self, ins):
        self.n += 1
        ins.then_inc(self.sem, 1)
        self.eng.wait_ge(self.sem, self.base + self.n)

    def apart(self, ins):
        self.n += 1
        ins.then_inc(self.sem, 1)
        self.eng.wait_ge(self.sem, self.alone(self.eng, self.base + self.n))


def build(nc, a, out):
    ctx = ExitStack()
    with ctx:
        def sb(name, shape, dt=F32):
            return ctx.enter_context(nc.sbuf_tensor(name, shape, dt))

        def sem(name):
            return ctx.enter_context(nc.semaphore(name))

        def dram(name, shape, dt=F32):
            return nc.dram_tensor(name, shape, dt).ap()

        qkS = dram("qkS", [B, 2, 3, E, T], BF16)
        qeS = dram("qeS", [B, N_EXT, H, T], BF16)
        vS = dram("vS", [B, P, TB, H * 32])
        gS = dram("gS", [B, E, T])
        oS = dram("oS", [B, E, T])
        ldS = dram("ldS", [B, H, TB])
        sS = dram("sS", [B, H, T])
        rS = dram("rS", [B, H, T])
        nS = dram("nS", [B * T, E])
        yS = dram("yS", [2 * B * T + SLOTS, E])

        bank = [ctx.enter_context(nc.psum_tensor(f"bank{i}", [P, 512], F32)) for i in range(4, 8)]
        score_ps = [ctx.enter_context(nc.psum_tensor(f"score{i}", [P, 2, 512], F32)) for i in range(2)]
        low = [score_ps[0][:, 0, :], score_ps[0][:, 1, :], score_ps[1][:, 0, :], score_ps[1][:, 1, :]]
        hib = [t[:, :] for t in bank]
        max_ps = hib[0:3]
        out_ps = hib[3]
        first_max = low

        X = sb("X", [P, NT, E])
        W = sb("W", [P, NE, 2, 2048])
        ident = sb("ident", [P, P])
        ones = sb("ones", [P, P])
        relu_t = sb("relu_t", [P, P])
        head_avg = sb("head_avg", [P, P])
        wT = sb("wT", [P, 5, KC, E])
        rows = sb("rows", [P, 4, B, E])
        modT = sb("modT", [P, 4, B])
        smallT = sb("smallT", [P, 56 + NE * HC])
        fcol = sb("fcol", [P, 12])
        bv_row = sb("bv_row", [P, E])
        bo_row = sb("bo_row", [P, E])
        mv1 = sb("mv1", [P, NT, 2])
        rst1 = sb("rst1", [P, NT])
        st6 = sb("st6", [P, NT, 6])
        tmpA = sb("tmpA", [P, NT])
        tmpB = sb("tmpB", [P, NT])
        LDb = sb("LDb", [P, B * H])

        def region(e, k, n, dt=F32):
            ap = W[:, :, :, :].rearrange("p e w x -> p (e w x)")[:, e * 4096 + k:e * 4096 + k + n]
            return ap if dt == F32 else ap.bitcast(dt)

        stackQ = [region(4 + i, 0, 2048, BF16).rearrange("p (h t) -> p h t", h=GH) for i in range(4)]
        stackK = [region(4 + i, 2048, 2048, BF16).rearrange("p (h t) -> p h t", h=GH) for i in range(4)]

        wn = region(0, 0, 2560).rearrange("p (w c e) -> p w c e", w=5, c=KC)
        wmod = region(0, 2560, 3072).rearrange("p (c e) -> p c e", c=KC)
        scT = region(1, 1536, 8).rearrange("p (c b) -> p c b", c=KC)
        scB = region(1, 1544, 1024).rearrange("p (c b x) -> p c b x", c=KC, b=B)
        wdn = region(1, 2568, 256)
        rwn = region(1, 2824, 256)
        cn = region(1, 3080, 256)
        cE = region(1, 3336, 8).rearrange("p (c b) -> p c b", c=KC)
        ebn = region(1, 3864, P)
        csT = sb("csT", [P, 2, T])
        cosT, sinT = csT[:, 0, :], csT[:, 1, :]
        sw2 = csT[:, :, :].rearrange("p a (b e) -> p (a b) e", e=E)
        OT = region(4, 0, 2048).rearrange("p (c t) -> p c t", c=KC)
        GT = region(4, 2048, 2048).rearrange("p (c t) -> p c t", c=KC)
        RB = region(5, 0, 2048).rearrange("p (c t) -> p c t", c=KC)
        H2 = region(5, 2048, 2048).rearrange("p (t e) -> p t e", t=TB)
        NTr = region(6, 0, 2048).rearrange("p (c t) -> p c t", c=KC)
        sw1 = region(6, 2048, 2048).rearrange("p (c h) -> p c h", c=KC)
        HT = region(7, 0, 4096).rearrange("p (c t) -> p c t", c=HC)
        U = wT[:, 0:2, :, :].rearrange("p w c e -> p w (c e)")
        sums = wT[:, 2, :, :].rearrange("p c e -> p (c e)").rearrange("p (b x) -> p b x", b=B)
        misc = sb("misc", [P, 4, E])
        qrow = misc[:, 0, 0:P]
        eight = misc[0:H, 0, P:2 * P]
        wdr = misc[:, 1, :].rearrange("p (c h q) -> p c h q", c=KC, h=H)
        mag, sgn = wT[:, 3, 0, :], wT[:, 3, 1, :]
        gabo, gbsb, sb2_row, nw_row = (misc[:, i, :] for i in range(4))
        sb1c = sb("sb1c", [P, HC])
        st3 = sb("st3", [P, 4, 6])
        mvf = sb("mvf", [P, KC, 2])
        gst = sb("gst", [P, KC, 2])
        q3 = sb("q3", [P, 8, KC])
        stx = sb("stx", [P, TB, 6])
        mvx = sb("mvx", [P, TB, 2])
        q8 = sb("q8", [P, 8, TB])
        LG = sb("LG", [P, NT, NE])
        xh = region(2, 0, 2048).rearrange("p (t e) -> p t e", t=TB)
        hT = region(2, 2048, 2048).rearrange("p (c t) -> p c t", c=KC)
        qs = region(3, 0, 4096).rearrange("p (c t) -> p c t", c=4)
        gz = region(1, 0, 2048).rearrange("p (n t) -> p n t", n=4)
        Vx = region(5, 0, 4096).rearrange("p (t h c) -> p t h c", t=TB, h=H)
        pb = region(6, 0, 4096 + 2048, BF16).rearrange("p (c k t) -> p c k t", c=4, k=3)
        rope_s = region(0, 0, 2048).rearrange("p (k t) -> p k t", k=2)
        rope_1 = region(0, 2048, 2048).rearrange("p (k t) -> p k t", k=2)
        rope_r = region(7, 2048, 2048).rearrange("p (k t) -> p k t", k=2)
        qeb = region(1, 3200, 384, BF16).rearrange("p (r x) -> p r x", r=6)
        qc = region(1, 3072, P)
        hsum = sb("hsum", [P, 4])
        mean2 = sb("mean2", [P, 2])
        bd16 = sb("bd16", [H, 1])
        lt = sb("lt", [P, 16])
        l3 = sb("l3", [P, 3], BF16)
        Pb = [region(0, 1024 * i, 1024).rearrange("p (h t) -> p h t", h=2) for i in range(4)] + \
             [region(1, 1024 * i, 1024).rearrange("p (h t) -> p h t", h=2) for i in range(4)]
        Vst = [region(2, 1024 * i, 1024).rearrange("p (t c) -> p t c", t=TB) for i in range(2)]
        Dec = [region(2, 2048 + 512 * i, 512).rearrange("p (h t) -> p h t", h=GH) for i in range(2)]
        Os = [region(3, 512 * i, 512) for i in range(2)]
        mp = sb("mp", [P, NMAX])
        mc = sb("mc", [P, NMAX // 2])
        mrow = sb("mrow", [NMAX // 2, P], BF16)

        def route(i):
            return region(4, 256 * i, 256).rearrange("p (t e) -> p t e", e=NE)
        PR, MK, OH1, OH2, P2, MM, TOT, EXC, POS = (route(i) for i in range(9))
        CUM = region(4, 2304, 256).rearrange("p (e t) -> p e t", e=NE)
        one32 = region(4, 2560, 32)
        m12 = region(4, 2592, 64).rearrange("p (k t) -> p k t", k=2)
        i12 = region(4, 2656, 64).rearrange("p (k t) -> p k t", k=2)
        sm = region(4, 2720, 32)
        pf = region(4, 2752, 64).rearrange("p (k t) -> p k t", k=2)
        ntf = region(4, 2816, NE)
        nti = region(4, 2824, NE, I32)
        tinc = region(4, 2832, NE)
        tslot = region(4, 2840, NE)
        etf = region(4, 2848, 80)
        eidx = region(5, 0, 256).rearrange("p (t e) -> p t e", e=NE)
        before = region(5, 256, P)
        tile_no = region(5, 384, NTILE)
        lane = region(5, 1680, P)
        place = region(5, 1808, 2 * NT).rearrange("p (k t) -> p k t", k=2)
        part = region(5, 1872, 1)
        spare = region(4, 3640, NTILE)
        TC = 8
        one_a = [region(5, 2048 + 512 * i, 512, BF16).rearrange("p (j x) -> p j x", j=TC) for i in range(4)]
        one_b = [x.bitcast(BF16).rearrange("p (j v x) -> p j v x", j=TC, v=2) for x in
                 (region(5, 512, 576), region(5, 1088, 576), misc[:, :, :].rearrange("p k e -> p (k e)")[:, 0:576],
                  wT[:, 2:4, :, :].rearrange("p w c e -> p (w c e)")[:, 0:576])]
        QF, RF = (region(4, 2960 + 64 * i, 64).rearrange("p (k t) -> p k t", k=2) for i in range(2))
        POSI, QI, RI = (region(4, 3088 + 64 * i, 64, I32).rearrange("p (k t) -> p k t", k=2) for i in range(3))
        unused, dest, token = (region(4, 3280 + NTILE * i, NTILE) for i in range(3))
        sums4 = region(4, 3496, 2 * NTILE)
        st_words = st6[:, :, :].rearrange("p t s -> p (t s)")
        WG = mv1[:, :, :].rearrange("p t k -> p k t")
        ET = sb("ET", [P, 80], I32)
        TIX = st_words[:, 0:NTILE].bitcast(I32)
        DIX = st_words[:, NTILE:2 * NTILE].bitcast(I32)
        GI = sb("GI", [P, 4], I32)
        DI = sb("DI", [P, 4], I32)
        Hn = [wT[:, 0:2, :, :].rearrange("p w c e -> p (w c e)"), csT[:, 1, :]]
        Ht = [wT[:, 2:4, :, :].rearrange("p w c e -> p (w c e)"), csT[:, 0, :]]
        Ht = [h.rearrange("p (c t) -> p c t", c=HC) for h in Ht]
        Yt = [wT[:, 4, i, :] for i in range(2)]
        Xg = [misc[:, i, :] for i in range(2)]
        XT = [misc[:, 2 + i, :].rearrange("p (c t) -> p c t", c=KC) for i in range(2)]
        eb2r = rows[:, 0:2, :, :].rearrange("p k b e -> p (k b) e")
        Yb = [[region(b, 2048 * k, 2048).rearrange("p (t e) -> p t e", t=TB) for k in range(2)] for b in range(B)]

        s_x = [sem(f"x_loaded{b}") for b in range(B)]
        s_cst = sem("constants_loaded")
        s_w = sem("weights_loaded")
        s_wm = sem("modulation_weights_loaded")
        s_rowc = sem("modulation_rows_copied")
        s_ones = sem("ones_set")
        s_wtr = sem("weights_transposed")
        s_wev = sem("weights_copied")
        s_ce = sem("c_exp")
        s_sc = sem("c_silu")
        s_mod = sem("modulation_made")
        s_modc = sem("modulation_copied")
        s_dve = sem("dve_chain")
        s_pool = sem("pool_chain")
        s_xh = sem("x_normalised")
        s_tr = sem("h_transposed")
        s_hT = sem("h_copied")
        s_proj = sem("projection_made")
        s_qkev = sem("qk_copied")
        s_vev = sem("v_copied")
        s_gate = sem("gate_made")
        s_cosm = sem("rope_cos_part")
        s_rr = sem("roped")
        s_p1 = sem("part1")
        s_r1 = sem("rest1")
        s_p2 = sem("part2")
        s_p3 = sem("part3")
        s_pout = sem("parts_stored")
        s_gout = sem("gate_stored")
        s_vout = sem("v_stored")
        s_mean = sem("h_mean")
        s_zb = sem("decay_z")
        s_e16 = sem("decay_exp")
        s_pd = sem("decay_pd")
        s_ld = sem("log_decay")
        s_qe = sem("decay_rows")
        s_qeo = sem("decay_rows_stored")
        s_ldo = sem("log_decay_stored")
        s_ldb = sem("log_decay_loaded")
        s_kx = [sem(f"key_rows_loaded{i}") for i in range(4)]
        s_stk = [sem(f"stack_loaded{i}") for i in range(4)]
        s_vld = [sem(f"v_loaded{i}") for i in range(2)]
        s_mm = sem("max_scores")
        s_mx = sem("max_taken")
        s_mc = sem("max_combined")
        s_mrow = sem("max_row_placed")
        s_s = sem("scores_made")
        s_exp = sem("exp_done")
        s_dect = sem("decay_tables")
        s_dec = sem("decay_applied")
        s_pv = sem("pv_done")
        s_oev = sem("out_copied")
        s_od = [sem(f"out_stored{i}") for i in range(2)]

        s_sums = sem("sums_loaded")
        s_inv = sem("sums_inverted")
        s_ro = sem("inverses_stored")
        s_ot = sem("attention_out_loaded")
        s_rb = sem("inverses_loaded")
        s_sw = sem("shared_weights_loaded")
        s_fst = sem("feature_stats")
        s_gmm = sem("head_stats")
        s_gst = sem("head_stats_copied")
        s_gt = sem("gated")
        s_xbo = sem("x_plus_bias")
        s_wo = sem("wo_made")
        s_woev = sem("wo_copied")
        s_h2 = sem("h2_made")
        s_n = sem("n_made")
        s_nst = sem("n_stored")
        s_ntr = sem("n_transposed")
        s_nT = sem("n_copied")
        s_lg = sem("logits_made")
        s_lgc = sem("logits_copied")
        s_g1 = sem("shared_up")
        s_relu = sem("shared_relu")
        s_g2 = sem("shared_down")
        s_g2m = sem("shared_scaled")
        s_g2e = sem("shared_added")
        s_c3 = sem("front_a_chain")
        s_c3b = sem("front_b_chain")
        s_c3c = sem("tail_chain")
        s_xsb = sem("x_plus_shared_bias")
        s_rc = sem("routing_tables_loaded")
        s_wl = [sem(f"expert_weights_loaded{e}") for e in range(NE)]
        s_ready = sem("experts_ready")
        s_pe4 = sem("routing_counts")
        s_ex4 = sem("routing_exp")
        s_m4 = sem("choice_made")
        s_pos = sem("positions_ready")
        s_tix = sem("slot_tokens_ready")
        s_ob = sem("slot_marks")
        s_tm = sem("slot_table_parts")
        s_yl = [sem(f"results_loaded{b}") for b in range(B)]
        s_w0 = sem("first_choice_weighted")
        s_eb2 = sem("expert_bias_loaded")
        s_gi = sem("gather_index_staged")
        s_gx = [sem(f"tokens_gathered{i}") for i in range(2)]
        s_xtr = sem("x_tile_transposed")
        s_xT = sem("x_tile_copied")
        s_u2 = sem("expert_up_half")
        s_hn = sem("hidden_copied")
        s_htr = sem("hidden_transposed")
        s_hr = sem("hidden_relu")
        s_d = sem("expert_down")
        s_y = sem("y_copied")
        s_yo = [sem(f"y_stored{i}") for i in range(2)]
        s_fin = sem("x_final")
        s_finp = sem("x_final_by_pool")
        s_out = sem("x_stored")
        s_c5 = sem("dve_chain5")
        s_c4 = sem("rows_chain")
        s_rows = sem("rows_ready")
        s_c6 = sem("dve_chain6")

        block = ctx.enter_context(nc.Block())
        N_W, N_CST = 10, 15

        count_reg = {}

        def apart(eng, count):
            if not isinstance(count, int):
                if eng not in count_reg:
                    count_reg[eng] = eng.alloc_register(f"count{len(count_reg)}")
                eng.reg_add(count_reg[eng], count, 0)
                count = count_reg[eng]
            eng.wait_ge(s_ones, 1)
            return count

        def base_of(b):
            return b * HG

        @block.sync
        def _(sp):
            for opened in (s_ldo, s_pout, s_gout, s_vout, s_qeo, s_od[0], s_od[1], s_mrow):
                sp.nop().then_inc(opened, OPEN)
            def first(dst, src):
                sp.dma_start(dst, src).then_inc(s_w, 16)

            def cst(dst, src):
                sp.dma_start(dst, src, allow_slow_non_contiguous=True).then_inc(s_cst, 16)

            def load_x(b):
                sp.dma_start(X[:, TB * b:TB * b + TB, :], a["L0_attn_x"][b].rearrange("(t p) e -> p t e", p=P)).then_inc(s_x[b], 16)
            first(ident[:, :], a["c_ident"])
            first(cn[0:B, :], a["L0_c"])
            first(wdn[0:H, :], a["L0_attn_wd"])
            first(rwn[0:NE, :], a["L0_ffn_router_w"])
            first(ebn[0:NE * HC, :], a["L0_ffn_eb1"].rearrange("e (c p) -> (e c) p", p=P))
            for i, w in enumerate(("wq", "wk", "wv", "wg", "wo")):
                first(wn[:, i, :, :], a["L0_attn_" + w].rearrange("(c p) e -> p c e", p=P))
            load_x(0)
            sp.dma_start(wmod, a["L0_wmod"].rearrange("(c p) e -> p c e", p=P)).then_inc(s_wm, 16)
            load_x(1)
            for i, w in enumerate(("bq", "bk", "bg", "gamma", "beta")):
                col = (0, 2, 4, 8, 10)[i]
                cst(fcol[:, col:col + KC], a["L0_attn_" + w].rearrange("(c p) -> p c", p=P))
            cst(cosT, a["c_cos"])
            cst(sinT, a["c_sin"])
            cst(bv_row[:, :], a["L0_attn_bv"].unsqueeze(0).broadcast_to([P, E]))
            cst(bd16[:, :], a["L0_attn_bd"].unsqueeze(1))
            cst(eight, a["c_eight"])
            cst(qrow, a["c_qrow"])
            cst(bo_row[:, :], a["L0_attn_bo"].unsqueeze(0).broadcast_to([P, E]))
            cst(relu_t[:, :], a["c_relu"])
            cst(head_avg[:, :], a["c_head"])
            cst(sb1c[:, :], a["L0_ffn_sb1"].rearrange("(c p) -> p c", p=P))
            load_x(2)
            load_x(3)

            def store1(b):
                for c in range(4):
                    w, oc = c // 2, c % 2
                    sp.wait_ge(s_p3, OPEN + 4 * b + c + 1)
                    sp.dma_start(qkS[bass.ds(b, 1), w, :, P * oc:P * oc + P, :].rearrange("o k p t -> p (o k) t"),
                                 pb[:, c, :, :]).then_inc(s_pout, 16)
                sp.wait_ge(s_gate, OPEN + 4 * b + 4)
                for oc in range(KC):
                    sp.dma_start(gS[bass.ds(b, 1), P * oc:P * oc + P, :].rearrange("o p t -> p (o t)"),
                                 gz[:, 2 * oc:2 * oc + 2, :].rearrange("p n t -> p (n t)")).then_inc(s_gout, 16)
                sp.wait_ge(s_vev, OPEN + 4 * b + 4)
                sp.dma_start(vS[bass.ds(b, 1), :, :, :].rearrange("o p t c -> p (o t) c"),
                             Vx.rearrange("p t h c -> p t (h c)")).then_inc(s_vout, 16)
                sp.wait_ge(s_ld, b + 1)
                sp.dma_start(ldS[bass.ds(b, 1), :, :].rearrange("o h q -> (h q) o"), lt[:, 8:9]).then_inc(s_ldo, 16)
                sp.wait_ge(s_qe, OPEN + b + 1)
                for r0, r1, src in ((0, 3, 0), (3, 6, 0), (6, 9, 3)):
                    sp.dma_start(qeS[bass.ds(b, 1), r0:r1, :, :].rearrange("o r h (q x) -> (h q) (o r) x", x=P),
                                 qeb[:, src:src + 3, :]).then_inc(s_qeo, 16)

            def load_key_rows(i):
                for h in range(GH):
                    sp.dma_start(stackK[i][ROW_M:ROWS_FAR, h, :], a["c_kext"].bitcast(BF16)).then_inc(s_kx[i], 16)

            def load_stack(b, hg):
                for j in range(6):
                    for w, part, st in ((0, Q_PART[j], stackQ[hg]), (1, K_PART[j], stackK[hg])):
                        src = qkS[bass.ds(b, 1), w, part, 64 * hg:64 * hg + 64, :].rearrange("o (h d) t -> d (o h) t", d=HD)
                        sp.dma_start(st[16 * j:16 * j + 16, :, :], src).then_inc(s_stk[hg], 16)
                sp.dma_start(stackQ[hg][ROWS_NEAR:ROWS_FAR, :, :],
                             qeS[bass.ds(b, 1), :, GH * hg:GH * hg + GH, :].rearrange("o r h t -> r (o h) t")).then_inc(s_stk[hg], 16)

            with sp.Fori(0, B - 1) as b:
                store1(b)
            sp.wait_ge(s_pout, OPEN + 64 * (B - 1))
            sp.wait_ge(s_qeo, OPEN + 48 * (B - 1))
            load_key_rows(0)
            load_stack(0, 0)
            store1(B - 1)
            sp.wait_ge(s_ldo, OPEN + 16 * B)
            sp.dma_start(LDb[:, :], ldS.rearrange("b h q -> (b h) q")[:, 0:1].rearrange("x o -> o x").broadcast_to([P, B * H]), allow_slow_non_contiguous=True).then_inc(s_ldb, 16)
            sp.wait_ge(s_pout, OPEN + 64 * B)
            sp.wait_ge(s_gout, OPEN + 32 * B)
            sp.wait_ge(s_vout, OPEN + 16 * B)
            sp.wait_ge(s_qeo, OPEN + 48 * B)
            for i in range(1, 4):
                load_key_rows(i)

            def load_v(b, hg):
                sp.dma_start(Vst[hg % 2], vS[bass.ds(b, 1), :, :, P * hg:P * hg + P].rearrange("o p t c -> p (o t) c")).then_inc(s_vld[hg % 2], 16)

            def place_max(g):
                sp.wait_ge(s_mx, MSEQ * (g + 1) + 2)
                st = stackQ[place_max.hg]
                sp.dma_start(st[ROW_M:ROW_M + 1, :, :].rearrange("o h (q t) -> o (h q) t", t=P), mrow[:, :]).then_inc(s_mrow, 16)

            def store_out(b, hg, qh):
                g = base_of(b) + hg
                sp.wait_ge(s_oev, 2 * g + qh + 3)
                for i in range(GH):
                    f0 = (GH * hg + i) * HD
                    sp.dma_start(sS[bass.ds(b, 1), GH * hg + i, 512 * qh:512 * qh + 512],
                                 Os[qh][32 * i + HD:32 * i + HD + 1, :]).then_inc(s_od[qh], 16)
                    sp.dma_start(oS[bass.ds(b, 1), f0:f0 + HD, 512 * qh:512 * qh + 512].rearrange("o p t -> p (o t)"),
                                 Os[qh][32 * i:32 * i + HD, :]).then_inc(s_od[qh], 16)

            def slot(b, hg, last):
                g = base_of(b) + hg
                nxt = hg + 2
                if not last or nxt < HG:
                    if nxt >= 4:
                        load_stack(b + 1, nxt - 4)
                    else:
                        load_stack(b, nxt)
                if not last or hg + 1 < HG:
                    if hg + 1 == HG:
                        load_v(b + 1, 0)
                    else:
                        load_v(b, hg + 1)
                store_out(b, hg, 0)
                if last and hg == HG - 2:
                    sp.wait_ge(s_inv, 1)
                    store_inverses(0, B - 1, 16)
                    load3(0)
                if last and hg == HG - 1:
                    sp.wait_ge(s_wo, 4)
                    load3(1)
                if not last or hg + 1 < HG:
                    place_max.hg = (hg + 1) % HG
                    place_max(g + 1)
                store_out(b, hg, 1)

            load_v(0, 0)
            load_stack(0, 1)
            place_max.hg = 0
            place_max(0)

            def load_sums(b0, b1):
                sp.dma_start(sums[:, b0:b1, :], sS[b0:b1, :, :].rearrange("b h (q x) -> (h q) b x", x=P)).then_inc(s_sums, 16)

            def store_inverses(b0, b1, count):
                sp.dma_start(rS[b0:b1, :, :].rearrange("b h (q x) -> (h q) b x", x=P), sums[:, b0:b1, :]).then_inc(s_ro, 16)
                sp.wait_ge(s_ro, count)

            def load3(b):
                sp.dma_start(OT, oS[bass.ds(b, 1), :, :].rearrange("o (c p) t -> p (o c) t", p=P)).then_inc(s_ot, 16)
                for h in range(H):
                    sp.dma_start(RB[HD * (h % 8):HD * (h % 8) + HD, h // 8, :],
                                 rS[bass.ds(b, 1), h, :].broadcast_to([HD, T])).then_inc(s_rb, 16)
                sp.dma_start(GT, gS[bass.ds(b, 1), :, :].rearrange("o (c p) t -> p (o c) t", p=P)).then_inc(s_ot, 16)

            def guarded(b, last):
                for hg in range(HG):
                    g = base_of(b) + hg
                    sp.wait_ge(s_pv, BLOCKS * g + 4)
                    if last and hg == 2:
                        for qh in range(QH):
                            sp.wait_ge(s_od[qh], OPEN + 128 * (NG - 2))
                        load_sums(0, B - 1)
                    if last and hg == 3:
                        sp.dma_start(sw1, a["L0_ffn_sw1"].rearrange("(c p) h -> p c h", p=P)).then_inc(s_sw, 16)
                        sp.dma_start(sw2, a["L0_ffn_sw2"].rearrange("(c p) e -> p c e", p=P)).then_inc(s_sw, 16)
                        sp.dma_start(sb2_row, a["L0_ffn_sb2"].unsqueeze(0).broadcast_to([P, E])).then_inc(s_sw, 16)
                        sp.dma_start(nw_row, a["L0_ffn_norm_weight"].unsqueeze(0).broadcast_to([P, E])).then_inc(s_sw, 16)
                    slot(b, hg, last)
            with sp.Fori(0, B - 1) as b:
                guarded(b, False)
            guarded(B - 1, True)
            def body3(b, last):
                if not last and not isinstance(b, int):
                    sp.wait_ge(s_wo, 4 * b + 4)
                    load3(b + 1)
                sp.wait_ge(s_n, b + 1)
                sp.dma_start(nS[bass.ds(b * T, T), :].rearrange("(t p) e -> p t e", p=P), H2).then_inc(s_nst, 16)
            body3(0, False)
            for qh in range(QH):
                sp.wait_ge(s_od[qh], OPEN + 128 * NG)
            load_sums(B - 1, B)
            sp.wait_ge(s_inv, 2)
            store_inverses(B - 1, B, 32)
            with sp.Fori(1, B - 1) as b:
                body3(b, False)
            body3(B - 1, True)
            def load_expert(e):
                for k, src in ((0, a["L0_ffn_ew1"][e].rearrange("(c p) h -> p c h", p=P)), (1, a["L0_ffn_ew2"][e].rearrange("(c p) o -> p c o", p=P))):
                    sp.dma_start(W[:, e, k, :].rearrange("p (c h) -> p c h", c=src.shape[1]), src).then_inc(s_wl[e], 16)

            sp.wait_ge(s_gt, B)
            sp.dma_start(region(5, 0, 256), a["c_eidx"]).then_inc(s_rc, 16)
            sp.dma_start(before, a["c_before"]).then_inc(s_rc, 16)
            sp.dma_start(tile_no, a["c_tile"]).then_inc(s_rc, 16)
            sp.dma_start(lane, a["c_lane"]).then_inc(s_rc, 16)
            sp.dma_start(place.rearrange("p k t -> p (k t)"), a["c_place"]).then_inc(s_rc, 16)
            sp.dma_start(part, a["c_part"]).then_inc(s_rc, 16)
            sp.dma_start(spare, a["c_spare"]).then_inc(s_rc, 16)
            for e in range(4):
                load_expert(e)
            sp.wait_ge(s_xsb, B)
            sp.wait_ge(s_woev, 4 * B)
            sp.dma_start(eb2r.rearrange("p e o -> p (e o)"),
                         a["L0_ffn_eb2"].rearrange("e o -> (e o)").unsqueeze(0).broadcast_to([P, NE * E])).then_inc(s_eb2, 16)
            sp.wait_ge(s_tix, 1)
            sp.wait_ge(s_nst, 16 * B)
            load_expert(4)
            load_expert(5)
            sp.wait_ge(s_g2, OPEN + 4 * B)
            load_expert(6)
            load_expert(7)

            for i in range(2):
                sp.wait_ge(s_yo[i], 16 * NTILE // 2)

            for b in range(B):
                for k in range(2):
                    sp.dma_start(Yb[b][k], yS[(k * B + b) * T:(k * B + b) * T + T, :].rearrange("(t p) e -> p t e", p=P)).then_inc(s_yl[b], 16)
            for b in range(B):
                if b < B - 1:
                    sp.wait_ge(s_finp, b + 1)
                else:
                    sp.wait_ge(s_fin, 1)
                sp.dma_start(out[b].rearrange("(t p) e -> p t e", p=P), X[:, TB * b:TB * b + TB, :]).then_inc(s_out, 16)
            sp.wait_ge(s_out, 16 * B)

        @block.gpsimd
        def _(pool):
            g = nc.gpsimd
            for opened in (s_cosm, s_dec, s_qe):
                pool.nop().then_inc(opened, OPEN)
            chain = Chain(pool, s_pool, apart)
            g.memset(ones[:, :], 1.0).then_inc(s_ones, 1)
            pool.wait_ge(s_cst, 16 * N_CST)
            POOL_CH = 6
            with pool.Fori(0, B) as b:
                chain.start(b * POOL_CH)
                for c in range(4):
                    pool.wait_ge(s_qkev, 8 * b + 2 * c + 2)
                    if c:
                        pool.wait_ge(s_rr, OPEN + 4 * b + c)
                    g.tensor_tensor(rope_1[:, c % 2, :], qs[:, c, :], cosT, ALU.mult).then_inc(s_cosm, 1)
                    if c:
                        pool.wait_ge(s_p1, 4 * b + c)
                        g.tensor_tensor(rope_r[:, (c - 1) % 2, :], rope_r[:, (c - 1) % 2, :], pb[:, c - 1, 0, :], ALU.subtract).then_inc(s_r1, 1)
                pool.wait_ge(s_p1, 4 * b + 4)
                g.tensor_tensor(rope_r[:, 1, :], rope_r[:, 1, :], pb[:, 3, 0, :], ALU.subtract).then_inc(s_r1, 1)
                pool.wait_ge(s_ld, b + 1)
                pool.wait_ge(s_qeo, apart(pool, OPEN + 48 * b))
                chain.apart(g.tensor_scalar(qc, qrow, lt[:, 9:10], None, ALU.mult))
                chain(g.tensor_copy(qeb[:, 3, :], qc))
                chain.apart(g.tensor_tensor(qc, qc, qeb[:, 3, :], ALU.subtract))
                chain(g.tensor_copy(qeb[:, 4, :], qc))
                chain.apart(g.tensor_tensor(qeb[:, 5, :], qc, qeb[:, 4, :], ALU.subtract))
                chain(g.tensor_copy(qeb[:, 0:3, :], l3[:, :].unsqueeze(2).broadcast_to([P, 3, P])))
                g.nop().then_inc(s_qe, 1)

            POOL3 = B * POOL_CH

            def output_bias(b):
                chain.start(POOL3 + 2 * b)
                bb = bass.ds(b, 1)
                chain.apart(g.tensor_tensor(gabo, rows[:, 0, bb, :].rearrange("p o e -> p (o e)"), bo_row[:, :], ALU.mult))
                xb = X[:, bass.ds(b * TB, TB), :]
                g.tensor_tensor(xb, xb, gabo.unsqueeze(1).broadcast_to([P, TB, E]), ALU.add).then_inc(s_xbo, 1)

            def shared_bias(b):
                chain.start(POOL3 + 2 * b + 1)
                bb = bass.ds(b, 1)
                pool.wait_ge(s_h2, apart(pool, b + 1))
                chain.apart(g.tensor_tensor(gbsb, rows[:, 3, bb, :].rearrange("p o e -> p (o e)"), sb2_row, ALU.mult))
                xb = X[:, bass.ds(b * TB, TB), :]
                g.tensor_tensor(xb, xb, gbsb.unsqueeze(1).broadcast_to([P, TB, E]), ALU.add).then_inc(s_xsb, 1)

            def pool_slot(b, hg, last=False):
                gr = base_of(b) + hg
                for s in range(STEPS):
                    qh, kt, hp = s // 16, s % 16 // 2, s % 2
                    if last and s == STEPS // 2:
                        pool.wait_ge(s_rows, 1)
                        output_bias(0)
                    if kt // 4 == qh:
                        if s == 0:
                            pool.wait_ge(s_dect, GH * (gr + 1))
                        pool.wait_ge(s_exp, STEPS * gr + s + 3)
                        j = kt % 4
                        blk = Pb[s % PRING][:, :, P * j:P * j + P]
                        g.tensor_tensor(blk, blk, Dec[hg % 2][:, 2 * hp:2 * hp + 2, :], ALU.mult).then_inc(s_dec, 1)
            with pool.Fori(0, B - 1) as b:
                for hg in range(HG):
                    pool_slot(b, hg)
            for hg in range(HG):
                pool_slot(B - 1, hg, hg == HG - 1)

            pool.wait_ge(s_sw, 64)
            pool.wait_ge(s_rows, 2)
            shared_bias(0)
            with pool.Fori(1, B) as b:
                output_bias(b)
                shared_bias(b)

            def stage_indices(dst, src, tile, count):
                g.tensor_copy(dst[:, :], src[:, bass.ds(tile, 4)]).then_inc(s_gi, 1)
                pool.wait_ge(s_gi, apart(pool, count) if not isinstance(count, int) else count)

            def gather(u):
                g.indirect_dma_start(out=Xg[u % 2], out_offset=None, in_=nS[:, :],
                                     in_offset=bass.IndirectOffsetOnAxis(ap=GI[:, u:u + 1].bitcast(U32), axis=0)).then_inc(s_gx[u % 2], 16)

            def scatter(u):
                g.indirect_dma_start(out=yS[:, :], out_offset=bass.IndirectOffsetOnAxis(ap=DI[:, u:u + 1].bitcast(U32), axis=0),
                                     in_=Yt[u % 2], in_offset=None).then_inc(s_yo[u % 2], 16)

            def relay(e):
                pool.wait_ge(s_wl[e], 32)
                pool.nop().then_inc(s_ready, 1)
            for e in range(4):
                relay(e)
            pool.wait_ge(s_tix, 1)
            stage_indices(GI, TIX, 0, 1)
            for u in range(4):
                if u >= 2:
                    pool.wait_ge(s_xtr, OPEN + u - 1)
                gather(u)
            for e in range(4, NE):
                relay(e)

            def pool5(it, last):
                pool.wait_ge(s_xtr, OPEN + 4 * it + 4)
                if not last:
                    stage_indices(GI, TIX, 4 * it + 4, 2 * it + 2)
                    stage_indices(DI, DIX, 4 * it, 2 * it + 3)
                else:
                    stage_indices(DI, DIX, 4 * it, 2 * it + 2)
                for u in range(4):
                    if not last:
                        if u >= 2:
                            pool.wait_ge(s_xtr, apart(pool, OPEN + 4 * it + 3 + u))
                        gather(u)
                    pool.wait_ge(s_y, apart(pool, 4 * it + u + 1))
                    scatter(u)
                for i in range(2):
                    pool.wait_ge(s_yo[i], 32 * it + 32)
            with pool.Fori(0, NTILE // 4 - 1) as it:
                pool5(it, False)
            pool5(NTILE // 4 - 1, True)

            for b in range(B - 1):
                pool.wait_ge(s_c6, 2 * b + 2)
                xb = X[:, TB * b:TB * b + TB, :]
                g.tensor_tensor(xb, xb, Yb[b][1], ALU.add).then_inc(s_finp, 1)

        @block.scalar
        def _(act):
            s = nc.scalar
            for opened in (s_relu, s_hT, s_gate):
                act.nop().then_inc(opened, OPEN)
            act.wait_ge(s_wev, 6)
            s.activation(cE, smallT[:, 48:56].rearrange("p (c b) -> p c b", c=KC), ACT.Exp, scale=-1.0).then_inc(s_ce, 1)
            for n in range(8):
                b, half = n // 2, n % 2
                act.wait_ge(s_mod, n + 2)
                s.copy(rows[:, 2 * half:2 * half + 2, b, :], low[n % 4].rearrange("p (k e) -> p k e", k=2)).then_inc(s_rowc, 1)
            act.wait_ge(s_cst, 16 * N_CST)
            def h_by_feature(b):
                for half in range(2):
                    for fc in range(KC):
                        n = 2 * half + fc
                        act.wait_ge(s_tr, apart(act, OPEN + 4 * b + n + 1))
                        if n == 0:
                            act.wait_ge(s_proj, OPEN + 17 * b)
                            act.wait_ge(s_mean, apart(act, OPEN + b))
                            act.wait_ge(s_modc, 1)
                        s.activation(hT[:, fc, 512 * half:512 * half + 512], low[n][:, :], ACT.Identity,
                                     bias=modT[:, fc, bass.ds(b, 1)], scale=modT[:, 2 + fc, bass.ds(b, 1)],
                                     accum_out=hsum[:, 2 * fc + half:2 * fc + half + 1]).then_inc(s_hT, 1)
            def act1(b, last):
                def part1(c):
                    act.wait_ge(s_rr, OPEN + 4 * b + c + 1)
                    if c == 0:
                        act.wait_ge(s_pout, OPEN + 64 * b)
                    s.copy(pb[:, c, 0, :], rope_r[:, c % 2, :]).then_inc(s_p1, 1)

                def part2(c):
                    act.wait_ge(s_r1, 4 * b + c + 1)
                    s.copy(pb[:, c, 1, :], rope_r[:, c % 2, :]).then_inc(s_p2, 1)
                for j in range(8):
                    c, half = j // 2, j % 2
                    w, oc = c // 2, c % 2
                    act.wait_ge(s_proj, OPEN + 17 * b + PROJECTED[j])
                    if j == 0:
                        act.wait_ge(s_rr, OPEN + 4 * b)
                        act.wait_ge(s_cosm, OPEN + 4 * b)
                    s.activation(qs[:, c, 512 * half:512 * half + 512], hib[j % 4], ACT.Identity,
                                 bias=fcol[:, 2 * w + oc:2 * w + oc + 1], scale=0.25 if w == 0 else 1.0).then_inc(s_qkev, 1)
                    if j == 5:
                        part1(0)
                    if j == 7:
                        part2(0)
                        part1(1)
                        act.wait_ge(s_zb, OPEN + b + 1)
                        s.activation(lt[:, 1:2], lt[:, 0:1], ACT.Exp, scale=-1.0).then_inc(s_e16, 1)
                for j in range(8, 12):
                    act.wait_ge(s_proj, OPEN + 17 * b + PROJECTED[j])
                    if j == 8:
                        act.wait_ge(s_gout, OPEN + 32 * b)
                    oc = (j - 8) // 2
                    s.activation(gz[:, j - 8, :], hib[j % 4], ACT.Silu, bias=fcol[:, 4 + oc:5 + oc]).then_inc(s_gate, 1)
                part2(1)
                part1(2)
                act.wait_ge(s_pd, b + 1)
                s.activation(lt[:, 3:4], lt[:, 2:3], ACT.Exp, scale=-8.0 * LN2).then_inc(s_e16, 1)
                if not last:
                    h_by_feature(b + 1)
                part2(2)
                part1(3)
                part2(3)

            h_by_feature(0)
            with act.Fori(0, B - 1) as b:
                act1(b, False)
            act1(B - 1, True)

            act.wait_ge(s_ldb, 16)
            act.wait_ge(s_pout, OPEN + 64 * B)
            act.wait_ge(s_qeo, OPEN + 48 * B)
            act.wait_ge(s_vout, OPEN + 16 * B)
            act.wait_ge(s_proj, OPEN + 17 * B)

            def out_copy(gr, qh):
                act.wait_ge(s_pv, BLOCKS * gr + 8 * qh + 8 + 4)
                act.wait_ge(s_od[qh], OPEN + 128 * gr)
                s.copy(Os[qh], out_ps).then_inc(s_oev, 1)

            def decay_tables(gr, hg, b):
                for i in range(GH):
                    s.activation(Dec[hg % 2][:, i, :], relu_t[:, :], ACT.Exp, scale=LDb[:, bass.ds(b * H + GH * hg + i, 1)]).then_inc(s_dect, 1)

            def act_slot(b, hg, first, last):
                gr = base_of(b) + hg
                for st in range(STEPS):
                    act.wait_ge(s_s, STEPS * gr + st + 1)
                    act.wait_ge(s_pv, BLOCKS * gr + st // 2 + 1)
                    s.activation(Pb[st % PRING], score_ps[st % 2][:, :, :], ACT.Exp).then_inc(s_exp, 1)
                    if st == 1 and not first:
                        out_copy(gr - 1, 1)
                    if st == 8 and not last:
                        act.wait_ge(s_dec, apart(act, OPEN + 16 * gr))
                        decay_tables(gr + 1, hg + 1, b)
                    if st == 17:
                        out_copy(gr, 0)
            act.nop().then_inc(s_exp, 2)
            act.nop().then_inc(s_oev, 2)
            decay_tables(0, 0, 0)
            for hg in range(HG):
                act_slot(0, hg, hg == 0, False)
            with act.Fori(1, B - 1) as b:
                for hg in range(HG):
                    act_slot(b, hg, False, False)
            for hg in range(HG):
                act_slot(B - 1, hg, False, hg == HG - 1)
            out_copy(NG - 1, 1)

            def act_shared(b):
                for half in range(2):
                    for hc in range(HC):
                        n = HC * half + hc
                        act.wait_ge(s_g1, 16 * b + n + 1)
                        if hc == 0:
                            act.wait_ge(s_g2, OPEN + 4 * b + 2 * half)
                        s.activation(HT[:, hc, :], hib[n % 2], ACT.Relu, bias=sb1c[:, hc:hc + 1]).then_inc(s_relu, 1)

            def act3b(b):
                for n in range(4):
                    act.wait_ge(s_ntr, 4 * b + n + 1)
                    half, fc = n // 2, n % 2
                    s.copy(NTr[:, fc, 512 * half:512 * half + 512], low[n]).then_inc(s_nT, 1)
            act3b(0)
            with act.Fori(1, B) as b:
                act_shared(b - 1)
                act3b(b)
            act.wait_ge(s_lgc, B)
            act.wait_ge(s_wo, 4 * B)
            s.activation(PR.rearrange("p t e -> p (t e)"), LG[:, :, :].rearrange("p t e -> p (t e)"), ACT.Exp, scale=-1.0).then_inc(s_ex4, 1)
            act_shared(B - 1)

            def x_copy(i, it, u):
                act.wait_ge(s_xtr, OPEN + i + 1)
                if not (isinstance(i, int) and i < 2):
                    act.wait_ge(s_u2, 2 * i - 2)
                s.copy(XT[u % 2].rearrange("p c t -> p (c t)"), hib[2 + u % 2][:, 0:KC * P]).then_inc(s_xT, 1)

            def relu(i, u, e):
                act.wait_ge(s_htr, apart(act, i + 1))
                if not (isinstance(i, int) and i < 2):
                    act.wait_ge(s_d, apart(act, i - 1))
                for hc in range(HC):
                    s.activation(Ht[u % 2][:, hc, :], low[2 + hc // 4][:, P * (hc % 4):P * (hc % 4) + P], ACT.Relu,
                                 bias=smallT[:, bass.ds(e * HC + 56 + hc, 1)]).then_inc(s_hr, 1)

            def act5(it, first, last):
                for u in range(4):
                    i = 4 * it + u
                    e = act.value_load(ET[0:1, bass.ds(i, 1)], min_val=0, max_val=NE - 1)
                    if not last or u + 2 < 4:
                        x_copy(i + 2, it, u + 2)
                    relu(i, u, e)
            act.wait_ge(s_pos, 1)
            x_copy(0, 0, 0)
            x_copy(1, 0, 1)
            act5(0, True, False)
            with act.Fori(1, NTILE // 4 - 1) as it:
                act5(it, False, False)
            act5(NTILE // 4 - 1, False, True)

            for b in range(B):
                act.wait_ge(s_yl[b], 32)
                for t in range(TB):
                    ins = s.activation(Yb[b][0][:, t, :], Yb[b][0][:, t, :], ACT.Identity, scale=WG[:, 0, TB * b + t:TB * b + t + 1])
                ins.then_inc(s_w0, 1)

        @block.vector
        def _(dve):
            v = nc.vector
            for opened in (s_p3, s_vev, s_rr, s_g2e, s_mean, s_zb, s_g2m, s_mc):
                dve.nop().then_inc(opened, OPEN)
            chain = Chain(dve, s_dve)
            for i in range(5):
                dve.wait_ge(s_wtr, i + 1)
                v.tensor_copy(wT[:, i, :, :].rearrange("p c e -> p (c e)"), (low + hib)[i]).then_inc(s_wev, 1)
            dve.wait_ge(s_wtr, 6)
            v.tensor_copy(smallT[:, :], hib[1][:, 0:56 + NE * HC]).then_inc(s_wev, 1)
            dve.wait_ge(s_wev, 6)
            chain(v.tensor_copy(wdr, smallT[:, 0:KC * H].rearrange("p (c h) -> p c h", c=KC).unsqueeze(3).broadcast_to([P, KC, H, TB])))
            dve.wait_ge(s_ce, 1)
            chain(v.tensor_scalar(cE, cE, 1.0, None, ALU.add))
            chain(v.reciprocal(cE, cE))
            chain(v.tensor_tensor(scT, smallT[:, 48:56].rearrange("p (c b) -> p c b", c=KC), cE, ALU.mult))
            dve.wait_ge(s_ones, 1)
            for c in range(KC):
                for b in range(B):
                    v.tensor_scalar(scB[:, c, b, :], ones[:, :], scT[:, c, b:b + 1], None, ALU.mult).then_inc(s_sc, 1)
            def rsqrt(step, r, w, x):
                ri, xi = r.bitcast(I32), x.bitcast(I32)
                step(v.tensor_scalar(ri, xi, 1, None, ALU.logical_shift_right))
                step(v.tensor_scalar(ri, ri, -1.0, float(0x5f3759df), ALU.mult, ALU.add))
                for _ in range(3):
                    step(v.scalar_tensor_tensor(w, r, -0.5, r, ALU.mult, ALU.mult))
                    step(v.tensor_tensor(w, w, x, ALU.mult))
                    step(v.scalar_tensor_tensor(r, w, 1.5, r, ALU.add, ALU.mult))

            def statistics(b):
                tiles = slice(TB * b, TB * b + TB)
                dve.wait_ge(s_x[b], 16)
                for t in range(TB * b, TB * b + TB):
                    ins = v.bn_stats(st6[:, t, :], X[:, t, :])
                chain(ins)
                for t in range(TB * b, TB * b + TB):
                    ins = v.bn_aggr(mv1[:, t, :], st6[:, t, :])
                chain(ins)
                chain(v.tensor_scalar(tmpA[:, tiles], mv1[:, tiles, 1], 1e-5, None, ALU.add))
                rsqrt(chain, rst1[:, tiles], tmpB[:, tiles], tmpA[:, tiles])
            statistics(0)
            dve.wait_ge(s_mod, 1)
            v.tensor_copy(modT[:, 0:2, :], hib[2][:, 0:8].rearrange("p (n b) -> p n b", n=2)).then_inc(s_dve, 1)
            chain.n += 1
            v.tensor_scalar(modT[:, 2:4, :], hib[2][:, 8:16].rearrange("p (n b) -> p n b", n=2), 1.0, None, ALU.add).then_inc(s_modc, 1)
            statistics(1)
            dve.wait_ge(s_cst, 16 * N_CST)
            chain(v.tensor_scalar(fcol[:, 0:2], fcol[:, 0:2], 0.25, None, ALU.mult))
            chain(v.memset(Vx[:, :, :, HD:32], 1.0))
            base1 = chain.n

            def normalise(b):
                for t in range(TB):
                    tt = b * TB + t
                    if t == 0:
                        dve.wait_ge(s_tr, OPEN + 4 * b)
                    v.tensor_scalar(xh[:, t, :], X[:, bass.ds(tt, 1), :].rearrange("p o e -> p (o e)"),
                                    mv1[:, bass.ds(tt, 1), 0], rst1[:, bass.ds(tt, 1)],
                                    ALU.subtract, ALU.mult).then_inc(s_xh, 1)

            def batch(b, base, last):
                chain.start(base)
                dve.wait_ge(s_hT, OPEN + 4 * b + 4)
                chain(v.tensor_tensor(mean2[:, :], hsum[:, 0:4:2], hsum[:, 1:4:2], ALU.add))
                v.tensor_scalar(mean2[:, :], mean2[:, :], 1.0 / T, None, ALU.mult).then_inc(s_mean, 1)

                def rest2(c):
                    dve.wait_ge(s_p2, 4 * b + c + 1)
                    v.tensor_tensor(pb[:, c, 2, :], rope_r[:, c % 2, :], pb[:, c, 1, :], ALU.subtract).then_inc(s_p3, 1)

                def log_decay(b):
                    dve.wait_ge(s_e16, 2 * b + 2)
                    chain(v.tensor_scalar(lt[:, 5:6], lt[:, 3:4], -2.0 ** -5, 1.0, ALU.mult, ALU.add))
                    chain(v.tensor_scalar(lt[:, 6:7], lt[:, 5:6], -1.0, 1.0, ALU.mult, ALU.add))
                    chain(v.tensor_scalar(lt[:, 7:8], lt[:, 6:7], 1.0 / 7, 1.0 / 6, ALU.mult, ALU.add))
                    for k in (5, 4, 3, 2, 1):
                        chain(v.tensor_scalar(lt[:, 7:8], lt[:, 7:8], lt[:, 6:7], 1.0 / k, ALU.mult, ALU.add))
                    chain(v.tensor_tensor(lt[:, 9:10], lt[:, 7:8], lt[:, 6:7], ALU.mult))
                    chain(v.tensor_scalar(lt[:, 8:9], lt[:, 9:10], -1.0, None, ALU.mult))
                    chain(v.tensor_copy(l3[:, 0:1], lt[:, 8:9]))
                    chain(v.tensor_tensor(lt[:, 10:11], lt[:, 8:9], l3[:, 0:1], ALU.subtract))
                    chain(v.tensor_copy(l3[:, 1:2], lt[:, 10:11]))
                    v.tensor_tensor(l3[:, 2:3], lt[:, 10:11], l3[:, 1:2], ALU.subtract).then_inc(s_ld, 1)

                for c in range(4):
                    dve.wait_ge(s_qkev, apart(dve, 8 * b + 2 * c + 2))
                    chain(v.stream_shuffle(rope_s[:, c % 2, :], qs[:, c, :], [i ^ 1 for i in range(32)]))
                    chain(v.tensor_tensor(rope_s[:, c % 2, :], rope_s[:, c % 2, :], sinT, ALU.mult))
                    dve.wait_ge(s_cosm, OPEN + 4 * b + c + 1)
                    if c >= 2:
                        rest2(c - 2)
                        dve.wait_ge(s_p3, OPEN + 4 * b + c - 1)
                    else:
                        dve.wait_ge(s_p3, OPEN + 4 * b)
                    v.tensor_tensor(rope_r[:, c % 2, :], rope_1[:, c % 2, :], rope_s[:, c % 2, :], ALU.add).then_inc(s_rr, 1)
                    if c == 1 and not last:
                        normalise(b + 1)
                    if c == 1:
                        dve.wait_ge(s_proj, OPEN + 17 * b + PROJECTED[16])
                        dve.wait_ge(s_ldo, OPEN + 16 * b)
                        dve.wait_ge(s_qe, OPEN + b)
                        v.tensor_copy(lt[:, 0:1], low[0][:, 0:1]).then_inc(s_zb, 1)
                    if c == 2:
                        dve.wait_ge(s_e16, 2 * b + 1)
                        chain(v.tensor_scalar(lt[:, 4:5], lt[:, 1:2], 1.0, None, ALU.add))
                        v.reciprocal(lt[:, 2:3], lt[:, 4:5]).then_inc(s_pd, 1)
                    if c == 3:
                        log_decay(b)
                for n in range(4):
                    dve.wait_ge(s_proj, OPEN + 17 * b + PROJECTED[12 + n])
                    if n == 0:
                        dve.wait_ge(s_vout, OPEN + 16 * b)
                    for k in range(2):
                        ins = v.tensor_tensor(Vx[:, 2 * n + k, :, 0:HD], hib[n][:, E * k:E * k + E].rearrange("p (h d) -> p h d", h=H),
                                              bv_row[:, :].rearrange("p (h d) -> p h d", h=H), ALU.add)
                    ins.then_inc(s_vev, 1)
                rest2(2)
                rest2(3)
            per1 = 1 + 8 + 1 + 3 + 5 + 2 + 3
            normalise(0)
            base1 = chain.n
            batch(0, base1, False)
            assert chain.n == per1
            statistics(2)
            statistics(3)
            base2 = chain.base + chain.n - per1
            with dve.Fori(1, B - 1) as b:
                batch(b, base2 + b * per1, False)
            batch(B - 1, base2 + (B - 1) * per1, True)

            def take_max(gr, x):
                dve.wait_ge(s_mm, MSEQ * gr + x + 1)
                if x == 0:
                    dve.wait_ge(s_mc, OPEN + gr)
                banks = first_max if isinstance(gr, int) and gr == 0 else max_ps
                v.tensor_reduce(mp[:, x:x + 1], banks[x % len(banks)], AX.X, ALU.max).then_inc(s_mx, 1)

            def combine(gr):
                dve.wait_ge(s_mx, MSEQ * gr + NMAX + 2)
                v.tensor_reduce(mc[:, :], mp[:, :].rearrange("p (x k) -> p x k", k=2), AX.X, ALU.max).then_inc(s_mc, 1)
                dve.wait_ge(s_mm, MSEQ * (gr + 1))
                dve.wait_ge(s_mrow, OPEN + 16 * gr)
                v.tensor_scalar(mrow[:, :], max_ps[0][0:NMAX // 2, 0:P], -1.0, None, ALU.mult).then_inc(s_mx, 1)

            dve.nop().then_inc(s_mx, 2)
            for x in range(NMAX):
                take_max(0, x)
            combine(0)
            def invert(b0, b1, count):
                dve.wait_ge(s_sums, count)
                v.reciprocal(sums[:, b0:b1, :], sums[:, b0:b1, :]).then_inc(s_inv, 1)

            def dve_slot(b, hg, last):
                gr = base_of(b) + hg
                if not last or hg + 1 < HG:
                    for x in range(NMAX):
                        if last and hg == HG - 2 and x == NMAX // 2:
                            invert(0, B - 1, 16)
                        take_max(gr + 1, x)
                    combine(gr + 1)
            with dve.Fori(0, B - 1) as b:
                for hg in range(HG):
                    dve_slot(b, hg, False)
            for hg in range(HG):
                dve_slot(B - 1, hg, True)

            ch3 = Chain(dve, s_c3, apart)

            def front_a(b):
                ch3.start(FRONT_A * b)
                dve.wait_ge(s_ot, 32 * b + 32)
                dve.wait_ge(s_rb, 256 * b + 256)
                ch3(v.tensor_tensor(OT, OT, RB, ALU.mult))
                for n in range(4):
                    ins = v.bn_stats(st3[:, n, :], OT[:, n // 2, 512 * (n % 2):512 * (n % 2) + 512])
                ch3.apart(ins)
                for c in range(KC):
                    ins = v.bn_aggr(mvf[:, c, :], st3[:, 2 * c:2 * c + 2, :].rearrange("p n s -> p (n s)"))
                ch3(ins)
                ch3(v.tensor_tensor(q3[:, 0, :], mvf[:, :, 0], mvf[:, :, 0], ALU.mult))
                v.tensor_tensor(mvf[:, :, 1], mvf[:, :, 1], q3[:, 0, :], ALU.add).then_inc(s_fst, 1)
                assert ch3.n == FRONT_A

            def front_b(b):
                ch3.sem = s_c3b
                ch3.start(FRONT_B * b)
                dve.wait_ge(s_gmm, b + 1)
                v.tensor_copy(gst[:, :, :].rearrange("p c k -> p (c k)"), hib[0][:, 0:4]).then_inc(s_gst, 1)
                dve.wait_ge(s_gst, b + 1)
                ch3(v.tensor_tensor(q3[:, 0, :], gst[:, :, 0], gst[:, :, 0], ALU.mult))
                ch3(v.tensor_tensor(q3[:, 1, :], gst[:, :, 1], q3[:, 0, :], ALU.subtract))
                ch3(v.tensor_scalar(q3[:, 1, :], q3[:, 1, :], 1e-5, None, ALU.add))
                rsqrt(ch3, q3[:, 3, :], q3[:, 4, :], q3[:, 1, :])
                ch3(v.tensor_tensor(q3[:, 3, :], q3[:, 3, :], fcol[:, 8:10], ALU.mult))
                ch3(v.tensor_tensor(q3[:, 4, :], q3[:, 3, :], gst[:, :, 0], ALU.mult))
                ch3(v.tensor_tensor(q3[:, 4, :], fcol[:, 10:12], q3[:, 4, :], ALU.subtract))
                for c in range(KC):
                    ins = v.tensor_scalar(OT[:, c, :], OT[:, c, :], q3[:, 3, c:c + 1], q3[:, 4, c:c + 1], ALU.mult, ALU.add)
                ch3(ins)
                v.tensor_tensor(OT, OT, GT, ALU.mult).then_inc(s_gt, 1)
                assert ch3.n == FRONT_B
                ch3.sem = s_c3

            def tail(b):
                ch3.sem = s_c3c
                ch3.start(TAIL * b)
                dve.wait_ge(s_xbo, b + 1)
                for n in range(4):
                    dve.wait_ge(s_wo, 4 * b + n + 1)
                    u = U[:, n % 2, :].rearrange("p (t e) -> p t e", t=2)
                    made = hib[n % 3] if isinstance(b, int) and b == 0 else low[n]
                    v.tensor_tensor(u, made.rearrange("p (t e) -> p t e", t=2),
                                    rows[:, 0, bass.ds(b, 1), :].broadcast_to([P, 2, E]), ALU.mult).then_inc(s_woev, 1)
                    dve.wait_ge(s_woev, 4 * b + n + 1)
                    xx = X[:, bass.ds(b * TB + 2 * n, 2), :]
                    ins = v.tensor_tensor(xx, xx, u, ALU.add)
                    if n < 3:
                        ch3(ins)
                ch3.apart(ins)
                for t in range(TB):
                    ins = v.bn_stats(stx[:, t, :], X[:, bass.ds(b * TB + t, 1), :].rearrange("p o e -> p (o e)"))
                ch3.apart(ins)
                for t in range(TB):
                    ins = v.bn_aggr(mvx[:, t, :], stx[:, t, :])
                ch3(ins)
                ch3(v.tensor_scalar(q8[:, 0, :], mvx[:, :, 1], 1e-5, None, ALU.add))
                rsqrt(ch3, q8[:, 5, :], q8[:, 6, :], q8[:, 0, :])
                dve.wait_ge(s_nst, 16 * b)
                dve.wait_ge(s_ntr, 4 * b)
                cb, sbr = (rows[:, k, bass.ds(b, 1), :].rearrange("p o e -> p (o e)") for k in (2, 1))
                for t in range(TB):
                    ins = v.scalar_tensor_tensor(H2[:, t, :], X[:, bass.ds(b * TB + t, 1), :].rearrange("p o e -> p (o e)"),
                                                 mvx[:, t, 0:1], cb, ALU.subtract, ALU.mult)
                ins.then_inc(s_h2, 1)
                dve.wait_ge(s_h2, b + 1)
                for t in range(TB):
                    ins = v.scalar_tensor_tensor(H2[:, t, :], H2[:, t, :], q8[:, 5, t:t + 1], sbr, ALU.mult, ALU.add)
                ch3.apart(ins)
                for t in range(TB):
                    ins = v.bn_stats(stx[:, t, :], H2[:, t, :])
                ch3.apart(ins)
                for t in range(TB):
                    ins = v.bn_aggr(mvx[:, t, :], stx[:, t, :])
                ch3(ins)
                ch3(v.tensor_tensor(q8[:, 1, :], mvx[:, :, 0], mvx[:, :, 0], ALU.mult))
                ch3(v.tensor_tensor(q8[:, 1, :], q8[:, 1, :], mvx[:, :, 1], ALU.add))
                ch3(v.tensor_scalar(q8[:, 3, :], q8[:, 1, :], 1e-8, None, ALU.add))
                rsqrt(ch3, q8[:, 5, :], q8[:, 6, :], q8[:, 3, :])
                for t in range(TB):
                    ins = v.scalar_tensor_tensor(H2[:, t, :], H2[:, t, :], q8[:, 5, t:t + 1], nw_row, ALU.mult, ALU.mult)
                ins.then_inc(s_n, 1)
                assert ch3.n == TAIL
                ch3.sem = s_c3

            def dve_shared(b, n0, n1):
                dve.wait_ge(s_xsb, b + 1)
                for n in range(n0, n1):
                    dve.wait_ge(s_g2, OPEN + 4 * b + n + 1)
                    u = U[:, n % 2, :].rearrange("p (t e) -> p t e", t=2)
                    v.tensor_tensor(u, hib[2 + n % 2].rearrange("p (t e) -> p t e", t=2),
                                    rows[:, 3, bass.ds(b, 1), :].broadcast_to([P, 2, E]), ALU.mult).then_inc(s_g2m, 1)
                    dve.wait_ge(s_g2m, OPEN + 4 * b + n + 1)
                    xx = X[:, bass.ds(b * TB + 2 * n, 2), :]
                    v.tensor_tensor(xx, xx, u, ALU.add).then_inc(s_g2e, 1)

            def dve3b(b):
                dve.wait_ge(s_lg, b + 1)
                v.tensor_copy(LG[:, bass.ds(b * TB, TB), :].rearrange("p t e -> p (t e)"), hib[3][:, 0:TB * NE]).then_inc(s_lgc, 1)
            RSQRT = 2 + 3 * 3
            FRONT_A, FRONT_B, TAIL = 4, 3 + RSQRT + 3 + 1, 3 + 3 + 1 + RSQRT + 2 + 1 + 3 + RSQRT
            ch4 = Chain(dve, s_c4)
            def gates(b, k):
                gr = rows[:, k, b, :]
                ch4(v.scalar_tensor_tensor(mag, gr, -1.0, gr, ALU.mult, ALU.max))
                ch4(v.tensor_scalar(sgn, gr, 0.0, 2.0, ALU.is_ge, ALU.mult))
                ch4(v.tensor_scalar(mag, mag, 0.25, None, ALU.max))
                ch4(v.scalar_tensor_tensor(gr, sgn, -1.0, mag, ALU.add, ALU.mult))
            ch4(v.tensor_scalar(rows[:, 2, :, :], rows[:, 2, :, :], 1.0, None, ALU.add))
            gates(0, 0)
            dve.nop().then_inc(s_rows, 1)
            front_a(0)
            front_b(0)
            dve.wait_ge(s_sw, 64)
            tail(0)
            front_a(1)
            front_b(1)
            for b, k in [(0, 3)] + [(b, k) for b in range(1, B) for k in (0, 3)]:
                gates(b, k)
            dve.nop().then_inc(s_rows, 1)
            invert(B - 1, B, 32)
            dve3b(0)
            with dve.Fori(1, B - 1) as b:
                tail(b)
                dve_shared(b - 1, 0, 2)
                front_a(b + 1)
                dve_shared(b - 1, 2, 4)
                front_b(b + 1)
                dve3b(b)
            tail(B - 1)
            dve_shared(B - 2, 0, 4)
            dve3b(B - 1)
            c5 = Chain(dve, s_c5)
            dve.wait_ge(s_rc, 112)
            dve.wait_ge(s_ex4, 1)
            flat = "p t e -> p (t e)"
            c5(v.tensor_scalar(PR.rearrange(flat), PR.rearrange(flat), 1.0, None, ALU.add))
            c5(v.reciprocal(PR.rearrange(flat), PR.rearrange(flat)))
            src = PR
            for k, OH in ((0, OH1), (1, OH2)):
                m, ix = m12[:, k, :], i12[:, k, :]
                c5(v.tensor_reduce(m, src, AX.X, ALU.max))
                c5(v.tensor_tensor(MK, src, m.unsqueeze(2).broadcast_to([P, NT, NE]), ALU.is_equal))
                c5(v.tensor_tensor(MK, MK, eidx, ALU.mult))
                c5(v.tensor_reduce(ix, MK, AX.X, ALU.min))
                c5(v.tensor_tensor(OH, eidx, ix.unsqueeze(2).broadcast_to([P, NT, NE]), ALU.is_equal))
                if k == 0:
                    c5(v.scalar_tensor_tensor(P2.rearrange(flat), OH.rearrange(flat), -2.0, PR.rearrange(flat), ALU.mult, ALU.add))
                    src = P2
            v.tensor_tensor(MM.rearrange(flat), OH1.rearrange(flat), OH2.rearrange(flat), ALU.add).then_inc(s_m4, 1)
            c5(v.tensor_tensor(sm, m12[:, 0, :], m12[:, 1, :], ALU.add))
            c5(v.tensor_scalar(sm, sm, 1e-6, None, ALU.add))
            c5(v.reciprocal(sm, sm))
            for k in range(2):
                c5(v.tensor_tensor(WG[:, k, :], m12[:, k, :], sm, ALU.mult))
            c5(v.memset(one32, 1.0))
            dve.wait_ge(s_pe4, 1)
            c5(v.tensor_copy(TOT.rearrange(flat), low[1][:, 0:NT * NE]))
            for e in range(NE):
                ins = v.tensor_tensor_scan(CUM[:, e, :], one32, TOT[:, :, e], 0.0, ALU.mult, ALU.add)
            c5(ins)
            c5(v.tensor_tensor(EXC, CUM.rearrange("p e t -> p t e"), TOT, ALU.subtract))
            c5(v.tensor_scalar(nti, CUM[:, :, NT - 1], 1.0 / P, (P - 1) / P - 0.5 + 0.5 / P, ALU.mult, ALU.add))
            c5(v.tensor_copy(ntf, nti))
            c5(v.tensor_tensor_scan(tinc, one32[:, 0:NE], ntf, 0.0, ALU.mult, ALU.add))
            c5(v.tensor_tensor(tslot, tinc, ntf, ALU.subtract))
            c5(v.tensor_scalar(tslot, tslot, float(P), None, ALU.mult))
            c5(v.tensor_tensor(EXC, EXC, tslot.unsqueeze(1).broadcast_to([P, NT, NE]), ALU.add))
            c5(v.tensor_tensor(POS.rearrange(flat), low[0][:, 0:NT * NE], EXC.rearrange(flat), ALU.add))
            for k, OH in ((0, OH1), (1, OH2)):
                c5(v.tensor_tensor(MK, OH, POS, ALU.mult))
                c5(v.tensor_reduce(pf[:, k, :], MK, AX.X, ALU.add))
            c5(v.tensor_copy(POSI, pf))
            c5(v.tensor_scalar(QI, POSI, 7, None, ALU.arith_shift_right))
            c5(v.tensor_scalar(RI, POSI, P - 1, None, ALU.bitwise_and))
            c5(v.tensor_copy(QF, QI))
            c5(v.tensor_copy(RF, RI))
            c5(v.tensor_scalar(etf[:, 0:NTILE], tile_no, tinc[:, 0:1], None, ALU.is_ge))
            for e in range(1, NE - 1):
                c5(v.scalar_tensor_tensor(etf[:, 0:NTILE], tile_no, tinc[:, e:e + 1], etf[:, 0:NTILE], ALU.is_ge, ALU.add))
            v.tensor_copy(ET[:, 0:NTILE], etf[:, 0:NTILE]).then_inc(s_pos, 1)
            def slot_marks(c):
                k, t0 = c * TC // NT, c * TC % NT
                if c >= 4:
                    dve.wait_ge(s_tm, c - 3)
                ob = one_b[c % 4]
                c5(v.tensor_tensor(one_a[c % 4], lane.unsqueeze(1).broadcast_to([P, TC, P]),
                                   RF[:, k, t0:t0 + TC].unsqueeze(2).broadcast_to([P, TC, P]), ALU.is_equal))
                c5(v.tensor_tensor(ob[:, :, 1, :], tile_no.unsqueeze(1).broadcast_to([P, TC, NTILE]),
                                   QF[:, k, t0:t0 + TC].unsqueeze(2).broadcast_to([P, TC, NTILE]), ALU.is_equal))
                c5(v.tensor_scalar(ob[:, :, 0, :], ob[:, :, 1, :], part[:, 0:1], None, ALU.mult))
                v.tensor_tensor(ob[:, :, 1, :], ob[:, :, 1, :], place[:, k, t0:t0 + TC].unsqueeze(2).broadcast_to([P, TC, NTILE]), ALU.mult).then_inc(s_ob, 1)
            dve.wait_ge(s_nst, 16 * B)
            dve.wait_ge(s_ntr, 4 * B)
            dve.wait_ge(s_xsb, B)
            slot_marks(0)
            slot_marks(1)
            dve_shared(B - 1, 0, 2)
            for c in range(2, 2 * NT // TC):
                slot_marks(c)
            dve.wait_ge(s_tm, 2 * NT // TC)
            c5(v.tensor_copy(sums4, low[2][:, 0:2 * NTILE]))
            c5(v.scalar_tensor_tensor(dest, sums4[:, NTILE:2 * NTILE], float(P), sums4[:, 0:NTILE], ALU.mult, ALU.add))
            c5(v.scalar_tensor_tensor(unused, sums4[:, NTILE:2 * NTILE], 0.5, spare, ALU.is_lt, ALU.mult))
            c5(v.tensor_scalar(token, dest, float(-P), 0.0, ALU.add, ALU.max))
            c5(v.scalar_tensor_tensor(dest, dest, float(-P), unused, ALU.add, ALU.add))
            c5(v.tensor_copy(DIX, dest))
            c5(v.tensor_scalar(unused, token, float(B * T), float(-B * T), ALU.is_ge, ALU.mult))
            c5(v.tensor_tensor(token, token, unused, ALU.add))
            v.tensor_copy(TIX, token).then_inc(s_tix, 1)
            dve_shared(B - 1, 2, 4)

            def hidden(i, u):
                for half in range(2):
                    dve.wait_ge(s_u2, 2 * i + half + 1)
                    if half == 0 and not (isinstance(i, int) and i < 2):
                        dve.wait_ge(s_htr, i - 1)
                    v.tensor_copy(Hn[u % 2][:, 512 * half:512 * half + 512], low[half]).then_inc(s_hn, 1)

            def result(i, it, u, e):
                dve.wait_ge(s_d, i + 1)
                if u >= 2:
                    dve.wait_ge(s_yo[u % 2], 32 * it + 16)
                elif not isinstance(it, int) or it > 0:
                    dve.wait_ge(s_yo[u % 2], 32 * it)
                v.tensor_tensor(Yt[u % 2], hib[u % 2][:, 0:E], eb2r[:, bass.ds(e, 1), :].rearrange("p o e -> p (o e)"), ALU.add).then_inc(s_y, 1)

            def dve5(it, last):
                for u in range(4):
                    i = 4 * it + u
                    e = dve.value_load(ET[0:1, bass.ds(i, 1)], min_val=0, max_val=NE - 1)
                    if not last or u + 1 < 4:
                        hidden(i + 1, u + 1)
                    result(i, it, u, e)
            dve.wait_ge(s_pos, 1)
            dve.wait_ge(s_eb2, 16)
            hidden(0, 0)
            dve5(0, False)
            with dve.Fori(1, NTILE // 4 - 1) as it:
                dve5(it, False)
            dve5(NTILE // 4 - 1, True)

            for b in range(B):
                y0, y1 = Yb[b]
                dve.wait_ge(s_w0, b + 1)
                for t in range(TB):
                    ins = v.scalar_tensor_tensor(y1[:, t, :], y1[:, t, :], WG[:, 1, TB * b + t:TB * b + t + 1], y0[:, t, :], ALU.mult, ALU.add)
                ins.then_inc(s_c6, 1)
                dve.wait_ge(s_c6, 2 * b + 1)
                v.tensor_tensor(y1, y1, rows[:, 3, b, :].unsqueeze(1).broadcast_to([P, TB, E]), ALU.mult).then_inc(s_c6, 1)
            dve.wait_ge(s_c6, 2 * B)
            xx = X[:, TB * (B - 1):TB * B, :]
            v.tensor_tensor(xx, xx, Yb[B - 1][1], ALU.add).then_inc(s_fin, 1)

        @block.tensor
        def _(pe):
            t = nc.tensor
            for opened in (s_g2, s_xtr, s_tr, s_proj):
                pe.nop().then_inc(opened, OPEN)
            pe.wait_ge(s_w, 16 * N_W)
            banks = low + hib
            for i in range(5):
                for ic in range(KC):
                    for oc in range(KC):
                        ins = t.transpose(banks[i][:, E * ic + P * oc:E * ic + P * oc + P], wn[:, i, oc, P * ic:P * ic + P], ident[:, :])
                ins.then_inc(s_wtr, 1)
            for src, n, col in ((wdn, H, 0), (rwn, NE, 32), (cn, B, 48)):
                for c in range(KC):
                    ins = t.transpose(hib[1][:, col + n * c:col + n * c + n], src[0:n, P * c:P * c + P], ident[0:n, 0:n])
            ins = t.transpose(hib[1][:, 56:56 + NE * HC], ebn[0:NE * HC, :], ident[0:NE * HC, 0:NE * HC])
            ins.then_inc(s_wtr, 1)
            pe.wait_ge(s_sc, 8)
            pe.wait_ge(s_wev, 6)
            pe.wait_ge(s_wm, 16)
            for n in range(4):
                for c in range(KC):
                    ins = t.matmul(hib[2][:, 4 * n:4 * n + 4], wmod[:, c, P * n:P * n + P], scT[:, c, :], start=c == 0, stop=c == KC - 1)
            ins.then_inc(s_mod, 1)
            for n in range(8):
                b, half = n // 2, n % 2
                if n >= 4:
                    pe.wait_ge(s_rowc, n - 3)
                for c in range(KC):
                    ins = t.matmul(low[n % 4], scB[:, c, b, :], wmod[:, c, 512 + 512 * half:1024 + 512 * half], start=c == 0, stop=c == KC - 1)
                ins.then_inc(s_mod, 1)
            pe.wait_ge(s_rowc, 8)
            pe.wait_ge(s_modc, 1)
            pe.wait_ge(s_cst, 16 * N_CST)

            def project(b, j):
                dst = hib[j % 4]
                if j < 12:
                    w, oc, half = (0, 1, 3)[j // 4], j % 4 // 2, j % 2
                    for c in range(KC):
                        ins = t.matmul(dst, wT[:, w, c, P * oc:P * oc + P], hT[:, c, 512 * half:512 * half + 512], start=c == 0, stop=c == KC - 1)
                elif j < 16:
                    for k in range(2):
                        tt = 2 * (j - 12) + k
                        for c in range(KC):
                            ins = t.matmul(dst[:, E * k:E * k + E], hT[:, c, P * tt:P * tt + P], wT[:, 2, c, :], start=c == 0, stop=c == KC - 1)
                else:
                    for c in range(KC):
                        ins = t.matmul(low[0][:, 0:1], wdr[:, c, :, :].rearrange("p h q -> p (h q)"), mean2[:, c:c + 1], start=c == 0, stop=False)
                    ins = t.matmul(low[0][:, 0:1], eight, bd16[:, :], start=False, stop=True)
                ins.then_inc(s_proj, 1)

            with pe.Fori(0, B) as b:
                for half in range(2):
                    for fc in range(KC):
                        n = 2 * half + fc
                        for k in range(4):
                            tt = 4 * half + k
                            pe.wait_ge(s_xh, TB * b + tt + 1)
                            if n == 0 and k == 0:
                                pe.wait_ge(s_hT, OPEN + 4 * b)
                                pe.wait_ge(s_zb, OPEN + b)
                            ins = t.transpose(low[n][:, P * k:P * k + P], xh[:, tt, P * fc:P * fc + P], ident[:, :])
                        ins.then_inc(s_tr, 1)
                for j in ORDER:
                    if j == 0:
                        pe.wait_ge(s_hT, OPEN + 4 * b + 4)
                        pe.wait_ge(s_vev, OPEN + 4 * b)
                    elif 4 <= j < 12:
                        pe.wait_ge(s_qkev, 8 * b + j - 3)
                    elif 12 <= j < 16:
                        pe.wait_ge(s_gate, OPEN + 4 * b + j - 11)
                    elif j == 16:
                        pe.wait_ge(s_mean, OPEN + b + 1)
                    project(b, j)

            pe.wait_ge(s_hT, OPEN + 4 * B)
            pe.wait_ge(s_zb, OPEN + B)
            pe.wait_ge(s_kx[0], 16 * GH)
            pe.nop().then_inc(s_pv, 4)

            def max_scores(gr, hg, x, uses):
                h, qt, kh = x // 16, x % 16 // 2, x % 2
                banks = first_max if isinstance(gr, int) and gr == 0 else max_ps
                if x == 0:
                    pe.wait_ge(s_stk[hg], 16 * 13 * uses)
                pe.wait_ge(s_mx, MSEQ * gr + 2 + max(x - len(banks) + 1, 0))
                t.matmul(banks[x % len(banks)], stackQ[hg][0:ROWS_QK, h, P * qt:P * qt + P],
                         stackK[hg][0:ROWS_QK, h, 512 * kh:512 * kh + 512], start=True, stop=True).then_inc(s_mm, 1)

            def max_turn(gr):
                pe.wait_ge(s_mc, OPEN + gr + 1)
                t.transpose(max_ps[0][0:NMAX // 2, 0:P], mc[:, :], ident[:, :]).then_inc(s_mm, 1)

            def scores(gr, hg, st):
                qh, kt, hp = st // 16, st % 16 // 2, st % 2
                far = P * min(max(kt - 4 * qh, 0), 4)
                pe.wait_ge(s_exp, STEPS * gr + st + 1)
                for k in range(2):
                    h = 2 * hp + k
                    key = slice(P * kt, P * kt + P)
                    for c0, c1, rws in ((0, far, ROWS_FAR), (far, 512, ROWS_NEAR)):
                        if c1 > c0:
                            ins = t.matmul(score_ps[st % 2][:, k, c0:c1], stackK[hg][0:rws, h, key],
                                           stackQ[hg][0:rws, h, 512 * qh + c0:512 * qh + c1], start=True, stop=True)
                ins.then_inc(s_s, 1)

            def weigh(gr, hg, blk):
                qh, kt = blk // TB, blk % TB
                if kt == 0:
                    pe.wait_ge(s_oev, 2 * gr + qh + 2)
                if kt // 4 == qh:
                    pe.wait_ge(s_dec, OPEN + 16 * gr + (2 * kt + 2 if qh == 0 else 8 + 2 * (kt - 4) + 2))
                else:
                    pe.wait_ge(s_exp, STEPS * gr + 2 * blk + 4)
                for i in range(GH):
                    ins = t.matmul(out_ps[32 * i:32 * i + 32, :], Vst[hg % 2][:, kt, 32 * i:32 * i + 32],
                                   Pb[(2 * blk + i // 2) % PRING][:, i % 2, :], start=kt == 0, stop=kt == TB - 1,
                                   tile_position=(0, 32 * i))
                ins.then_inc(s_pv, 1)

            def head_stats(b):
                pe.wait_ge(s_fst, b + 1)
                t.matmul(hib[0][:, 0:4], head_avg[:, :], mvf[:, :, :].rearrange("p c k -> p (c k)"), start=True, stop=True).then_inc(s_gmm, 1)

            def gated_wo(b):
                pe.wait_ge(s_gt, b + 1)
                for n in range(4):
                    if isinstance(b, int) and b == 0:
                        if n == 3:
                            pe.wait_ge(s_woev, 1)
                    elif n == 0:
                        pe.wait_ge(s_nT, 4 * b)
                    made = hib[n % 3] if isinstance(b, int) and b == 0 else low[n]
                    for k in range(2):
                        tt = 2 * n + k
                        for c in range(KC):
                            ins = t.matmul(made[:, E * k:E * k + E], OT[:, c, P * tt:P * tt + P], wT[:, 4, c, :], start=c == 0, stop=c == KC - 1)
                    ins.then_inc(s_wo, 1)

            def pe_slot(b, hg, last, first=False):
                gr = base_of(b) + hg
                nxt = not last or hg + 1 < HG
                nhg = (hg + 1) % HG
                uses = b + 1 if hg + 1 < HG else b + 2
                pe.wait_ge(s_mrow, OPEN + 16 * (gr + 1))
                pe.wait_ge(s_vld[hg % 2], 16 * (2 * b + hg // 2 + 1))
                done = [0]

                def max_here(place):
                    while nxt and done[0] < max_items(place):
                        max_scores(gr + 1, nhg, done[0], uses)
                        done[0] += 1
                for blk in range(BLOCKS):
                    max_here(4 * blk)
                    scores(gr, hg, 2 * blk)
                    max_here(4 * blk + 1)
                    if nxt and blk == TURN_BLOCK:
                        max_turn(gr + 1)
                    if not nxt and blk == STATS_BLOCK:
                        pe.wait_ge(s_mx, MSEQ * NG + 2)
                        head_stats(0)
                    if not nxt and blk == WO_BLOCK:
                        pe.wait_ge(s_gst, 1)
                        gated_wo(0)
                    scores(gr, hg, 2 * blk + 1)
                    max_here(4 * blk + 2)
                    max_here(4 * blk + 3)
                    if blk:
                        weigh(gr, hg, blk - 1)
                    elif not first:
                        weigh(gr - 1, (hg - 1) % HG, BLOCKS - 1)

            for x in range(NMAX):
                max_scores(0, 0, x, 1)
            pe.wait_ge(s_vev, OPEN + 4 * B)
            max_turn(0)
            for i in range(1, 4):
                pe.wait_ge(s_kx[i], 16 * GH)
            for hg in range(HG):
                pe_slot(0, hg, False, first=hg == 0)
            with pe.Fori(1, B - 1) as b:
                for hg in range(HG):
                    pe_slot(b, hg, False)
            for hg in range(HG):
                pe_slot(B - 1, hg, True)
            weigh(NG - 1, HG - 1, BLOCKS - 1)

            def pe_shared(b, between=lambda place: None):
                pe.wait_ge(s_sw, 64)
                pe.wait_ge(s_gst, b + 2 if not isinstance(b, int) else B)
                for half in range(2):
                    for hc in range(HC):
                        n = HC * half + hc
                        if n >= 2:
                            pe.wait_ge(s_relu, OPEN + 16 * b + n - 1)
                        else:
                            pe.wait_ge(s_relu, OPEN + 16 * b)
                        for c in range(KC):
                            ins = t.matmul(hib[n % 2], sw1[:, c, P * hc:P * hc + P], NTr[:, c, 512 * half:512 * half + 512], start=c == 0, stop=c == KC - 1)
                        ins.then_inc(s_g1, 1)
                        between(n)
                    pe.wait_ge(s_relu, OPEN + 16 * b + 8 * half + 8)
                    for m in range(2):
                        n = 2 * half + m
                        if n == 0:
                            pe.wait_ge(s_g2m, OPEN + 4 * b)
                            pe.wait_ge(s_lgc, b + 1)
                        elif n >= 2:
                            pe.wait_ge(s_g2m, OPEN + 4 * b + n - 1)
                        for k in range(2):
                            for hc in range(HC):
                                ins = t.matmul(hib[2 + n % 2][:, E * k:E * k + E], HT[:, hc, P * (2 * m + k):P * (2 * m + k) + P], sw2[:, hc, :],
                                               start=hc == 0, stop=hc == HC - 1)
                        ins.then_inc(s_g2, 1)
                        between(2 * HC + n)

            def pe3b(b):
                pe.wait_ge(s_n, b + 1)
                pe.wait_ge(s_woev, 4 * b + 4)
                for n in range(4):
                    half, fc = n // 2, n % 2
                    for k in range(4):
                        ins = t.transpose(low[n][:, P * k:P * k + P], H2[:, 4 * half + k, P * fc:P * fc + P], ident[:, :])
                    ins.then_inc(s_ntr, 1)
                pe.wait_ge(s_nT, 4 * b + 4)
                pe.wait_ge(s_g2m, OPEN + 4 * b)
                for tt in range(TB):
                    for c in range(KC):
                        ins = t.matmul(hib[3][:, NE * tt:NE * tt + NE], NTr[:, c, P * tt:P * tt + P], smallT[:, 32 + NE * c:32 + NE * c + NE],
                                       start=c == 0, stop=c == KC - 1)
                ins.then_inc(s_lg, 1)

            pe.wait_ge(s_oev, 2 * NG + 2)
            pe.wait_ge(s_exp, STEPS * NG + 2)
            pe.wait_ge(s_woev, 4)
            head_stats(1)
            pe3b(0)
            with pe.Fori(1, B - 1) as b:
                gated_wo(b)
                pe_shared(b - 1)
                head_stats(b + 1)
                pe3b(b)
            gated_wo(B - 1)
            pe_shared(B - 2)
            pe3b(B - 1)
            def counts():
                pe.wait_ge(s_m4, 1)
                pe.wait_ge(s_nT, 4 * B)
                mm = MM.rearrange("p t e -> p (t e)")
                t.matmul(low[0][:, 0:NT * NE], before, mm, start=True, stop=True)
                t.matmul(low[1][:, 0:NT * NE], ones[:, :], mm, start=True, stop=True).then_inc(s_pe4, 1)

            def slot_table(c):
                pe.wait_ge(s_ob, c + 1)
                for j in range(TC):
                    ins = t.matmul(low[2][:, 0:2 * NTILE], one_a[c % 4][:, j, :], one_b[c % 4][:, j, :, :].rearrange("p v x -> p (v x)"),
                                   start=c == 0 and j == 0, stop=c == 2 * NT // TC - 1 and j == TC - 1)
                ins.then_inc(s_tm, 1)

            def routing(place):
                if place == HC - 1:
                    counts()
                for c in {2 * HC + 1: (0, 1), HC + 5: (2, 3), 2 * HC + 2: (4, 5, 6, 7)}.get(place, ()):
                    slot_table(c)
            pe_shared(B - 1, routing)

            def x_turn(i, it, u):
                pe.wait_ge(s_gx[u % 2], 32 * it + (16 if u % 4 < 2 else 32))
                if not (isinstance(i, int) and i < 2):
                    pe.wait_ge(s_xT, i - 1)
                for c in range(KC):
                    ins = t.transpose(hib[2 + u % 2][:, P * c:P * c + P], Xg[u % 2][:, P * c:P * c + P], ident[:, :])
                ins.then_inc(s_xtr, 1)

            def up(i, u, e):
                pe.wait_ge(s_xT, i + 1)
                if isinstance(i, int) and i < 5:
                    pe.wait_ge(s_ready, e + 1)
                for half in range(2):
                    if not isinstance(i, int) or i > 0:
                        pe.wait_ge(s_hn, 2 * i + half - 1)
                    for c in range(KC):
                        ins = t.matmul(low[half], XT[u % 2][:, c, :], W[:, bass.ds(e, 1), 0, 1024 * c + 512 * half:1024 * c + 512 * half + 512].rearrange("p o x -> p (o x)"),
                                       start=c == 0, stop=c == KC - 1)
                    ins.then_inc(s_u2, 1)

            def hidden_turn(i, u):
                if not isinstance(i, int) or i > 0:
                    pe.wait_ge(s_hr, HC * i)
                for hc in range(HC):
                    if hc % 4 == 0:
                        pe.wait_ge(s_hn, 2 * i + hc // 4 + 1)
                    ins = t.transpose(low[2 + hc // 4][:, P * (hc % 4):P * (hc % 4) + P], Hn[u % 2][:, P * hc:P * hc + P], ident[:, :])
                ins.then_inc(s_htr, 1)

            def down(i, u, e):
                if not (isinstance(i, int) and i < 2):
                    pe.wait_ge(s_y, i - 1)
                for hc in range(HC):
                    pe.wait_ge(s_hr, HC * i + hc + 1)
                    ins = t.matmul(hib[u % 2][:, 0:E], Ht[u % 2][:, hc, :], W[:, bass.ds(e, 1), 1, E * hc:E * hc + E].rearrange("p o x -> p (o x)"),
                                   start=hc == 0, stop=hc == HC - 1)
                ins.then_inc(s_d, 1)

            def expert_of(i):
                return pe.value_load(ET[0:1, bass.ds(i, 1)], min_val=0, max_val=NE - 1)

            def pe5(it, last):
                e = [expert_of(4 * it + u) for u in range(4 if last else 5)]
                for u in range(4):
                    i = 4 * it + u
                    if not last or u + 2 < 4:
                        x_turn(i + 2, it + (u + 2) // 4, (u + 2) % 4)
                    hidden_turn(i, u)
                    if not last or u + 1 < 4:
                        up(i + 1, u + 1, e[u + 1])
                    down(i, u, e[u])
            pe.wait_ge(s_pos, 1)
            pe.wait_ge(s_g2e, OPEN + 4 * B)
            pe.wait_ge(s_tix, 1)
            x_turn(0, 0, 0)
            x_turn(1, 0, 1)
            up(0, 0, expert_of(0))
            pe5(0, False)
            pe.wait_ge(s_ready, NE)
            with pe.Fori(1, NTILE // 4 - 1) as it:
                pe5(it, False)
            pe5(NTILE // 4 - 1, True)


def names():
    return ["L0_attn_x", "L0_attn_wq", "L0_attn_bq", "L0_attn_wk", "L0_attn_bk", "L0_attn_wv", "L0_attn_bv",
            "L0_attn_wg", "L0_attn_bg", "L0_attn_wo", "L0_attn_bo", "L0_attn_wd", "L0_attn_bd", "L0_attn_gamma",
            "L0_attn_beta", "L0_ffn_norm_weight", "L0_ffn_router_w", "L0_ffn_sw1", "L0_ffn_sb1", "L0_ffn_sw2",
            "L0_ffn_sb2", "L0_ffn_ew1", "L0_ffn_eb1", "L0_ffn_ew2", "L0_ffn_eb2", "L0_c", "L0_wmod"]

def kernel(**inputs):
    import concourse.bacc as bacc
    from concourse.bass_utils import run_bass_kernel_spmd

    nc = bacc.Bacc("TRN2", target_bir_lowering=False, num_devices=1)
    given = {name: np.ascontiguousarray(inputs[name]) for name in names()}
    given.update(constants())
    handles = {name: nc.dram_tensor(f"in_{name}_dram", x.shape, mybir.dt.from_np(x.dtype), kind="ExternalInput").ap()
               for name, x in given.items()}
    out = nc.dram_tensor("out_0_dram", (B, T, E), F32, kind="ExternalOutput").ap()
    build(nc, handles, out)
    done = run_bass_kernel_spmd(nc, [{f"in_{name}_dram": x for name, x in given.items()}], core_ids=[0])
    return done.results[0]["out_0_dram"]
```
